# Optimizing a Trainium2 kernel written in Bass

```python
import numpy as np
import jax
import jax.numpy as jnp

def _softmax(x, axis=-1):
    return jax.nn.softmax(x, axis=axis)

def _gelu(x):
    return jax.nn.gelu(x, approximate=True)

def _silu(x):
    return jax.nn.silu(x)

def _sigmoid(x):
    return jax.nn.sigmoid(x)

def _layernorm(x, axis=-1, eps=1e-05):
    m = jnp.mean(x, axis=axis, keepdims=True)
    v = jnp.var(x, axis=axis, keepdims=True)
    return (x - m) / jnp.sqrt(v + eps)

def _scatter_add(tgt, idx, src, axis=0):
    return tgt.at[idx].add(src)

def _segment_sum(src, seg, n):
    return jax.ops.segment_sum(src, seg, n)
kernel_name = 'mk_perceiver_d2_seqx_r4_f11f9a'

def setup_inputs(seed: int=0):
    np.random.seed(seed)
    _w = jnp.asarray

    def _rec_inputs():
        import jax
        import jax.numpy as jnp
        _rk = jax.random.key(seed)
        x = -0.000125 + 0.9999 * jax.random.normal(jax.random.fold_in(_rk, 1), (8, 64, 512), jnp.float32)
        _lenS = 64 - jax.random.randint(jax.random.fold_in(_rk, 7), (8,), 0, max(1, 64 // 4) + 1, jnp.int32)
        _lenS2 = 1601 - jax.random.randint(jax.random.fold_in(_rk, 8), (8,), 0, max(1, 1601 // 4) + 1, jnp.int32)
        _ctx_2048P = jax.random.normal(jax.random.fold_in(_rk, 11), (8, 16, 512), jnp.float32)
        _ctx_2048c = jax.random.dirichlet(jax.random.fold_in(_rk, 511), 0.3 * jnp.ones((16,), jnp.float32), (8, 1601))
        _ctx_2048t = jnp.einsum('bsk,bkd->bsd', _ctx_2048c, _ctx_2048P)
        _ctx_2048t = _ctx_2048t * jax.lax.rsqrt(jnp.mean(jnp.square(_ctx_2048t)) + 1e-12) * 0.953939
        ctx_2048 = -1.52775e-05 + 0.999936 * (_ctx_2048t + 0.3 * jax.random.normal(jax.random.fold_in(_rk, 611), (8, 1601, 512), jnp.float32))
        return (x, ctx_2048, _lenS2)
    x, ctx_2048, _lenS2 = _rec_inputs()

    def _L0_xattn_setup():
        import jax, jax.numpy as jnp
        import numpy as np
        EPS = 1e-06
        NUM_HEADS = 16

        def _feature_map(x):
            return jnp.where(x > 0, x + 1.0, jnp.exp(x))
        key = jax.random.key(seed)
        ks = jax.random.split(key, 7)
        B, L, S, D = (4, 1024, 1024, 512)
        sc = 1.0 / np.sqrt(D)
        return {'query': jax.random.normal(ks[0], (B, L, D), jnp.float32), 'kv': jax.random.normal(ks[1], (B, S, D), jnp.float32), 'Wq': jax.random.normal(ks[2], (D, D), jnp.float32) * sc, 'Wg': jax.random.normal(ks[3], (D, D), jnp.float32) * sc, 'bg': jnp.ones((D,), jnp.float32), 'Wkv': jax.random.normal(ks[4], (2 * D, D), jnp.float32) * sc, 'Wo': jax.random.normal(ks[5], (D, D), jnp.float32) * sc}
    _L0_xattn_all = _L0_xattn_setup()
    _L0_xattn_in = {k: v for k, v in _L0_xattn_all.items() if k in ('Wq', 'Wg', 'bg', 'Wkv', 'Wo')}
    del _L0_xattn_all

    def _L0_attn_setup():
        import jax, jax.numpy as jnp
        import numpy as np
        B, S, HID = (2, 512, 512)
        H, KV, D = (8, 2, 64)
        SW = 128
        SCALAR = 256.0
        EPS = 1e-06
        THETA = 1000000.0
        SOFTCAP = 30.0

        def _layernorm_unit(x, eps=EPS):
            x = x.astype(jnp.float32)
            mu = jnp.mean(x, axis=-1, keepdims=True)
            xc = x - mu
            var = jnp.mean(xc * xc, axis=-1, keepdims=True)
            return xc * jax.lax.rsqrt(var + eps)

        def _rope_cache(seq_len, head_dim, theta):
            inv_freq = 1.0 / theta ** (jnp.arange(0, head_dim, 2, dtype=jnp.float32) / head_dim)
            pos = jnp.arange(seq_len, dtype=jnp.float32)
            freqs = pos[:, None] * inv_freq[None, :]
            emb = jnp.concatenate([freqs, freqs], axis=-1)
            return (jnp.cos(emb), jnp.sin(emb))

        def _rotate_half(x):
            x1, x2 = jnp.split(x, 2, axis=-1)
            return jnp.concatenate([-x2, x1], axis=-1)
        key = jax.random.key(seed)
        ks = jax.random.split(key, 5)
        sc = 0.02
        return {'hidden_states': jax.random.normal(ks[0], (B, S, HID), dtype=jnp.float32), 'Wq': jax.random.normal(ks[1], (H * D, HID), dtype=jnp.float32) * sc, 'Wk': jax.random.normal(ks[2], (KV * D, HID), dtype=jnp.float32) * sc, 'Wv': jax.random.normal(ks[3], (KV * D, HID), dtype=jnp.float32) * sc, 'Wo': jax.random.normal(ks[4], (HID, HID), dtype=jnp.float32) * sc}
    _L0_attn_all = _L0_attn_setup()
    _L0_attn_in = {k: v for k, v in _L0_attn_all.items() if k in ('Wq', 'Wk', 'Wv', 'Wo')}
    del _L0_attn_all

    def _L0_ffn_setup():
        import jax, jax.numpy as jnp
        import numpy as np
        E = 8
        TOP_K = 2
        B, T, C = (4, 512, 512)
        F = 1408

        def _moe(x, Wg, W1, W3, W2, top_k=TOP_K, norm_probs=True):
            Bb, Tt, Cc = x.shape
            xf = x.reshape(-1, Cc)
            logits = xf @ Wg
            probs = jax.nn.softmax(logits.astype(jnp.float32), axis=-1)
            probs, indices = jax.lax.top_k(probs, top_k)
            if norm_probs:
                probs = probs / probs.sum(axis=-1, keepdims=True)
            probs = probs.astype(x.dtype)
            N, Ee = (xf.shape[0], W1.shape[0])
            w = jnp.zeros((N, Ee), x.dtype).at[jnp.arange(N)[:, None], indices].add(probs)

            def body(y, ws):
                w1, w3, w2, we = ws
                h = jax.nn.silu(xf @ w1) * (xf @ w3)
                return (y + we[:, None] * (h @ w2), None)
            y, _ = jax.lax.scan(body, jnp.zeros_like(xf), (W1, W3, W2, w.T))
            return y.reshape(Bb, Tt, Cc)
        key = jax.random.key(seed)
        k = jax.random.split(key, 5)
        s = 0.02
        return {'x': jax.random.normal(k[0], (B, T, C), jnp.float32), 'Wg': jax.random.normal(k[1], (C, E), jnp.float32) * s, 'W1': jax.random.normal(k[2], (E, C, F), jnp.float32) * s, 'W3': jax.random.normal(k[3], (E, C, F), jnp.float32) * s, 'W2': jax.random.normal(k[4], (E, F, C), jnp.float32) * s}
    _L0_ffn_all = _L0_ffn_setup()
    _L0_ffn_in = {k: v for k, v in _L0_ffn_all.items() if k in ('Wg', 'W1', 'W3', 'W2')}
    del _L0_ffn_all

    def _L1_xattn_setup():
        import jax, jax.numpy as jnp
        import numpy as np
        DIM = 512
        HEADS = 16
        HEAD_DIM = DIM // HEADS
        EPS = 1e-06
        IMG_TOKENS = 257
        B, L1, L2 = (2, 1024, 769)
        SCALE = 1.0 / np.sqrt(HEAD_DIM).astype(np.float32)

        def rms_norm(x, g):
            return x * jax.lax.rsqrt(jnp.mean(x * x, axis=-1, keepdims=True) + EPS) * g

        def attention(q, k, v, kv_mask=None):
            s = jnp.einsum('bqhd,bkhd->bhqk', q, k) * SCALE
            if kv_mask is not None:
                s = jnp.where(kv_mask[:, None, None, :], s, jnp.float32(-1000000000.0))
            p = jax.nn.softmax(s, axis=-1)
            return jnp.einsum('bhqk,bkhd->bqhd', p, v)
        key = jax.random.key(seed)
        ks = jax.random.split(key, 20)
        std = 0.02

        def lin(i):
            return (jax.random.normal(ks[i], (DIM, DIM), jnp.float32) * std, jnp.zeros((DIM,), jnp.float32))
        w_q, b_q = lin(0)
        w_k, b_k = lin(1)
        w_v, b_v = lin(2)
        w_k_img, b_k_img = lin(3)
        w_v_img, b_v_img = lin(4)
        w_o, b_o = lin(5)
        return {'x': jax.random.normal(ks[6], (B, L1, DIM), jnp.float32), 'context': jax.random.normal(ks[7], (B, L2, DIM), jnp.float32), 'context_lens': jax.random.randint(ks[8], (B,), 64, 513, jnp.int64 if jax.config.jax_enable_x64 else jnp.int32), 'w_q': w_q, 'b_q': b_q, 'w_k': w_k, 'b_k': b_k, 'w_v': w_v, 'b_v': b_v, 'w_k_img': w_k_img, 'b_k_img': b_k_img, 'w_v_img': w_v_img, 'b_v_img': b_v_img, 'w_o': w_o, 'b_o': b_o, 'g_q': jnp.ones((DIM,), jnp.float32), 'g_k': jnp.ones((DIM,), jnp.float32), 'g_k_img': jnp.ones((DIM,), jnp.float32)}
    _L1_xattn_all = _L1_xattn_setup()
    _L1_xattn_in = {k: v for k, v in _L1_xattn_all.items() if k in ('w_q', 'b_q', 'w_k', 'b_k', 'w_v', 'b_v', 'w_k_img', 'b_k_img', 'w_v_img', 'b_v_img', 'w_o', 'b_o', 'g_q', 'g_k', 'g_k_img')}
    del _L1_xattn_all

    def _L1_attn_setup():
        import jax, jax.numpy as jnp
        import numpy as np
        DIM = 512
        N_HEADS = 32
        N_KV_HEADS = 8
        HEAD_DIM = 64
        REPEATS = N_HEADS // N_KV_HEADS
        SLIDING_WINDOW = 256
        EPS = 1e-06
        B, T = (2, 512)

        def _alibi_slopes(n):
            r = 2.0 ** (-8.0 / n)
            return jnp.asarray([r ** i for i in range(n)], dtype=jnp.float32)

        def _rms_norm(x, w, eps):
            var = jnp.mean(x * x, axis=-1, keepdims=True)
            return x * jax.lax.rsqrt(var + eps) * w
        key = jax.random.key(seed)
        ks = jax.random.split(key, 6)
        s = 0.02
        return {'x': jax.random.normal(ks[0], (B, T, DIM), jnp.float32), 'wq': jax.random.normal(ks[1], (N_HEADS * HEAD_DIM, DIM), jnp.float32) * s, 'wk': jax.random.normal(ks[2], (N_KV_HEADS * HEAD_DIM, DIM), jnp.float32) * s, 'wv': jax.random.normal(ks[3], (N_KV_HEADS * HEAD_DIM, DIM), jnp.float32) * s, 'wo': jax.random.normal(ks[4], (DIM, N_HEADS * HEAD_DIM), jnp.float32) * s, 'q_norm_w': jnp.ones((N_HEADS * HEAD_DIM,), jnp.float32), 'k_norm_w': jnp.ones((N_KV_HEADS * HEAD_DIM,), jnp.float32)}
    _L1_attn_all = _L1_attn_setup()
    _L1_attn_in = {k: v for k, v in _L1_attn_all.items() if k in ('wq', 'wk', 'wv', 'wo', 'q_norm_w', 'k_norm_w')}
    del _L1_attn_all

    def _L1_ffn_setup():
        import jax, jax.numpy as jnp
        import numpy as np
        ROPE_THETA = 1000000.0
        TOP_K = 2

        def rmsnorm(x, w, eps=1e-06):
            xf = x.astype(jnp.float32)
            n = jax.lax.rsqrt(jnp.mean(xf * xf, axis=-1, keepdims=True) + eps)
            return (xf * n).astype(x.dtype) * w

        def rope_tables(seq_len, head_dim):
            freqs = 1.0 / ROPE_THETA ** (jnp.arange(0, head_dim, 2, dtype=jnp.float32) / head_dim)
            t = jnp.arange(seq_len, dtype=jnp.float32)
            f = jnp.outer(t, freqs)
            return (jnp.cos(f), jnp.sin(f))

        def apply_rope(x, cos, sin):
            half = x.shape[-1] // 2
            x1, x2 = (x[..., :half], x[..., half:])
            c = cos[None, None]
            s = sin[None, None]
            return jnp.concatenate([x1 * c - x2 * s, x2 * c + x1 * s], axis=-1)
        key = jax.random.key(seed)
        ks = jax.random.split(key, 8)
        B, S, D = (2, 512, 512)
        Hq, Hkv, hd = (16, 4, 128)
        E, I = (8, 352)
        sc = 0.02
        return {'hidden': jax.random.normal(ks[0], (B, S, D), jnp.float32), 'attn_norm_w': jnp.ones((D,), jnp.float32), 'q_w': jax.random.normal(ks[1], (Hq * hd, D), jnp.float32) * sc, 'k_w': jax.random.normal(ks[2], (Hkv * hd, D), jnp.float32) * sc, 'v_w': jax.random.normal(ks[3], (Hkv * hd, D), jnp.float32) * sc, 'o_w': jax.random.normal(ks[4], (D, Hq * hd), jnp.float32) * sc, 'q_norm_w': jnp.ones((hd,), jnp.float32), 'k_norm_w': jnp.ones((hd,), jnp.float32), 'ffn_norm_w': jnp.ones((D,), jnp.float32), 'gate_w': jax.random.normal(ks[5], (E, D), jnp.float32) * sc, 'wg': jax.random.normal(ks[6], (E, I, D), jnp.float32) * sc, 'wu': jax.random.normal(ks[7], (E, I, D), jnp.float32) * sc, 'wd': jax.random.normal(jax.random.fold_in(key, 99), (E, D, I), jnp.float32) * sc}
    _L1_ffn_all = _L1_ffn_setup()
    _L1_ffn_in = {k: v for k, v in _L1_ffn_all.items() if k in ('attn_norm_w', 'q_w', 'k_w', 'v_w', 'o_w', 'q_norm_w', 'k_norm_w', 'ffn_norm_w', 'gate_w', 'wg', 'wu', 'wd')}
    del _L1_ffn_all
    return {'x': x, 'ctx_2048': ctx_2048, '_lenS2': _lenS2, 'L0_xattn_Wq': _L0_xattn_in['Wq'], 'L0_xattn_Wg': _L0_xattn_in['Wg'], 'L0_xattn_bg': _L0_xattn_in['bg'], 'L0_xattn_Wkv': _L0_xattn_in['Wkv'], 'L0_xattn_Wo': _L0_xattn_in['Wo'], 'L0_attn_Wq': _L0_attn_in['Wq'], 'L0_attn_Wk': _L0_attn_in['Wk'], 'L0_attn_Wv': _L0_attn_in['Wv'], 'L0_attn_Wo': _L0_attn_in['Wo'], 'L0_ffn_Wg': _L0_ffn_in['Wg'], 'L0_ffn_W1': _L0_ffn_in['W1'], 'L0_ffn_W3': _L0_ffn_in['W3'], 'L0_ffn_W2': _L0_ffn_in['W2'], 'L1_xattn_w_q': _L1_xattn_in['w_q'], 'L1_xattn_b_q': _L1_xattn_in['b_q'], 'L1_xattn_w_k': _L1_xattn_in['w_k'], 'L1_xattn_b_k': _L1_xattn_in['b_k'], 'L1_xattn_w_v': _L1_xattn_in['w_v'], 'L1_xattn_b_v': _L1_xattn_in['b_v'], 'L1_xattn_w_k_img': _L1_xattn_in['w_k_img'], 'L1_xattn_b_k_img': _L1_xattn_in['b_k_img'], 'L1_xattn_w_v_img': _L1_xattn_in['w_v_img'], 'L1_xattn_b_v_img': _L1_xattn_in['b_v_img'], 'L1_xattn_w_o': _L1_xattn_in['w_o'], 'L1_xattn_b_o': _L1_xattn_in['b_o'], 'L1_xattn_g_q': _L1_xattn_in['g_q'], 'L1_xattn_g_k': _L1_xattn_in['g_k'], 'L1_xattn_g_k_img': _L1_xattn_in['g_k_img'], 'L1_attn_wq': _L1_attn_in['wq'], 'L1_attn_wk': _L1_attn_in['wk'], 'L1_attn_wv': _L1_attn_in['wv'], 'L1_attn_wo': _L1_attn_in['wo'], 'L1_attn_q_norm_w': _L1_attn_in['q_norm_w'], 'L1_attn_k_norm_w': _L1_attn_in['k_norm_w'], 'L1_ffn_attn_norm_w': _L1_ffn_in['attn_norm_w'], 'L1_ffn_q_w': _L1_ffn_in['q_w'], 'L1_ffn_k_w': _L1_ffn_in['k_w'], 'L1_ffn_v_w': _L1_ffn_in['v_w'], 'L1_ffn_o_w': _L1_ffn_in['o_w'], 'L1_ffn_q_norm_w': _L1_ffn_in['q_norm_w'], 'L1_ffn_k_norm_w': _L1_ffn_in['k_norm_w'], 'L1_ffn_ffn_norm_w': _L1_ffn_in['ffn_norm_w'], 'L1_ffn_gate_w': _L1_ffn_in['gate_w'], 'L1_ffn_wg': _L1_ffn_in['wg'], 'L1_ffn_wu': _L1_ffn_in['wu'], 'L1_ffn_wd': _L1_ffn_in['wd']}

def reference(x, ctx_2048, _lenS2, L0_xattn_Wq, L0_xattn_Wg, L0_xattn_bg, L0_xattn_Wkv, L0_xattn_Wo, L0_attn_Wq, L0_attn_Wk, L0_attn_Wv, L0_attn_Wo, L0_ffn_Wg, L0_ffn_W1, L0_ffn_W3, L0_ffn_W2, L1_xattn_w_q, L1_xattn_b_q, L1_xattn_w_k, L1_xattn_b_k, L1_xattn_w_v, L1_xattn_b_v, L1_xattn_w_k_img, L1_xattn_b_k_img, L1_xattn_w_v_img, L1_xattn_b_v_img, L1_xattn_w_o, L1_xattn_b_o, L1_xattn_g_q, L1_xattn_g_k, L1_xattn_g_k_img, L1_attn_wq, L1_attn_wk, L1_attn_wv, L1_attn_wo, L1_attn_q_norm_w, L1_attn_k_norm_w, L1_ffn_attn_norm_w, L1_ffn_q_w, L1_ffn_k_w, L1_ffn_v_w, L1_ffn_o_w, L1_ffn_q_norm_w, L1_ffn_k_norm_w, L1_ffn_ffn_norm_w, L1_ffn_gate_w, L1_ffn_wg, L1_ffn_wu, L1_ffn_wd):
    import jax
    import jax.numpy as jnp

    def _L0_xattn_ref(query, kv, Wq, Wg, bg, Wkv, Wo):
        import jax, jax.numpy as jnp
        import numpy as np
        EPS = 1e-06
        NUM_HEADS = 16

        def _feature_map(x):
            return jnp.where(x > 0, x + 1.0, jnp.exp(x))
        B, L, D = query.shape
        S = kv.shape[1]
        H = NUM_HEADS
        hd = D // H
        q = query @ Wq.T
        gate = jax.nn.sigmoid(query @ Wg.T + bg)
        kvp = kv @ Wkv.T
        k, v = jnp.split(kvp, 2, axis=-1)
        q = _feature_map(q.reshape(B, L, H, hd).transpose(0, 2, 1, 3))
        k = _feature_map(k.reshape(B, S, H, hd).transpose(0, 2, 1, 3))
        v = v.reshape(B, S, H, hd).transpose(0, 2, 1, 3)
        kv_summary = jnp.einsum('bhsd,bhse->bhde', k, v)
        k_sum = k.sum(axis=-2)
        z = 1.0 / (jnp.einsum('bhld,bhd->bhl', q, k_sum)[..., None] + EPS)
        attn = jnp.einsum('bhld,bhde->bhle', q, kv_summary) * z
        attn = attn.transpose(0, 2, 1, 3).reshape(B, L, D)
        out = attn * gate @ Wo.T
        return out

    def _L0_attn_ref(hidden_states, Wq, Wk, Wv, Wo):
        import jax, jax.numpy as jnp
        import numpy as np
        B, S, HID = (2, 512, 512)
        H, KV, D = (8, 2, 64)
        SW = 128
        SCALAR = 256.0
        EPS = 1e-06
        THETA = 1000000.0
        SOFTCAP = 30.0

        def _layernorm_unit(x, eps=EPS):
            x = x.astype(jnp.float32)
            mu = jnp.mean(x, axis=-1, keepdims=True)
            xc = x - mu
            var = jnp.mean(xc * xc, axis=-1, keepdims=True)
            return xc * jax.lax.rsqrt(var + eps)

        def _rope_cache(seq_len, head_dim, theta):
            inv_freq = 1.0 / theta ** (jnp.arange(0, head_dim, 2, dtype=jnp.float32) / head_dim)
            pos = jnp.arange(seq_len, dtype=jnp.float32)
            freqs = pos[:, None] * inv_freq[None, :]
            emb = jnp.concatenate([freqs, freqs], axis=-1)
            return (jnp.cos(emb), jnp.sin(emb))

        def _rotate_half(x):
            x1, x2 = jnp.split(x, 2, axis=-1)
            return jnp.concatenate([-x2, x1], axis=-1)
        b, s, _ = hidden_states.shape
        q = jnp.einsum('bsh,oh->bso', hidden_states, Wq).reshape(b, s, H, D).transpose(0, 2, 1, 3)
        k = jnp.einsum('bsh,oh->bso', hidden_states, Wk).reshape(b, s, KV, D).transpose(0, 2, 1, 3)
        v = jnp.einsum('bsh,oh->bso', hidden_states, Wv).reshape(b, s, KV, D).transpose(0, 2, 1, 3)
        cos, sin = _rope_cache(s, D, THETA)
        cos = cos[None, None]
        sin = sin[None, None]
        q = q * cos + _rotate_half(q) * sin
        k = k * cos + _rotate_half(k) * sin
        q = _layernorm_unit(q) * SCALAR
        k = _layernorm_unit(k)
        v = _layernorm_unit(v)
        rep = H // KV
        k = jnp.repeat(k, rep, axis=1)
        v = jnp.repeat(v, rep, axis=1)
        scores = jnp.einsum('bhqd,bhkd->bhqk', q, k) / jnp.sqrt(jnp.float32(D))
        i = jnp.arange(s)[:, None]
        j = jnp.arange(s)[None, :]
        allowed = (j <= i) & (j > i - SW)
        mask = jnp.where(allowed, 0.0, -jnp.inf).astype(scores.dtype)
        scores = scores + mask
        scores = jnp.tanh(scores / SOFTCAP) * SOFTCAP
        probs = jax.nn.softmax(scores.astype(jnp.float32), axis=-1).astype(v.dtype)
        out = jnp.einsum('bhqk,bhkd->bhqd', probs, v)
        out = out.transpose(0, 2, 1, 3).reshape(b, s, H * D)
        return jnp.einsum('bso,ho->bsh', out, Wo)

    def _L0_ffn_ref(x, Wg, W1, W3, W2):
        import jax, jax.numpy as jnp
        import numpy as np
        E = 8
        TOP_K = 2
        B, T, C = (4, 512, 512)
        F = 1408

        def _moe(x, Wg, W1, W3, W2, top_k=TOP_K, norm_probs=True):
            Bb, Tt, Cc = x.shape
            xf = x.reshape(-1, Cc)
            logits = xf @ Wg
            probs = jax.nn.softmax(logits.astype(jnp.float32), axis=-1)
            probs, indices = jax.lax.top_k(probs, top_k)
            if norm_probs:
                probs = probs / probs.sum(axis=-1, keepdims=True)
            probs = probs.astype(x.dtype)
            N, Ee = (xf.shape[0], W1.shape[0])
            w = jnp.zeros((N, Ee), x.dtype).at[jnp.arange(N)[:, None], indices].add(probs)

            def body(y, ws):
                w1, w3, w2, we = ws
                h = jax.nn.silu(xf @ w1) * (xf @ w3)
                return (y + we[:, None] * (h @ w2), None)
            y, _ = jax.lax.scan(body, jnp.zeros_like(xf), (W1, W3, W2, w.T))
            return y.reshape(Bb, Tt, Cc)
        return _moe(x, Wg, W1, W3, W2)

    def _L1_xattn_ref(x, context, context_lens, w_q, b_q, w_k, b_k, w_v, b_v, w_k_img, b_k_img, w_v_img, b_v_img, w_o, b_o, g_q, g_k, g_k_img):
        import jax, jax.numpy as jnp
        import numpy as np
        DIM = 512
        HEADS = 16
        HEAD_DIM = DIM // HEADS
        EPS = 1e-06
        IMG_TOKENS = 257
        B, L1, L2 = (2, 1024, 769)
        SCALE = 1.0 / np.sqrt(HEAD_DIM).astype(np.float32)

        def rms_norm(x, g):
            return x * jax.lax.rsqrt(jnp.mean(x * x, axis=-1, keepdims=True) + EPS) * g

        def attention(q, k, v, kv_mask=None):
            s = jnp.einsum('bqhd,bkhd->bhqk', q, k) * SCALE
            if kv_mask is not None:
                s = jnp.where(kv_mask[:, None, None, :], s, jnp.float32(-1000000000.0))
            p = jax.nn.softmax(s, axis=-1)
            return jnp.einsum('bhqk,bkhd->bqhd', p, v)
        b = x.shape[0]
        ctx_img = context[:, :IMG_TOKENS]
        ctx_txt = context[:, IMG_TOKENS:]
        q = rms_norm(x @ w_q.T + b_q, g_q).reshape(b, -1, HEADS, HEAD_DIM)
        k = rms_norm(ctx_txt @ w_k.T + b_k, g_k).reshape(b, -1, HEADS, HEAD_DIM)
        v = (ctx_txt @ w_v.T + b_v).reshape(b, -1, HEADS, HEAD_DIM)
        k_img = rms_norm(ctx_img @ w_k_img.T + b_k_img, g_k_img).reshape(b, -1, HEADS, HEAD_DIM)
        v_img = (ctx_img @ w_v_img.T + b_v_img).reshape(b, -1, HEADS, HEAD_DIM)
        txt_len = ctx_txt.shape[1]
        kv_mask = jnp.arange(txt_len)[None, :] < context_lens[:, None]
        img_x = attention(q, k_img, v_img)
        txt_x = attention(q, k, v, kv_mask)
        out = (txt_x + img_x).reshape(b, -1, DIM)
        return out @ w_o.T + b_o

    def _L1_attn_ref(x, wq, wk, wv, wo, q_norm_w, k_norm_w):
        import jax, jax.numpy as jnp
        import numpy as np
        DIM = 512
        N_HEADS = 32
        N_KV_HEADS = 8
        HEAD_DIM = 64
        REPEATS = N_HEADS // N_KV_HEADS
        SLIDING_WINDOW = 256
        EPS = 1e-06
        B, T = (2, 512)

        def _alibi_slopes(n):
            r = 2.0 ** (-8.0 / n)
            return jnp.asarray([r ** i for i in range(n)], dtype=jnp.float32)

        def _rms_norm(x, w, eps):
            var = jnp.mean(x * x, axis=-1, keepdims=True)
            return x * jax.lax.rsqrt(var + eps) * w
        bsz, seqlen, _ = x.shape
        xq = _rms_norm(x @ wq.T, q_norm_w, EPS)
        xk = _rms_norm(x @ wk.T, k_norm_w, EPS)
        xv = x @ wv.T
        xq = xq.reshape(bsz, seqlen, N_HEADS, HEAD_DIM).transpose(0, 2, 1, 3)
        xk = xk.reshape(bsz, seqlen, N_KV_HEADS, HEAD_DIM).transpose(0, 2, 1, 3)
        xv = xv.reshape(bsz, seqlen, N_KV_HEADS, HEAD_DIM).transpose(0, 2, 1, 3)
        xk = jnp.repeat(xk, REPEATS, axis=1)
        xv = jnp.repeat(xv, REPEATS, axis=1)
        pos = jnp.arange(seqlen)
        dist = pos[None, :] - pos[:, None]
        slopes = _alibi_slopes(N_HEADS)
        alibi = slopes[:, None, None] * dist.astype(jnp.float32)
        allowed = (dist <= 0) & (dist >= -SLIDING_WINDOW)
        bias = jnp.where(allowed[None], alibi, -jnp.inf)
        scale = 1.0 / jnp.sqrt(jnp.asarray(HEAD_DIM, jnp.float32))
        scores = jnp.einsum('bhtd,bhsd->bhts', xq, xk) * scale + bias[None]
        attn = jax.nn.softmax(scores, axis=-1)
        out = jnp.einsum('bhts,bhsd->bhtd', attn, xv)
        out = out.transpose(0, 2, 1, 3).reshape(bsz, seqlen, N_HEADS * HEAD_DIM)
        return out @ wo.T

    def _L1_ffn_ref(hidden, attn_norm_w, q_w, k_w, v_w, o_w, q_norm_w, k_norm_w, ffn_norm_w, gate_w, wg, wu, wd):
        import jax, jax.numpy as jnp
        import numpy as np
        ROPE_THETA = 1000000.0
        TOP_K = 2

        def rmsnorm(x, w, eps=1e-06):
            xf = x.astype(jnp.float32)
            n = jax.lax.rsqrt(jnp.mean(xf * xf, axis=-1, keepdims=True) + eps)
            return (xf * n).astype(x.dtype) * w

        def rope_tables(seq_len, head_dim):
            freqs = 1.0 / ROPE_THETA ** (jnp.arange(0, head_dim, 2, dtype=jnp.float32) / head_dim)
            t = jnp.arange(seq_len, dtype=jnp.float32)
            f = jnp.outer(t, freqs)
            return (jnp.cos(f), jnp.sin(f))

        def apply_rope(x, cos, sin):
            half = x.shape[-1] // 2
            x1, x2 = (x[..., :half], x[..., half:])
            c = cos[None, None]
            s = sin[None, None]
            return jnp.concatenate([x1 * c - x2 * s, x2 * c + x1 * s], axis=-1)
        B, S, D = hidden.shape
        hd = q_norm_w.shape[0]
        Hq = q_w.shape[0] // hd
        Hkv = k_w.shape[0] // hd
        n_rep = Hq // Hkv
        h = rmsnorm(hidden, attn_norm_w)
        q = (h @ q_w.T).reshape(B, S, Hq, hd)
        k = (h @ k_w.T).reshape(B, S, Hkv, hd)
        v = (h @ v_w.T).reshape(B, S, Hkv, hd)
        q = rmsnorm(q, q_norm_w).transpose(0, 2, 1, 3)
        k = rmsnorm(k, k_norm_w).transpose(0, 2, 1, 3)
        v = v.transpose(0, 2, 1, 3)
        cos, sin = rope_tables(S, hd)
        q = apply_rope(q, cos, sin)
        k = apply_rope(k, cos, sin)
        k = jnp.repeat(k, n_rep, axis=1)
        v = jnp.repeat(v, n_rep, axis=1)
        scale = 1.0 / jnp.sqrt(jnp.float32(hd))
        scores = jnp.einsum('bhqd,bhkd->bhqk', q, k) * scale
        causal = jnp.tril(jnp.ones((S, S), bool))
        scores = jnp.where(causal[None, None], scores, jnp.finfo(scores.dtype).min)
        attn = jnp.einsum('bhqk,bhkd->bhqd', jax.nn.softmax(scores, axis=-1), v)
        attn = attn.transpose(0, 2, 1, 3).reshape(B, S, Hq * hd)
        hidden = hidden + attn @ o_w.T
        h2 = rmsnorm(hidden, ffn_norm_w)
        T = B * S
        E = gate_w.shape[0]
        tok = h2.reshape(T, D)
        probs = jax.nn.softmax(tok @ gate_w.T, axis=-1)
        topv, topi = jax.lax.top_k(probs, TOP_K)
        topw = topv / (jnp.sum(topv, axis=-1, keepdims=True) + 1e-09)
        combine = jnp.zeros((T, E), tok.dtype).at[jnp.arange(T)[:, None], topi].set(topw)
        eg = jnp.einsum('td,eid->eti', tok, wg)
        eu = jnp.einsum('td,eid->eti', tok, wu)
        eo = jnp.einsum('eti,edi->etd', jax.nn.silu(eg) * eu, wd)
        moe_out = jnp.einsum('te,etd->td', combine, eo).reshape(B, S, D)
        return hidden + moe_out
    x = x + _L0_xattn_ref(_layernorm(x, axis=-1), ctx_2048, L0_xattn_Wq, L0_xattn_Wg, L0_xattn_bg, L0_xattn_Wkv, L0_xattn_Wo)
    x = x + _L0_attn_ref(_layernorm(x, axis=-1), L0_attn_Wq, L0_attn_Wk, L0_attn_Wv, L0_attn_Wo)
    x = x + _L0_ffn_ref(_layernorm(x, axis=-1), L0_ffn_Wg, L0_ffn_W1, L0_ffn_W3, L0_ffn_W2)
    x = x + _L1_xattn_ref(_layernorm(x, axis=-1), ctx_2048, _lenS2, L1_xattn_w_q, L1_xattn_b_q, L1_xattn_w_k, L1_xattn_b_k, L1_xattn_w_v, L1_xattn_b_v, L1_xattn_w_k_img, L1_xattn_b_k_img, L1_xattn_w_v_img, L1_xattn_b_v_img, L1_xattn_w_o, L1_xattn_b_o, L1_xattn_g_q, L1_xattn_g_k, L1_xattn_g_k_img)
    x = x + _L1_attn_ref(_layernorm(x, axis=-1), L1_attn_wq, L1_attn_wk, L1_attn_wv, L1_attn_wo, L1_attn_q_norm_w, L1_attn_k_norm_w)
    x = x + _L1_ffn_ref(_layernorm(x, axis=-1), L1_ffn_attn_norm_w, L1_ffn_q_w, L1_ffn_k_w, L1_ffn_v_w, L1_ffn_o_w, L1_ffn_q_norm_w, L1_ffn_k_norm_w, L1_ffn_ffn_norm_w, L1_ffn_gate_w, L1_ffn_wg, L1_ffn_wu, L1_ffn_wd)
    return x

_drawn_inputs = setup_inputs


def setup_inputs(seed=0):
    import zlib

    import numpy as np

    out = dict(_drawn_inputs(seed))
    spreads = {'L0_xattn_bg': (1.0, 0.6),
     'L1_xattn_b_q': (0.0, 0.655),
     'L1_xattn_b_k': (0.0, 0.8),
     'L1_xattn_b_v': (0.0, 0.1),
     'L1_xattn_b_k_img': (0.0, 0.8),
     'L1_xattn_b_v_img': (0.0, 0.1),
     'L1_xattn_b_o': (0.0, 0.1),
     'L1_xattn_g_q': (1.0, 0.6),
     'L1_xattn_g_k': (1.0, 0.6),
     'L1_xattn_g_k_img': (1.0, 0.6),
     'L1_attn_q_norm_w': (1.0, 0.6),
     'L1_attn_k_norm_w': (1.0, 0.6),
     'L1_ffn_attn_norm_w': (1.0, 0.6),
     'L1_ffn_q_norm_w': (1.0, 0.6),
     'L1_ffn_k_norm_w': (1.0, 0.6),
     'L1_ffn_ffn_norm_w': (1.0, 0.6)}
    factors = {'L0_xattn_Wq': 4.957,
     'L1_ffn_gate_w': 4.351,
     'L1_ffn_wg': 3.909,
     'L1_ffn_wu': 3.83,
     'L1_ffn_wd': 3.842}
    for name, (base, spread) in spreads.items():
        noise = np.random.default_rng([zlib.crc32(name.encode()), seed]).standard_normal(out[name].shape)
        drawn = base * np.exp(spread * noise) if base else spread * noise
        out[name] = jnp.asarray(drawn.astype(out[name].dtype))
    for name, factor in factors.items():
        out[name] = (out[name] * factor).astype(out[name].dtype)
    return out
```

```python
from contextlib import ExitStack

import numpy as np
import concourse.bass as bass
from concourse import mybir

ALU = mybir.AluOpType
ACT = mybir.ActivationFunctionType
AX = mybir.AxisListType
F32 = mybir.dt.float32
F32R = mybir.dt.float32r
I32 = mybir.dt.int32

P = 128
B, SEQ, C = 8, 64, 512
TOK = B * SEQ
TT = TOK // P
KC = C // P
CTX = 1601
CT = 13
LAST = CTX - 12 * P
IMG = 257
TXT = CTX - IMG
E8 = 8
F0, F1 = 1408, 352
NF0, NF1 = F0 // P, 3
H0 = 8
NEG = -1.0e30


class Link:

    def __init__(self, eng, sem):
        self.eng, self.sem, self.n, self.base = eng, sem, 0, 0

    def __call__(self, ins):
        self.n += 1
        ins.then_inc(self.sem, 1)
        self.eng.wait_ge(self.sem, self.base + self.n)

    def at(self, ins):
        self.n += 1
        ins.then_inc(self.sem, 1)

    def sync(self):
        self.eng.wait_ge(self.sem, self.base + self.n)


def plus(a, b):
    return a + b if b else a


def build(nc, D, out):
    ctx = ExitStack()
    sems = {}

    def S(name):
        if name not in sems:
            sems[name] = ctx.enter_context(nc.semaphore(name))
        return sems[name]

    def sb(name, shape, dt=F32):
        return ctx.enter_context(nc.sbuf_tensor(name, shape, dt))

    with ctx:
        X = sb("X", [P, TT, C])
        XN = sb("XN", [P, TT, C])
        XNT = sb("XNT", [P, KC, TOK])
        CONST = sb("CONST", [P, D["const"].shape[1]])
        SM = sb("SM", [P, 480])
        VEC = sb("VEC", [P, 64])
        LEN = sb("LEN", [P, B], I32)
        with nc.sbuf_tensor("ARENA", [P, 45200], F32) as ARENA:
            pass
        PS = ctx.enter_context(nc.psum_tensor("PS", [P, 8, 512], F32))

        ident = CONST[:, 0:128]
        ones = CONST[:, 128:256]
        block32 = CONST[:, 256:384]
        cosT = CONST[:, 384:448]
        sinT = CONST[:, 448:512]
        causal01 = CONST[:, 512:576]
        causalm1 = CONST[:, 576:640]
        tri8 = CONST[:, 640:704]
        bg = CONST[:, 704:708]
        cos6, sin6 = CONST[:, 708:772], CONST[:, 772:836]
        mask6 = CONST[:, 836:964]
        PSF = PS[:, :, :].rearrange("p a b -> p (a b)")
        bq1, bk1, bki1, bv1, bvi1, gq1, gk1, gki1 = (VEC[:, 4 * n:4 * n + 4] for n in range(8))
        qw5, kw5 = VEC[:, 32:48], VEC[:, 48:52]
        hw6, qw6, kw6, fw6 = VEC[:, 52:56], VEC[:, 56:57], VEC[:, 57:58], VEC[:, 58:62]

        def area(at, *shape):
            n = int(np.prod(shape))
            v = ARENA[:, at:at + n]
            if len(shape) == 2:
                v = v.rearrange("p (a b) -> p a b", a=shape[0])
            if len(shape) == 3:
                v = v.rearrange("p (a b c) -> p a b c", a=shape[0], b=shape[1])
            return v

        def parts(hi, lo, *shape):
            both = []
            for at in (hi, lo):
                with nc.sbuf_tensor(f"before{len(split)}", [P, at], F32):
                    with nc.sbuf_tensor(f"split{len(split)}", [P, *shape], F32R) as v:
                        both.append(v[tuple(slice(None) for _ in range(1 + len(shape)))])
                split.append(at)
            return both

        split = []

        def rest(eng, dst, src, hi):
            return eng.tensor_tensor(dst, src, hi.bitcast(F32), ALU.subtract)

        small = [0]

        def tiny(*shape):
            n = int(np.prod(shape))
            v = SM[:, small[0]:small[0] + n]
            small[0] += n
            if len(shape) == 2:
                v = v.rearrange("p (a b) -> p a b", a=shape[0])
            if len(shape) == 3:
                v = v.rearrange("p (a b c) -> p a b c", a=shape[0], b=shape[1])
            return v

        eps5, eps6, zero1 = tiny(1), tiny(1), tiny(1)
        stat = tiny(TT, 6)
        mv = tiny(TT, 2)
        std = tiny(TT)
        rstd = tiny(TT)
        nbg = tiny(KC)
        ksum = tiny(KC)
        red = tiny(48)
        red2 = tiny(48)
        red3 = tiny(48)
        gp = tiny(TT, E8)
        gw = tiny(TT, E8)
        gs = tiny(TT)
        lens = tiny(B)
        lenb = tiny(1)
        gqs, bvv = tiny(KC), tiny(KC)
        mx, nmx, lsum, rls = tiny(2, 2), tiny(2, 2), tiny(2, 2), tiny(2, 2)
        qws = tiny(16)
        nm5, l5, rl5 = tiny(2, 4), tiny(2, 4), tiny(2, 4)
        ms = tiny(TT)

        WK = area(0, KC, C)
        WV = area(2048, KC, C)
        WQ = area(4096, KC, C)
        WG = area(6144, KC, C)
        WO = area(8192, KC, C)
        RING = area(10240, CT, 1024)
        KM = area(23552, 3, 512)
        KE = area(25088, 3, 512)
        KB = area(26624, 4, 512)
        KACC = area(28672, 512)
        CTK = area(29184, KC, C)
        QT = area(31232, KC, TOK)
        G1 = area(33280, KC, TOK)
        KV = area(35328, B, KC, P)
        KS = area(39424, B, KC, P)
        TMP = area(43520, 2, 512)
        AT = area(10240, KC, TOK)
        DEN = area(12288, KC, TOK)
        W2 = area(16896, KC, 768)
        WO2 = area(19968, KC, C)
        QKV = area(22016, TT, 12 * 64)
        XR = area(25088, TT, 12 * 64)
        TA = area(28160, TT, 12 * 64)
        TB = area(31232, TT, 12 * 64)
        PF = area(34304, TT, H0, P)
        TANH = area(22016, TT, H0, 64)
        MASKED = area(28160, TT * H0, 64)
        VAL = XR[:, :, 640:768]
        QT2 = area(38400, TT, 4, P)
        KT2 = area(40448, TT, P)
        PT2 = area(40960, 2, 512)
        OT2 = area(41984, 4, TOK)
        WQ4, WK4, WKI4, WV4, WVI4, WO4 = (area(25088 + 2048 * n, KC, C) for n in range(6))
        CO = [0, 321, 833, 1345]
        CN = [321, 512, 512, 256]
        CC = [area(37376 + 4 * CO[c], KC, CN[c]) for c in range(4)]
        BIAS = area(43780, TXT)
        KT4 = area(0, KC, CTX + 3)
        V4 = area(6416, CT, C)
        PB4 = area(13072, 2, CTX + 3)
        PT4 = area(16280, CT, P)
        ACC4 = area(16280, CTX + 3)
        SQ4 = area(17884, 512)
        QT4 = area(19608, KC, TOK)
        QB4 = area(21656, KC, 4 * SEQ)
        OS4 = area(22680, 2, SEQ)
        BO4 = area(22808, C)
        IOTA = area(23704, TXT // 2).bitcast(mybir.dt.int16)
        RS4 = XNT[:, :, :].rearrange("p k n -> p (k n)")
        AT4 = XN[:, :, :]
        TILES = [(0, P), (P, P), (2 * P, 65)] + [(321 + P * n, P) for n in range(10)]
        GROUPS = [[0, 1, 3, 4], [5, 6, 7, 8], [9, 10, 11, 12], [2]]
        PROD = [("K", c, j) for c in range(4) for j in range(KC)]
        for t in [0, 1, 2, -2, "R0", 3, 4, "R1", 5, 6, "R2", 7, 8, 9, "R3", 10, 11, 12]:
            PROD.append(("R", int(t[1]), 0) if isinstance(t, str) else ("V", t, 0))
        NV = CT + 1
        WQ5 = area(0, KC, 2048)
        WK5 = area(8192, KC, C)
        WV5 = area(10240, KC, C)
        WO5 = area(12288, 16, C)
        QT5 = area(20480, 16, TOK)
        KT5 = area(28672, 4, TOK)
        V5 = area(30720, TT, C)
        OT5 = area(32768, 16, TOK)
        ALIBI = area(40960, 8, 4, P)
        ACC5 = area(32768, 2, 512)
        SQ5 = area(33792, 512)
        RS5 = area(34304, 2, 512)
        PB5 = XN[:, 0:2, :]
        PT5 = XN[:, 2:4, :]
        HN6 = area(40960, TT, C)
        PB6 = area(43008, 2, 512)
        PT6 = area(44032, 2, 512)
        SQ6 = area(32768, 2, 512)
        RS6 = area(33792, 2, 512)
        RA6 = area(34816, 2, 512)
        RB6 = area(35840, 2, 512)
        MW1 = area(0, NF1, 1536)
        GATE1 = area(4608, KC, E8)
        W1S = [P, P, F1 - 2 * P]
        SIL1 = area(20480, 2, 512)
        XS1 = parts(12288, 14336, KC, TOK)
        UP1 = parts(5120, 7168, 2, 1024)
        DOWN1 = parts(9216, 10240, 2, 512)
        HS1 = parts(16384, 17408, 2, 512)
        MW0 = area(0, NF0, 1536)
        GATE0 = area(44032, KC, E8)
        SIL0 = area(22016, 2, 512)
        XS0 = parts(16896, 18944, KC, TOK)
        UP0 = parts(37376, 39424, 2, 1024)
        DOWN0 = parts(41472, 42496, 2, 512)
        HS0 = parts(20992, 23040, 2, 512)

        NORMS = ["xn", "an", "mn", "cn", "dn", "en", "fn"]
        before = {p: n for n, p in enumerate(NORMS)}
        SLOT = {"c": 0, "m": 16 * B, "x": 32 * B, "n": 48 * B}

        MOE = {"m0_": 0, "m1_": E8 * NF0}
        ACC = {"m0_": 0, "m1_": E8 * TT}
        GATED = {"m0": 0, "m1": 1}
        XS_OF = {"mn": 0, "fn": 1}
        SECOND = {"d_": 0, "e_": 1}
        ROWS = {p: TT * n for n, p in enumerate(("x_", "a_", "c_", "d_", "e_"))}
        CORE = {"d_": 0, "e_": 32}
        HEADS_OUT = {"d_": 0, "e_": 16}

        block = ctx.enter_context(nc.Block())

        @block.sync
        def _(sp):
            def load(dst, name, sem):
                sp.dma_start(dst, D[name]).then_inc(S(sem), 16)

            load(X[:, :, :], "x", "ld_x")
            load(CONST[:, :], "const", "ld_const")
            load(WQ, "xq", "ld_wq")
            load(WG, "xg", "ld_wg")
            load(WK, "xk", "ld_wk")

            def tiles(b, first):
                for t in range(CT):
                    if not first:
                        sp.wait_ge(S("c_used"), b * CT + (t + 1 - CT))
                    sp.dma_start(RING[:, t, :], D["ctx0"][b, t]).then_inc(S(f"ld_slot{t}"), 16)

            tiles(0, True)
            load(WV, "xv", "ld_wv")
            load(WO, "xo", "ld_wo")
            with sp.Fori(1, B) as b:
                tiles(b, False)
            sp.wait_ge(S("c_used"), B * CT)
            load(W2, "aqkv", "ld_self")
            load(WO2, "ao", "ld_self")
            sp.wait_ge(S("x_added"), ROWS["x_"] + TT)
            sp.dma_start(GATE0, D["m0gate"]).then_inc(S("ld_gate"), 16)

            load(VEC[:, :], "vec", "ld_vec")
            load(LEN[:, :], "len", "ld_vec")

            def experts0(e, first):
                for f in range(NF0):
                    if not first:
                        sp.wait_ge(S("w_down"), e * NF0 + (f + 1 - NF0))
                    sp.dma_start(MW0[:, f, :], D["m0w"][e, f]).then_inc(S(f"ld_slot{f}"), 16)

            experts0(0, True)
            with sp.Fori(1, E8) as e:
                experts0(e, False)
            for n, name in enumerate(("cq", "ck", "cki", "cv", "cvi", "co")):
                sp.dma_start(area(25088 + 2048 * n, KC, C), D[name]).then_inc(S("ld_cross"), 16)

            def context1(b, first):
                for c in range(4):
                    if not first:
                        sp.wait_ge(S("c_v"), b * NV)
                    sp.dma_start(CC[c], D["ctx1"][b, :, 4 * CO[c]:4 * (CO[c] + CN[c])]
                                 .rearrange("p (k n) -> p k n", k=KC)).then_inc(S(f"ld_slot{c}"), 16)

            sp.wait_ge(S("moe_acc"), E8 * TT)
            sp.dma_start(IOTA, D["iota"]).then_inc(S("ld_bo"), 16)
            load(BO4, "bo", "ld_bo")
            context1(0, True)
            with sp.Fori(1, B) as b:
                context1(b, False)
            sp.wait_ge(S("x_added"), ROWS["c_"] + TT)
            load(WQ5, "dq", "ld_q")
            load(WK5, "dk", "ld_k")
            load(WV5, "dv", "ld_v")
            load(WO5, "do", "ld_o")
            load(ALIBI, "alibi", "ld_alibi")
            sp.wait_ge(S("proj_q"), 16)
            load(WQ5, "eq", "ld_q")
            sp.wait_ge(S("proj_k"), 4)
            load(WK5, "ek", "ld_k")
            sp.wait_ge(S("proj_v"), TT)
            load(WV5, "ev", "ld_v")
            sp.wait_ge(S("x_added"), ROWS["d_"] + TT)
            load(WO5, "eo", "ld_o")
            sp.wait_ge(S("proj_v"), 2 * TT)
            load(GATE1, "m1gate", "ld_gate")

            def experts1(e, first):
                for f in range(NF1):
                    if not first:
                        sp.wait_ge(S("w_down"), e * NF1 + (MOE["m1_"] + f + 1 - NF1))
                    sp.dma_start(MW1[:, f, :], D["m1w"][e, f]).then_inc(S(f"ld_slot{f}"), 16)

            experts1(0, True)
            with sp.Fori(1, E8) as e:
                experts1(e, False)
            sp.wait_ge(S("x_final"), 1)
            sp.dma_start(out, X[:, :, :]).then_inc(S("stored"), 16)
            sp.wait_ge(S("stored"), 16)

        @block.gpsimd
        def _(pool):
            chain = Link(pool, S("pool_chain"))

            def ksum_tiles(b, first):
                kb = lambda t, n: KB[0:n, t % 3 if t < CT - 1 else 3, :]
                for t in range(1, CT):
                    n = P if t < CT - 1 else LAST
                    pool.wait_ge(S("k_ready"), plus(b * CT, t + 1))
                    if t == 1:
                        if not first:
                            pool.wait_ge(S("x_kv"), b)
                        pool.tensor_tensor(KACC, kb(0, n), kb(1, n), ALU.add).then_inc(S("k_summed"), 1)
                    else:
                        pool.wait_ge(S("k_summed"), plus(b * (CT - 1), t - 1))
                        pool.tensor_tensor(KACC[0:n, :], KACC[0:n, :], kb(t, n), ALU.add).then_inc(S("k_summed"), 1)

            def rests(p, nf, e, MW, UP, DOWN):
                def up(f):
                    pool.wait_ge(S("w_up_hi"), plus(e * nf, MOE[p] + f + 1))
                    rest(pool, UP[1][:, f % 2, :], MW[:, f, 0:1024], UP[0][:, f % 2, :]).then_inc(S("w_up"), 1)

                def down(f):
                    pool.wait_ge(S("w_down_hi"), plus(e * nf, MOE[p] + f + 1))
                    rest(pool, DOWN[1][:, f % 2, :], MW[:, f, 1024:1536],
                         DOWN[0][:, f % 2, :]).then_inc(S("w_down"), 1)

                up(0)
                down(0)
                up(1)
                for f in range(nf):
                    if f + 2 < nf:
                        up(f + 2)
                    if f + 1 < nf:
                        down(f + 1)

            ksum_tiles(0, True)
            with pool.Fori(1, B) as b:
                ksum_tiles(b, False)
            pool.wait_ge(S("x_added"), ROWS["x_"] + TT)
            pool.memset(PF, 0.0).then_inc(S("a_pf0"), 1)
            rests("m0_", NF0, 0, MW0, UP0, DOWN0)
            with pool.Fori(1, E8) as e:
                rests("m0_", NF0, e, MW0, UP0, DOWN0)
            pool.wait_ge(S("moe_acc"), E8 * TT)
            pool.memset(QB4, 0.0).then_inc(S("c_qb0"), 1)

            def squares(b):
                for c in range(4):
                    v = slice(CO[c], CO[c] + CN[c])
                    for j in range(KC):
                        pool.wait_ge(S("c_kt"), plus(b * 16, 4 * c + j + 1))
                        dst = ACC4[:, v] if j == 0 else SQ4[:, 0:CN[c]]
                        chain(pool.tensor_tensor(dst, KT4[:, j, v], KT4[:, j, v], ALU.mult))
                        if j:
                            ins = pool.tensor_tensor(ACC4[:, v], ACC4[:, v], SQ4[:, 0:CN[c]], ALU.add)
                            if j < 3:
                                chain(ins)
                            else:
                                ins.then_inc(S("c_sq"), 1)

            squares(0)
            n0 = chain.n
            with pool.Fori(1, B) as b:
                chain.n, chain.base = 0, b * n0
                squares(b)
                assert chain.n == n0
            chain.n, chain.base = n0 * B, 0

            for m in range(20):
                src = QT5[:, m, :] if m < 16 else KT5[:, m - 16, :]
                acc = ACC5[:, m // 16, :]
                pool.wait_ge(S("proj_out"), m + 1)
                if m % 16 == 0:
                    chain(pool.tensor_tensor(acc, src, src, ALU.mult))
                else:
                    chain(pool.tensor_tensor(SQ5, src, src, ALU.mult))
                    ins = pool.tensor_tensor(acc, acc, SQ5, ALU.add)
                    if m in (15, 19):
                        ins.then_inc(S("d_sq"), 1)
                    else:
                        chain(ins)

            def core(p, n, PB):
                for i in range(n):
                    pool.wait_ge(S("core_rl"), CORE[p] + i + 1)
                    v = PB[:, i % 2, :].rearrange("p (h n) -> p h n", h=4)
                    pool.tensor_tensor(v, v, rl5[:, i % 2, :].unsqueeze(2).to_broadcast([P, 4, P]),
                                       ALU.mult).then_inc(S("core_pn"), 1)

            core("d_", 32, PB5)
            for m in range(20):
                v = (QT5[:, m, :] if m < 16 else KT5[:, m - 16, :]).rearrange("p (b n) -> p b n", b=B)
                ra = RA6[:, m % 2, :].rearrange("p (b n) -> p b n", b=B)
                rb = RB6[:, m % 2, :].rearrange("p (b n) -> p b n", b=B)
                pool.wait_ge(S("e_n"), m + 1)
                chain(pool.tensor_tensor(ra, v, cos6.unsqueeze(1).to_broadcast([P, B, SEQ]), ALU.mult))
                pool.wait_ge(S("e_rb"), m + 1)
                pool.tensor_tensor(v, ra, rb, ALU.add).then_inc(S("e_rope"), 1)
            core("e_", 16, PB6)
            rests("m1_", NF1, 0, MW1, UP1, DOWN1)
            with pool.Fori(1, E8) as e:
                rests("m1_", NF1, e, MW1, UP1, DOWN1)

        @block.scalar
        def _(act):
            A = nc.scalar.activation
            chain = Link(act, S("act_chain"))

            def norm(p):
                act.wait_ge(S("n_var"), before[p] * TT + TT)
                A(std, mv[:, :, 1], ACT.Sqrt, bias=eps5).then_inc(S("n_std"), 1)
                for t in range(TT):
                    act.wait_ge(S("n_xt"), before[p] * TT + t + 1)
                    A(XNT[:, :, t * P:(t + 1) * P], PS[:, t, :].rearrange("p (k n) -> p k n", k=KC),
                      ACT.Copy).then_inc(S("n_xnT"), 1)

            def gate(p):
                act.wait_ge(S("gsub"), GATED[p] + 1)
                A(gw, gw, ACT.Exp).then_inc(S("gexp"), 1)

            def experts(p, nf, e, widths, SIL, MW, UP, DOWN, first, ld):
                n0 = MOE[p]

                def up(f):
                    act.wait_ge(S(f"ld_slot{f}"), plus(e * 16, SLOT[ld] + 16))
                    if f >= 2:
                        act.wait_ge(S("moe_h"), plus(e * nf, n0 + f - 1))
                    elif not first:
                        act.wait_ge(S("moe_h"), plus(e * nf, n0))
                    A(UP[0][:, f % 2, :], MW[:, f, 0:1024], ACT.Copy).then_inc(S("w_up_hi"), 1)

                def down(f):
                    if f >= 2:
                        act.wait_ge(S("moe_out"), plus(e * nf, n0 + f - 1))
                    elif not first:
                        act.wait_ge(S("moe_out"), plus(e * nf, n0))
                    A(DOWN[0][:, f % 2, :], MW[:, f, 1024:1536], ACT.Copy).then_inc(S("w_down_hi"), 1)

                up(0)
                down(0)
                up(1)
                for f in range(nf):
                    m = widths[f]
                    act.wait_ge(S("moe_h"), plus(e * nf, n0 + f + 1))
                    if f >= 2:
                        act.wait_ge(S("moe_hT"), plus(e * nf, n0 + f - 1))
                    elif not first:
                        act.wait_ge(S("moe_hT"), plus(e * nf, n0))
                    A(SIL[0:m, f % 2, :], PS[0:m, 4 + f % 2 * 2, :], ACT.Silu).then_inc(S("moe_silu"), 1)
                    if f + 2 < nf:
                        up(f + 2)
                    if f + 1 < nf:
                        down(f + 1)

            act.wait_ge(S("eps"), 3)
            norm("xn")
            for j in range(KC):
                act.wait_ge(S("x_qmin"), j + 1)
                A(TMP[:, j % 2, :], TMP[:, j % 2, :], ACT.Exp).then_inc(S("x_qexp"), 1)
            act.wait_ge(S("x_nbg"), 1)
            for j in range(KC):
                act.wait_ge(S("x_g"), j + 1)
                A(G1[:, j, :], PS[:, 4 + j, :], ACT.Exp, bias=nbg[:, j:j + 1], scale=-1.0).then_inc(S("x_gexp"), 1)

            def ctk_out(b1):
                act.wait_ge(S("c_used"), b1 * CT)
                for c in range(KC):
                    ins = A(CTK[:, c, :], PS[:, c, :], ACT.Copy)
                ins.then_inc(S("x_ctks"), 1)

            def keys(b, first):
                for t in range(CT):
                    if t == 0 and not first:
                        ctk_out(b)
                    n = P if t < CT - 1 else LAST
                    s = t % 2 if t < CT - 1 else 2
                    act.wait_ge(S("k_min"), plus(b * CT, t + 1))
                    A(KE[0:n, s, :], KM[0:n, s, :], ACT.Exp).then_inc(S("k_exp"), 1)

            keys(0, True)
            with act.Fori(1, B) as b:
                keys(b, False)
            ctk_out(B)

            norm("an")
            for t in range(TT):
                act.wait_ge(S("a_qkv"), t + 1)
                A(QKV[:, t, 0:512], PS[:, 2 * t, :], ACT.Copy)
                A(QKV[:, t, 512:768], PS[:, 2 * t + 1, 0:256], ACT.Copy).then_inc(S("a_qkvs"), 1)
            act.wait_ge(S("a_stat"), 1)
            A(TB, TA, ACT.Square).then_inc(S("a_func"), 1)
            act.wait_ge(S("a_stat"), 2)
            A(red2, red2, ACT.Sqrt, bias=eps6, scale=1.0 / 64).then_inc(S("a_func"), 1)
            for t in range(TT):
                act.wait_ge(S("a_qt"), t + 1)
                A(QT2[:, t, :, :], PS[:, t, :].rearrange("p (c n) -> p c n", c=4), ACT.Copy).then_inc(S("a_qts"), 1)
            act.wait_ge(S("a_kt"), 1)
            A(KT2, PS[:, 4, :].rearrange("p (c n) -> p c n", c=4), ACT.Copy).then_inc(S("a_kts"), 1)
            TH = TANH
            for i in range(2 * TT):
                act.wait_ge(S("a_s"), i + 1)
                t, g = i // 2, i % 2
                v = PS[:, i, :].rearrange("p (c n) -> p c n", c=4)
                for h in (0, 1):
                    r = slice(64 * h, 64 * h + 64)
                    ins = A(TH[r, t, 4 * g:4 * g + 4, :], v[r, :, 64 * h:64 * h + 64], ACT.Tanh,
                            scale=256.0 / 8.0 / 30.0)
                ins.then_inc(S("a_tanh"), 1)
            act.wait_ge(S("a_stat"), 3)
            A(MASKED, MASKED, ACT.Exp, scale=30.0).then_inc(S("a_func"), 1)
            for i in range(2 * TT):
                act.wait_ge(S("a_pt"), i + 1)
                A(PT2[:, i % 2, :], PS[:, i % 2, :], ACT.Copy).then_inc(S("a_pts"), 1)

            norm("mn")
            gate("m0")
            experts("m0_", NF0, 0, [P] * NF0, SIL0, MW0, UP0, DOWN0, True, "m")
            with act.Fori(1, E8) as e:
                experts("m0_", NF0, e, [P] * NF0, SIL0, MW0, UP0, DOWN0, False, "m")

            norm("cn")
            act.wait_ge(S("ld_vec"), 32)
            SQQ = area(0, KC, C)
            for j in range(KC):
                act.wait_ge(S("c_q"), j + 1)
                A(QT4[:, j, :], PS[:, j, :], ACT.Identity, bias=bq1[:, j:j + 1])
                A(SQQ[:, j, :], PS[:, j, :], ACT.Square, bias=bq1[:, j:j + 1]).then_inc(S("c_qe"), 1)
            act.wait_ge(S("c_qr"), 1)
            A(RS4[:, 0:512], PS[:, 4, :], ACT.Sqrt, bias=eps6, scale=1.0 / C).then_inc(S("c_qstd"), 1)

            def cross(b, first):
                nk = 0
                for u, (kind, c, j) in enumerate(PROD):
                    bank = 4 + u % 4
                    if kind == "K":
                        act.wait_ge(S("c_k"), plus(b * 16, nk + 1))
                        nk += 1
                        lo = CO[c]
                        if c == 0:
                            A(KT4[:, j, 0:IMG], PS[:, bank, 0:IMG], ACT.Identity, bias=bki1[:, j:j + 1])
                            ins = A(KT4[:, j, IMG:CN[0]], PS[:, bank, IMG:CN[0]], ACT.Identity, bias=bk1[:, j:j + 1])
                        else:
                            ins = A(KT4[:, j, lo:lo + CN[c]], PS[:, bank, 0:CN[c]], ACT.Identity, bias=bk1[:, j:j + 1])
                        ins.then_inc(S("c_kt"), 1)
                    if kind == "R":
                        act.wait_ge(S("c_r"), plus(b * 4, c + 1))
                        A(RS4[:, CO[c]:CO[c] + CN[c]], PS[:, bank, 0:CN[c]], ACT.Sqrt, bias=eps6,
                          scale=1.0 / C).then_inc(S("c_rs"), 1)
                def out_rows(i):
                    if i % 2 == 0 and (i or not first):
                        act.wait_ge(S("c_ot"), plus(b * 4, i // 2))
                    act.wait_ge(S("c_pv"), plus(b * 8, i + 1))
                    A(OS4[:, i % 2, :], PS[:, 6, 0:64], ACT.Copy).then_inc(S("c_os"), 1)
                for i in range(8):
                    pb = PB4[:, i % 2, :]
                    act.wait_ge(S("c_max"), plus(b * 8, i + 1))
                    A(pb[:, 0:IMG], PSF[:, 0:IMG], ACT.Exp, bias=nmx[:, i % 2, 0:1],
                      accum_out=lsum[:, i % 2, 0:1]).then_inc(S("c_ei"), 1)
                    A(pb[:, IMG:CTX], pb[:, IMG:CTX], ACT.Exp, bias=nmx[:, i % 2, 1:2],
                      accum_out=lsum[:, i % 2, 1:2]).then_inc(S("c_et"), 1)
                    if i:
                        out_rows(i - 1)
                    for n, g in enumerate((0, 2)):
                        act.wait_ge(S("c_t"), plus(b * 32, 4 * i + g + 1))
                        A(PT4[:, 4 * g:4 * g + 4, :], PS[:, 4, :].rearrange("p (a n) -> p a n", a=4),
                          ACT.Copy).then_inc(S("c_pta"), 1)
                out_rows(7)

            cross(0, True)
            with act.Fori(1, B) as b:
                cross(b, False)

            norm("dn")

            def evac(p, lo, hi):
                for m in range(lo, hi):
                    dst = QT5[:, m, :] if m < 16 else KT5[:, m - 16, :]
                    if m < 16:
                        act.wait_ge(S("proj_q"), 16 * SECOND[p] + m + 1)
                    else:
                        act.wait_ge(S("proj_k"), 4 * SECOND[p] + m - 15)
                    ins = A(dst, PS[:, m % 4, :], ACT.Copy)
                    if p == "e_":
                        if m >= 2:
                            act.wait_ge(S("sq_sum"), 2 + m - 1)
                        ins = A(SQ6[:, m % 2, :], PS[:, m % 4, :], ACT.Square)
                    ins.then_inc(S("proj_out"), 1)
                    if p == "e_" and m >= 1:
                        std6(m - 1)

            def std6(m):
                act.wait_ge(S("sq_sum"), 2 + m + 1)
                if m >= 2:
                    act.wait_ge(S("e_n"), m - 1)
                A(RS6[:, m % 2, :], PS[:, 4 + m % 2, :], ACT.Sqrt, bias=eps6, scale=1.0 / 128).then_inc(S("sq_root"), 1)

            def values(p):
                for t in range(TT):
                    act.wait_ge(S("proj_v"), TT * SECOND[p] + t + 1)
                    A(V5[:, t, :], PS[:, t, :], ACT.Copy).then_inc(S("values_out"), 1)

            evac("d_", 0, 20)
            for n, w in enumerate((2048, 512)):
                act.wait_ge(S("sq_sum"), n + 1)
                A(RS5[:, n, :], PS[:, 4 + n, :], ACT.Sqrt, bias=eps6, scale=1.0 / w).then_inc(S("sq_root"), 1)
            values("d_")

            def core(p, n, PB, PT):
                def turn(i):
                    act.wait_ge(S("core_t"), CORE[p] + i + 1)
                    A(PT[:, i % 2, :], PS[:, 3 + i % 2, :], ACT.Copy).then_inc(S("core_pts"), 1)
                for i in range(n):
                    act.wait_ge(S("core_m"), CORE[p] + i + 1)
                    for h in range(4):
                        v = PB[:, i % 2, h * P:(h + 1) * P]
                        ins = A(v, v, ACT.Exp, bias=nm5[:, i % 2, h:h + 1], accum_out=l5[:, i % 2, h:h + 1])
                    ins.then_inc(S("core_e"), 1)
                    if i >= 1:
                        turn(i - 1)
                turn(n - 1)

            core("d_", 32, PB5, PT5)

            act.wait_ge(S("n_var"), before["en"] * TT + TT)
            A(std, mv[:, :, 1], ACT.Sqrt, bias=eps5).then_inc(S("n_std"), 1)

            def rms_rows(p, src):
                act.wait_ge(S("hidden"), TT if p == "en" else 2 * TT)
                for t in range(TT):
                    ins = A(HN6[:, t, :], src[:, t, :], ACT.Square, accum_out=ms[:, t:t + 1])
                    ins.then_inc(S("n_ms"), 1)
                act.wait_ge(S("n_ms"), TT if p == "en" else 2 * TT)
                A(std, ms, ACT.Sqrt, bias=eps6, scale=1.0 / C).then_inc(S("n_std"), 1)

            def rms_turn(p, w):
                for t in range(TT):
                    act.wait_ge(S("n_xt"), before[p] * TT + t + 1)
                    for k in range(KC):
                        ins = A(XNT[:, k, t * P:(t + 1) * P], PS[:, t, k * P:(k + 1) * P], ACT.Copy,
                                scale=w[:, k:k + 1])
                    ins.then_inc(S("n_xnT"), 1)

            rms_rows("en", XN)
            rms_turn("en", hw6)
            evac("e_", 0, 20)
            std6(19)
            values("e_")
            core("e_", 16, PB6, PT6)
            rms_rows("fn", XN)
            rms_turn("fn", fw6)
            gate("m1")
            experts("m1_", NF1, 0, W1S, SIL1, MW1, UP1, DOWN1, True, "n")
            with act.Fori(1, E8) as e:
                experts("m1_", NF1, e, W1S, SIL1, MW1, UP1, DOWN1, False, "n")


        @block.vector
        def _(dve):
            V = nc.vector
            link = Link(dve, S("dve_chain"))

            def norm(p):
                for t in range(TT):
                    link.at(V.bn_stats(stat[:, t, :], X[:, t, :]))
                link.sync()
                for t in range(TT):
                    V.bn_aggr(mv[:, t, :], stat[:, t, :]).then_inc(S("n_var"), 1)
                dve.wait_ge(S("n_std"), before[p] + 1 + (p in ("en", "fn")))
                link(V.reciprocal(rstd, std))
                for t in range(TT):
                    V.tensor_scalar(XN[:, t, :], X[:, t, :], mv[:, t, 0:1], rstd[:, t:t + 1],
                                    ALU.subtract, ALU.mult).then_inc(S("n_xn"), 1)

            def add_to_x(p, bank=0):
                for t in range(TT):
                    dve.wait_ge(S("rows"), ROWS[p] + t + 1)
                    V.tensor_tensor(X[:, t, :], X[:, t, :], PS[:, bank + t, :], ALU.add).then_inc(S("x_added"), 1)
                dve.wait_ge(S("x_added"), ROWS[p] + TT)

            def gate(p, eps):
                dve.wait_ge(S("glog"), GATED[p] + 1)
                lg = PS[:, 3, 0:TT * E8].rearrange("p (t e) -> p t e", t=TT)
                link(V.tensor_reduce(gs, lg, AX.X, ALU.max))
                V.tensor_tensor(gw, lg, gs.unsqueeze(2).to_broadcast([P, TT, E8]), ALU.subtract).then_inc(S("gsub"), 1)
                dve.wait_ge(S("gexp"), GATED[p] + 1)
                link(V.tensor_reduce(gs, gw, AX.X, ALU.add))
                link(V.reciprocal(gs, gs))
                link(V.tensor_tensor(gp, gw, gs.unsqueeze(2).to_broadcast([P, TT, E8]), ALU.mult))
                other = gp.unsqueeze(2).to_broadcast([P, TT, E8, E8])
                mine = gp.unsqueeze(3).to_broadcast([P, TT, E8, E8])
                r1 = area(24064, TT, E8, E8)
                r2 = area(24320, TT, E8, E8)
                link.at(V.tensor_tensor(r1, other, mine, ALU.is_gt))
                link(V.tensor_tensor(r2, other, mine, ALU.is_equal))
                tri = tri8.rearrange("p (a b) -> p a b", a=8).unsqueeze(1).to_broadcast([P, TT, E8, E8])
                link(V.tensor_tensor(r2, r2, tri, ALU.mult))
                link(V.tensor_tensor(r1, r1, r2, ALU.add))
                link(V.tensor_reduce(gw, r1, AX.X, ALU.add))
                link(V.tensor_scalar(gw, gw, 2.0, None, ALU.is_lt))
                link(V.tensor_tensor(gw, gw, gp, ALU.mult))
                link(V.tensor_reduce(gs, gw, AX.X, ALU.add))
                if eps:
                    link(V.tensor_scalar(gs, gs, eps, None, ALU.add))
                link(V.reciprocal(gs, gs))
                link(V.tensor_tensor(gw, gw, gs.unsqueeze(2).to_broadcast([P, TT, E8]), ALU.mult))

            def split_tokens(p, XS):
                dve.wait_ge(S("n_xnT"), before[p] * TT + TT)
                V.tensor_copy(XS[0], XNT[:, :, :]).then_inc(S("xs_hi"), 1)
                dve.wait_ge(S("xs_hi"), XS_OF[p] + 1)
                rest(V, XS[1], XNT[:, :, :], XS[0]).then_inc(S("xs"), 1)

            def experts(p, nf, e, widths, SIL, HS):
                for f in range(nf):
                    m = widths[f]
                    dve.wait_ge(S("moe_silu"), plus(e * nf, MOE[p] + f + 1))
                    h = SIL[0:m, f % 2, :]
                    V.tensor_tensor(h, h, PS[0:m, 5 + f % 2 * 2, :], ALU.mult).then_inc(S("h_step"), 1)
                    dve.wait_ge(S("h_step"), plus(e * 2 * nf, 2 * (MOE[p] + f) + 1))
                    V.tensor_copy(HS[0][0:m, f % 2, :], h).then_inc(S("h_step"), 1)
                    dve.wait_ge(S("h_step"), plus(e * 2 * nf, 2 * (MOE[p] + f) + 2))
                    rest(V, HS[1][0:m, f % 2, :], h, HS[0][0:m, f % 2, :]).then_inc(S("moe_hT"), 1)
                dve.wait_ge(S("moe_out"), plus(e * nf, MOE[p] + nf))
                for t in range(TT):
                    ins = V.scalar_tensor_tensor(X[:, t, :], PS[:, t, :], gw[:, t, :][:, bass.ds(e, 1)], X[:, t, :],
                                                 ALU.mult, ALU.add).then_inc(S("moe_acc"), 1)

            V.memset(eps5, 1e-5).then_inc(S("eps"), 1)
            V.memset(eps6, 1e-6).then_inc(S("eps"), 1)
            V.memset(zero1, 0.0).then_inc(S("eps"), 1)
            dve.wait_ge(S("ld_x"), 16)
            norm("xn")
            dve.wait_ge(S("ld_const"), 16)
            V.tensor_scalar(nbg, bg, -1.0, None, ALU.mult).then_inc(S("x_nbg"), 1)
            for j in range(KC):
                dve.wait_ge(S("x_q"), j + 1)
                if j >= 2:
                    link.sync()
                V.tensor_scalar(TMP[:, j % 2, :], PS[:, j, :], 0.0, None, ALU.min).then_inc(S("x_qmin"), 1)
                dve.wait_ge(S("x_qexp"), j + 1)
                link.at(V.scalar_tensor_tensor(QT[:, j, :], PS[:, j, :], 0.0, TMP[:, j % 2, :], ALU.max, ALU.add))
            link.sync()
            for j in range(KC):
                dve.wait_ge(S("x_gexp"), j + 1)
                V.tensor_scalar(G1[:, j, :], G1[:, j, :], 1.0, None, ALU.add).then_inc(S("x_pre"), 1)

            def kv_out(b0, b1):
                dve.wait_ge(S("x_kv"), b1)
                k = V.tensor_copy(ksum, PS[:, 7, 0:KC])
                link(k)
                for j in range(KC):
                    V.tensor_tensor(KV[:, bass.ds(b0, 1), j, :], PS[:, 6, j * P:(j + 1) * P].unsqueeze(1), block32.unsqueeze(1), ALU.mult)
                    ins = V.tensor_scalar(KS[:, bass.ds(b0, 1), j, :], block32.unsqueeze(1), ksum[:, j:j + 1], None, ALU.mult)
                ins.then_inc(S("x_kvs"), 1)

            def keys(b, first):
                for t in range(CT):
                    n = P if t < CT - 1 else LAST
                    s = t % 2 if t < CT - 1 else 2
                    kb = KB[0:n, t % 3 if t < CT - 1 else 3, :]
                    ps = PS[0:n, 4 + t % 2, :]
                    dve.wait_ge(S("k_ps"), plus(b * CT, t + 1))
                    V.tensor_scalar(KM[0:n, s, :], ps, 0.0, None, ALU.min).then_inc(S("k_min"), 1)
                    dve.wait_ge(S("k_exp"), plus(b * CT, t + 1))
                    if not first or t > 2:
                        dve.wait_ge(S("c_used"), plus(b * CT, t - 2))
                        dve.wait_ge(S("k_summed"), plus(b * (CT - 1), max(t - 3, 1) if t > 2 else t - 3))
                    V.scalar_tensor_tensor(kb, ps, 0.0, KE[0:n, s, :], ALU.max, ALU.add).then_inc(S("k_ready"), 1)
                    if t == 0 and not first:
                        kv_out(plus(b, -1), b)

            keys(0, True)
            n0 = link.n
            with dve.Fori(1, B) as b:
                link.n, link.base = 0, n0 + (b - 1) * 1
                keys(b, False)
                assert link.n == 1
            link.n, link.base = n0 + (B - 1), 0
            kv_out(B - 1, B)
            for j in range(KC):
                dve.wait_ge(S("x_num"), j + 1)
                link(V.tensor_scalar(DEN[:, j, :], PS[:, 4 + j, :], 1e-6, None, ALU.add))
                link(V.tensor_tensor(DEN[:, j, :], DEN[:, j, :], G1[:, j, :], ALU.mult))
                link(V.reciprocal(DEN[:, j, :], DEN[:, j, :]))
                V.tensor_tensor(AT[:, j, :], PS[:, j, :], DEN[:, j, :], ALU.mult).then_inc(S("x_aT"), 1)
            add_to_x("x_")

            norm("an")
            h12 = lambda v: v.rearrange("p t (h d) -> p (t h) d", d=64)
            for t in range(TT):
                dve.wait_ge(S("a_qkvs"), t + 1)
                q = QKV[:, t, 0:640].rearrange("p (h d) -> p h d", d=64)
                a = TA[:, t, 0:640].rearrange("p (h d) -> p h d", d=64)
                r = XR[:, t, 0:640].rearrange("p (h d) -> p h d", d=64)
                co = cosT.unsqueeze(1).to_broadcast([P, 10, 64])
                si = sinT.unsqueeze(1).to_broadcast([P, 10, 64])
                link.at(V.tensor_tensor(a, q, co, ALU.mult))
                link.at(V.tensor_tensor(r[:, :, 0:32], q[:, :, 32:64], si[:, :, 0:32], ALU.mult))
                link.at(V.tensor_tensor(r[:, :, 32:64], q[:, :, 0:32], si[:, :, 32:64], ALU.mult))
                link.at(V.tensor_copy(XR[:, t, 640:768], QKV[:, t, 640:768]))
                link.sync()
                link.at(V.tensor_tensor(r, r, a, ALU.add))
            link.sync()
            link(V.tensor_reduce(red, h12(XR), AX.X, ALU.add))
            link(V.tensor_scalar(red, red, 1.0 / 64, None, ALU.mult))
            V.tensor_tensor(h12(TA), h12(XR), red.unsqueeze(2).to_broadcast([P, 48, 64]), ALU.subtract).then_inc(S("a_stat"), 1)
            dve.wait_ge(S("a_func"), 1)
            V.tensor_reduce(red2, h12(TB), AX.X, ALU.add).then_inc(S("a_stat"), 1)
            dve.wait_ge(S("a_func"), 2)
            link(V.reciprocal(red3, red2))
            V.tensor_tensor(h12(XR), h12(TA), red3.unsqueeze(2).to_broadcast([P, 48, 64]), ALU.mult).then_inc(S("a_qkvn"), 1)
            TM = MASKED
            dve.wait_ge(S("a_tanh"), 2 * TT)
            th = TANH.rearrange("p t h n -> p (t h) n")
            link(V.tensor_tensor(TM, th, causal01.unsqueeze(1).to_broadcast([P, 32, 64]), ALU.mult))
            link(V.tensor_tensor(TM, TM, causalm1.unsqueeze(1).to_broadcast([P, 32, 64]), ALU.add))
            link(V.tensor_reduce(red[:, 0:32], TM, AX.X, ALU.max))
            V.tensor_tensor(TM, TM, red[:, 0:32].unsqueeze(2).to_broadcast([P, 32, 64]), ALU.subtract).then_inc(S("a_stat"), 1)
            dve.wait_ge(S("a_func"), 3)
            link(V.tensor_reduce(red[:, 0:32], TM, AX.X, ALU.add))
            link(V.reciprocal(red[:, 0:32], red[:, 0:32]))
            dve.wait_ge(S("a_pf0"), 1)
            pf = PF.rearrange("p t h n -> p (t h) n")
            for h in (0, 1):
                r = slice(64 * h, 64 * h + 64)
                V.tensor_tensor(pf[r, :, 64 * h:64 * h + 64], TM[r, :, :],
                                red[r, 0:32].unsqueeze(2).to_broadcast([64, 32, 64]), ALU.mult).then_inc(S("a_p"), 1)
            for t in range(TT):
                dve.wait_ge(S("a_pv"), 2 * t + 2)
                V.tensor_copy(OT2[:, :, t * P:(t + 1) * P], PS[:, 2 + t % 2, :].rearrange("p (c n) -> p c n", c=4)).then_inc(S("a_oT"), 1)
            add_to_x("a_", 4)

            norm("mn")
            split_tokens("mn", XS0)
            gate("m0", 0.0)
            experts("m0_", NF0, 0, [P] * NF0, SIL0, HS0)
            with dve.Fori(1, E8) as e:
                dve.wait_ge(S("moe_acc"), e * TT)
                experts("m0_", NF0, e, [P] * NF0, SIL0, HS0)
            dve.wait_ge(S("moe_acc"), E8 * TT)

            norm("cn")
            dve.wait_ge(S("ld_vec"), 32)
            link.at(V.tensor_copy(lens, LEN[:, :]))
            link.at(V.tensor_scalar(gqs, gq1, 1.0 / 32 ** 0.5, None, ALU.mult))
            link.at(V.tensor_tensor(bvv, bv1, bvi1, ALU.add))
            dve.wait_ge(S("c_qstd"), 1)
            link(V.reciprocal(RS4[:, 0:512], RS4[:, 0:512]))
            for j in range(KC):
                link.at(V.scalar_tensor_tensor(QT4[:, j, :], QT4[:, j, :], gqs[:, j:j + 1], RS4[:, 0:512],
                                               ALU.mult, ALU.mult))
            link.sync()
            dve.wait_ge(S("c_qb0"), 1)
            dve.wait_ge(S("ld_bo"), 32)

            def cross(b, first):
                if not first:
                    dve.wait_ge(S("c_s"), b * 8)
                for h in range(4):
                    r = slice(32 * h, 32 * h + 32)
                    link.at(V.tensor_copy(QB4[r, :, h * SEQ:(h + 1) * SEQ], QT4[r, :, bass.ds(b * SEQ, SEQ)]))
                link(V.tensor_copy(lenb, lens[:, bass.ds(b, 1)]))
                link.at(V.tensor_scalar(BIAS, IOTA, lenb, -1e9, ALU.is_ge, ALU.mult))
                nv = 0
                for u, (kind, c, j) in enumerate(PROD):
                    bank = 4 + u % 4
                    if kind == "V":
                        dve.wait_ge(S("c_v"), plus(b * NV, nv + 1))
                        if c == -2:
                            dve.wait_ge(S("c_vs"), plus(b * NV, nv))
                        nv += 1
                        n = 1 if c == -2 else TILES[c][1]
                        t = 2 if c == -2 else c
                        ins = V.tensor_copy(V4[0:n, t, :], PS[0:n, bank, :])
                        ins.then_inc(S("c_vs"), 1)
                    if kind == "R":
                        dve.wait_ge(S("c_rs"), plus(b * 4, c + 1))
                        lo, hi = CO[c], CO[c] + CN[c]
                        link(V.reciprocal(RS4[:, lo:hi], RS4[:, lo:hi]))
                        tl = IMG if c == 0 else lo
                        link(V.scalar_tensor_tensor(RS4[:, tl:hi], IOTA[:, tl - IMG:hi - IMG], lenb, RS4[:, tl:hi],
                                                    ALU.is_lt, ALU.mult))
                        for jj in range(KC):
                            if c == 0:
                                V.scalar_tensor_tensor(KT4[:, jj, 0:IMG], KT4[:, jj, 0:IMG], gki1[:, jj:jj + 1],
                                                       RS4[:, 0:IMG], ALU.mult, ALU.mult)
                            ins = V.scalar_tensor_tensor(KT4[:, jj, tl:hi], KT4[:, jj, tl:hi], gk1[:, jj:jj + 1],
                                                         RS4[:, tl:hi], ALU.mult, ALU.mult)
                        ins.then_inc(S("c_kn"), 1)

                def heads_out(j):
                    dve.wait_ge(S("c_ot"), plus(b * 4, j + 1))
                    for h in range(4):
                        r = slice(32 * h, 32 * h + 32)
                        ins = V.tensor_copy(AT4[r, j, bass.ds(b * SEQ, SEQ)],
                                            PS[r, 7, 64 * (h % 2):64 * (h % 2) + 64])
                    ins.then_inc(S("c_at"), 1)

                for i in range(8):
                    pb = PB4[:, i % 2, :]
                    dve.wait_ge(S("c_s"), plus(b * 8, i + 1))
                    link.at(V.tensor_reduce(mx[:, i % 2, 0:1], PSF[:, 0:IMG], AX.X, ALU.max))
                    link(V.tensor_tensor_reduce(pb[:, IMG:CTX], PSF[:, IMG:CTX], BIAS, 1.0, -3e38, ALU.add,
                                                ALU.max, mx[:, i % 2, 1:2]))
                    V.tensor_scalar(nmx[:, i % 2, :], mx[:, i % 2, :], -1.0, None, ALU.mult).then_inc(S("c_max"), 1)
                    dve.wait_ge(S("c_et"), plus(b * 8, i + 1))
                    link(V.reciprocal(rls[:, i % 2, :], lsum[:, i % 2, :]))
                    V.tensor_scalar(pb[:, 0:IMG], pb[:, 0:IMG], rls[:, i % 2, 0:1], None, ALU.mult)
                    V.tensor_scalar(pb[:, IMG:CTX], pb[:, IMG:CTX], rls[:, i % 2, 1:2], None,
                                    ALU.mult).then_inc(S("c_pn"), 1)
                    if i >= 2 and i % 2 == 0:
                        heads_out(i // 2 - 1)
                    dve.wait_ge(S("c_t"), plus(b * 32, 4 * i + 2))
                    V.tensor_copy(PT4[:, 4:8, :], PS[:, 5, :].rearrange("p (a n) -> p a n", a=4)).then_inc(S("c_ptd"), 1)
                    dve.wait_ge(S("c_t"), plus(b * 32, 4 * i + 4))
                    V.tensor_copy(PT4[0:65, 12, :], PS[0:65, 5, 0:P]).then_inc(S("c_ptd"), 1)
                heads_out(3)

            n1 = link.n
            cross(0, True)
            per = link.n - n1
            with dve.Fori(1, B) as b:
                link.n, link.base = 0, n1 + b * per
                cross(b, False)
                assert link.n == per
            link.n, link.base = n1 + B * per, 0
            dve.wait_ge(S("c_at"), B * 4)
            for j in range(KC):
                V.tensor_scalar(AT4[:, j, :], AT4[:, j, :], bvv[:, j:j + 1], None, ALU.add).then_inc(S("c_att"), 1)
            for t in range(TT):
                link.at(V.tensor_tensor(X[:, t, :], X[:, t, :], BO4, ALU.add))
            link.sync()
            add_to_x("c_")

            norm("dn")
            link(V.tensor_scalar(qws, qw5, 0.125, None, ALU.mult))
            for n in (0, 1):
                dve.wait_ge(S("sq_root"), n + 1)
                link(V.reciprocal(RS5[:, n, :], RS5[:, n, :]))
                for m in (range(16) if n == 0 else range(4)):
                    v, w = (QT5[:, m, :], qws[:, m:m + 1]) if n == 0 else (KT5[:, m, :], kw5[:, m:m + 1])
                    ins = V.scalar_tensor_tensor(v, v, w, RS5[:, n, :], ALU.mult, ALU.mult)
                ins.then_inc(S("d_qkn"), 1)

            def core(p, n, PB, bias, o_at):
                def rest(i):
                    dve.wait_ge(S("core_e"), CORE[p] + i + 1)
                    V.reciprocal(rl5[:, i % 2, :], l5[:, i % 2, :]).then_inc(S("core_rl"), 1)

                def outs(i):
                    dst, src, need = o_at(i)
                    dve.wait_ge(S("core_pv"), CORE[p] + need)
                    V.tensor_copy(dst, src).then_inc(S("core_oT"), 1)

                for i in range(n):
                    v = PB[:, i % 2, :].rearrange("p (h n) -> p h n", h=4)
                    dve.wait_ge(S("core_s"), CORE[p] + i + 1)
                    if i >= 2:
                        dve.wait_ge(S("core_t"), CORE[p] + i - 1)
                    ins = V.tensor_tensor(v, PS[:, i % 3, :].rearrange("p (h n) -> p h n", h=4), bias(i), ALU.add)
                    ins.then_inc(S("core_sb"), 1)
                    dve.wait_ge(S("core_sb"), CORE[p] + i + 1)
                    V.tensor_reduce(nm5[:, i % 2, :], v, AX.X, ALU.max, negate=True).then_inc(S("core_m"), 1)
                    if i >= 1:
                        rest(i - 1)
                    if i >= 4 and o_at(i - 4):
                        outs(i - 4)
                rest(n - 1)
                for i in range(n - 4, n):
                    if o_at(i):
                        outs(i)

            def o5(i):
                t, g = i // 8, i % 8
                if g % 2 == 0:
                    return None
                return (OT5[:, 4 * (g // 2):4 * (g // 2) + 4, t * P:(t + 1) * P],
                        PS[:, 5 + i // 2 % 2, :].rearrange("p (c n) -> p c n", c=4), i + 1)

            dve.wait_ge(S("ld_alibi"), 16)
            core("d_", 32, PB5, lambda i: ALIBI[:, i % 8, :, :], o5)
            add_to_x("d_")

            link_n = link
            for t in range(TT):
                link.at(V.bn_stats(stat[:, t, :], X[:, t, :]))
            link.sync()
            for t in range(TT):
                V.bn_aggr(mv[:, t, :], stat[:, t, :]).then_inc(S("n_var"), 1)
            dve.wait_ge(S("n_std"), before["en"] + 1)
            link(V.reciprocal(rstd, std))
            for t in range(TT):
                V.tensor_scalar(XN[:, t, :], X[:, t, :], mv[:, t, 0:1], rstd[:, t:t + 1],
                                ALU.subtract, ALU.mult).then_inc(S("hidden"), 1)

            def rms_rows(p):
                dve.wait_ge(S("n_std"), before[p] + 1 + (p in ("en", "fn")))
                link(V.reciprocal(rstd, std))
                for t in range(TT):
                    V.tensor_scalar(HN6[:, t, :], XN[:, t, :], rstd[:, t:t + 1], None, ALU.mult).then_inc(S("n_xn"), 1)

            rms_rows("en")
            link(V.tensor_scalar(qws[:, 0:1], qw6, 1.0 / 128 ** 0.5, None, ALU.mult))
            for m in range(20):
                v = QT5[:, m, :] if m < 16 else KT5[:, m - 16, :]
                w = qws[:, 0:1] if m < 16 else kw6
                dve.wait_ge(S("sq_root"), 2 + m + 1)
                link(V.reciprocal(RS6[:, m % 2, :], RS6[:, m % 2, :]))
                V.scalar_tensor_tensor(v, v, w, RS6[:, m % 2, :], ALU.mult, ALU.mult).then_inc(S("e_n"), 1)
                dve.wait_ge(S("e_n"), m + 1)
                if m >= 2:
                    dve.wait_ge(S("e_rope"), m - 1)
                for lo, hi in ((0, 64), (64, 0)):
                    ins = V.tensor_tensor(RB6[lo:lo + 64, m % 2, :].rearrange("p (b n) -> p b n", b=B),
                                          v[hi:hi + 64, :].rearrange("p (b n) -> p b n", b=B) if lo == 0 else
                                          v[0:64, :].rearrange("p (b n) -> p b n", b=B),
                                          sin6[(64 if lo == 0 else 0):(128 if lo == 0 else 64), :].unsqueeze(1).to_broadcast([64, B, SEQ]), ALU.mult)
                ins.then_inc(S("e_rb"), 1)

            def o6(i):
                t, g = i // 4, i % 4
                return (OT5[:, 4 * g:4 * g + 4, t * P:(t + 1) * P],
                        PS[:, 5 + i % 2, :].rearrange("p (c n) -> p c n", c=4), i + 1)

            core("e_", 16, PB6, lambda i: mask6.unsqueeze(1).to_broadcast([P, 4, P]), o6)
            for t in range(TT):
                dve.wait_ge(S("rows"), ROWS["e_"] + t + 1)
                V.tensor_tensor(XN[:, t, :], XN[:, t, :], PS[:, t, :], ALU.add).then_inc(S("hidden"), 1)
            dve.wait_ge(S("hidden"), 2 * TT)
            for t in range(TT):
                link.at(V.tensor_tensor(X[:, t, :], X[:, t, :], XN[:, t, :], ALU.add))
            rms_rows("fn")
            split_tokens("fn", XS1)
            gate("m1", 1e-9)
            experts("m1_", NF1, 0, W1S, SIL1, HS1)
            with dve.Fori(1, E8) as e:
                dve.wait_ge(S("moe_acc"), e * TT + E8 * TT)
                experts("m1_", NF1, e, W1S, SIL1, HS1)
            dve.wait_ge(S("moe_acc"), 2 * E8 * TT)
            V.memset(zero1, 0.0).then_inc(S("x_final"), 1)

        @block.tensor
        def _(pe):
            M = nc.tensor.matmul

            def M3(out, a, b, start, stop):
                M(out, a[0], b[0], start=start, stop=False)
                M(out, a[0], b[1], start=False, stop=False)
                return M(out, a[1], b[0], start=False, stop=stop)

            def norm(p):
                for t in range(TT):
                    pe.wait_ge(S("n_xn"), before[p] * TT + t + 1)
                    for k in range(KC):
                        ins = nc.tensor.transpose(PS[:, t, k * P:(k + 1) * P], XN[:, t, k * P:(k + 1) * P], ident)
                    ins.then_inc(S("n_xt"), 1)
                pe.wait_ge(S("n_xnT"), before[p] * TT + TT)

            def to_rows(p, lhs, rhs, nk, bank=0):
                for t in range(TT):
                    for k in range(nk):
                        ins = M(PS[:, bank + t, :], lhs[:, k, t * P:(t + 1) * P], rhs[:, k, :],
                                start=(k == 0), stop=(k == nk - 1))
                    ins.then_inc(S("rows"), 1)

            def gate(p, W):
                for t in range(TT):
                    for k in range(KC):
                        ins = M(PS[:, 3, t * E8:(t + 1) * E8], XNT[:, k, t * P:(t + 1) * P], W[:, k, :],
                                start=(k == 0), stop=(k == KC - 1))
                ins.then_inc(S("glog"), 1)

            def experts(p, nf, e, widths, XS, UP, DOWN, HS, first):
                if first:
                    pe.wait_ge(S("xs"), GATED[p[:-1]] + 1)

                def up(f):
                    m = widths[f]
                    pe.wait_ge(S("w_up"), plus(e * nf, MOE[p] + f + 1))
                    if f >= 2:
                        pe.wait_ge(S("moe_hT"), plus(e * nf, MOE[p] + f - 1))
                    for w in (0, 1):
                        for k in range(KC):
                            c = w * 512 + k * P
                            ins = M3(PS[0:m, 4 + f % 2 * 2 + w, :], [u[:, f % 2, c:c + m] for u in UP],
                                     [x[:, k, :] for x in XS], k == 0, k == KC - 1)
                    ins.then_inc(S("moe_h"), 1)

                def down(f):
                    m = widths[f]
                    pe.wait_ge(S("moe_hT"), plus(e * nf, MOE[p] + f + 1))
                    pe.wait_ge(S("w_down"), plus(e * nf, MOE[p] + f + 1))
                    if f == 0 and first:
                        pe.wait_ge(S("gsub"), GATED[p[:-1]] + 1)
                    if f == 0 and not first:
                        pe.wait_ge(S("moe_acc"), plus(e * TT, ACC[p]))
                    for t in range(TT):
                        ins = M3(PS[:, t, :], [h[0:m, f % 2, t * P:(t + 1) * P] for h in HS],
                                 [d[0:m, f % 2, :] for d in DOWN], f == 0, f == nf - 1)
                    ins.then_inc(S("moe_out"), 1)

                up(0)
                for f in range(nf):
                    if f + 1 < nf:
                        up(f + 1)
                    down(f)

            pe.wait_ge(S("ld_const"), 16)
            norm("xn")
            for name, W, ld, base in (("x_q", WQ, "ld_wq", 0), ("x_g", WG, "ld_wg", 4)):
                pe.wait_ge(S(ld), 16)
                for j in range(KC):
                    for k in range(KC):
                        ins = M(PS[:, base + j, :], W[:, k, j * P:(j + 1) * P], XNT[:, k, :],
                                start=(k == 0), stop=(k == KC - 1))
                    ins.then_inc(S(name), 1)
            pe.wait_ge(S("ld_wk"), 16)
            pe.wait_ge(S("x_pre"), KC)

            def kv_sum(b1):
                pe.wait_ge(S("x_ctks"), b1)
                pe.wait_ge(S("k_summed"), b1 * (CT - 1))
                for j in range(KC):
                    for k in range(KC):
                        M(PS[:, 6, j * P:(j + 1) * P], CTK[:, k, j * P:(j + 1) * P], WV[:, k, j * P:(j + 1) * P],
                          start=(k == 0), stop=(k == KC - 1))
                for j in range(KC):
                    ins = M(PS[:, 7, j:j + 1], KACC[:, j * P:(j + 1) * P], ones[:, 0:1], start=True, stop=True)
                ins.then_inc(S("x_kv"), 1)

            def keys(b, first):
                def proj(t):
                    n = P if t < CT - 1 else LAST
                    pe.wait_ge(S(f"ld_slot{t}"), plus(b * 16, SLOT["c"] + 16))
                    for k in range(KC):
                        ins = M(PS[0:n, 4 + t % 2, :], RING[:, t, k * P:k * P + n], WK[:, k, :],
                                start=(k == 0), stop=(k == KC - 1))
                    ins.then_inc(S("k_ps"), 1)

                def outer(t):
                    n = P if t < CT - 1 else LAST
                    pe.wait_ge(S("k_ready"), plus(b * CT, t + 1))
                    kb = KB[0:n, t % 3 if t < CT - 1 else 3, :]
                    for c in range(KC):
                        ins = M(PS[:, c, :], RING[0:n, t, 512 + c * P:512 + (c + 1) * P], kb,
                                start=(t == 0), stop=(t == CT - 1))
                    ins.then_inc(S("c_used"), 1)

                proj(0)
                if not first:
                    kv_sum(b)
                for t in range(CT):
                    if t + 1 < CT:
                        proj(t + 1)
                    outer(t)

            pe.wait_ge(S("ld_wv"), 16)
            keys(0, True)
            with pe.Fori(1, B) as b:
                keys(b, False)
            kv_sum(B)
            pe.wait_ge(S("x_kvs"), B)
            for j in range(KC):
                for b in range(B):
                    s = slice(b * SEQ, (b + 1) * SEQ)
                    M(PS[:, j, s], KV[:, b, j, :], QT[:, j, s], start=True, stop=True)
                    ins = M(PS[:, 4 + j, s], KS[:, b, j, :], QT[:, j, s], start=True, stop=True)
                ins.then_inc(S("x_num"), 1)
            pe.wait_ge(S("x_aT"), KC)
            pe.wait_ge(S("ld_wo"), 16)
            to_rows("x_", AT, WO, KC)

            norm("an")
            pe.wait_ge(S("ld_self"), 32)
            for t in range(TT):
                for lo, hi, bank in ((0, 512, 2 * t), (512, 768, 2 * t + 1)):
                    for k in range(KC):
                        ins = M(PS[:, bank, 0:hi - lo], XNT[:, k, t * P:(t + 1) * P], W2[:, k, lo:hi],
                                start=(k == 0), stop=(k == KC - 1))
                ins.then_inc(S("a_qkv"), 1)
            pe.wait_ge(S("a_qkvn"), 1)
            for t in range(TT):
                for c in range(4):
                    ins = nc.tensor.transpose(PS[:, t, c * P:(c + 1) * P], XR[:, t, c * P:(c + 1) * P], ident)
                ins.then_inc(S("a_qt"), 1)
            for t in range(TT):
                ins = nc.tensor.transpose(PS[:, 4, t * P:(t + 1) * P], XR[:, t, 512:640], ident)
            ins.then_inc(S("a_kt"), 1)
            pe.wait_ge(S("a_qts"), TT)
            pe.wait_ge(S("a_kts"), 1)
            for t in range(TT):
                for g in range(2):
                    r = slice(64 * g, 64 * g + 64)
                    for c in range(4):
                        ins = M(PS[:, 2 * t + g, c * P:(c + 1) * P], QT2[r, t, c, :], KT2[r, t, :],
                                start=True, stop=True)
                    ins.then_inc(S("a_s"), 1)
            pe.wait_ge(S("a_p"), 2)

            def trans(i):
                t, g = i // 2, i % 2
                if i >= 2:
                    pe.wait_ge(S("a_pts"), i - 1)
                for c in range(4):
                    ins = nc.tensor.transpose(PS[:, i % 2, c * P:(c + 1) * P], PF[:, t, 4 * g + c, :], ident)
                ins.then_inc(S("a_pt"), 1)

            trans(0)
            for i in range(2 * TT):
                t, g = i // 2, i % 2
                if i + 1 < 2 * TT:
                    trans(i + 1)
                pe.wait_ge(S("a_pts"), i + 1)
                if t >= 2 and g == 0:
                    pe.wait_ge(S("a_oT"), t - 1)
                M(PS[64 * g:64 * g + 64, 2 + t % 2, :], VAL[:, t, 64 * g:64 * g + 64], PT2[:, i % 2, :],
                  start=True, stop=True).then_inc(S("a_pv"), 1)
            pe.wait_ge(S("a_oT"), TT)
            to_rows("a_", OT2, WO2, 4, 4)

            norm("mn")
            pe.wait_ge(S("ld_gate"), 16)
            gate("m0", GATE0)
            experts("m0_", NF0, 0, [P] * NF0, XS0, UP0, DOWN0, HS0, True)
            with pe.Fori(1, E8) as e:
                experts("m0_", NF0, e, [P] * NF0, XS0, UP0, DOWN0, HS0, False)

            norm("cn")
            pe.wait_ge(S("moe_acc"), E8 * TT)
            pe.wait_ge(S("ld_cross"), 16 * 6)
            for j in range(KC):
                for k in range(KC):
                    ins = M(PS[:, j, :], WQ4[:, k, j * P:(j + 1) * P], XNT[:, k, :], start=(k == 0), stop=(k == KC - 1))
                ins.then_inc(S("c_q"), 1)
            SQQ = area(0, KC, C)
            for j in range(KC):
                pe.wait_ge(S("c_qe"), j + 1)
                ins = M(PS[:, 4, :], ones, SQQ[:, j, :], start=(j == 0), stop=(j == KC - 1))
            ins.then_inc(S("c_qr"), 1)
            pe.wait_ge(S("c_qstd"), 1)

            def cross(b, first):
                order = {"K": 0, "V": 0, "R": 0}
                at = []
                for c in range(4):
                    pe.wait_ge(S(f"ld_slot{c}"), plus(b * 16, SLOT["x"] + 16))
                if not first:
                    pe.wait_ge(S("c_at"), b * 4)
                for u, (kind, c, j) in enumerate(PROD):
                    bank = 4 + u % 4
                    if u >= 4:
                        k0, n0 = at[u - 4]
                        sem, per = {"K": ("c_kt", 16), "V": ("c_vs", NV), "R": ("c_rs", 4)}[k0]
                        pe.wait_ge(S(sem), plus(b * per, n0 + 1))
                    at.append((kind, order[kind]))
                    order[kind] += 1
                    if kind == "K":
                        for W, lo, hi in (((WKI4, 0, IMG), (WK4, IMG, CN[0])) if c == 0 else ((WK4, 0, CN[c]),)):
                            for k in range(KC):
                                ins = M(PS[:, bank, lo:hi], W[:, k, j * P:(j + 1) * P], CC[c][:, k, lo:hi],
                                        start=(k == 0), stop=(k == KC - 1))
                        ins.then_inc(S("c_k"), 1)
                    if kind == "V":
                        lo, n = (256, 1) if c == -2 else TILES[c]
                        W = WVI4 if c in (0, 1, -2) else WV4
                        ch = max(x for x in range(4) if CO[x] <= lo)
                        for k in range(KC):
                            ins = M(PS[0:n, bank, :], CC[ch][:, k, lo - CO[ch]:lo - CO[ch] + n], W[:, k, :],
                                    start=(k == 0), stop=(k == KC - 1))
                        ins.then_inc(S("c_v"), 1)
                    if kind == "R":
                        pe.wait_ge(S("c_sq"), plus(b * 4, c + 1))
                        M(PS[:, bank, 0:CN[c]], ones, ACC4[:, CO[c]:CO[c] + CN[c]], start=True,
                          stop=True).then_inc(S("c_r"), 1)
                pe.wait_ge(S("c_vs"), plus(b * NV, NV))
                pe.wait_ge(S("c_kn"), plus(b * 4, 4))

                def scores(i):
                    j, half = i // 2, i % 2
                    r = slice(64 * half, 64 * half + 64)
                    if i >= 1:
                        pe.wait_ge(S("c_ei"), plus(b * 8, i))
                    elif not first:
                        pe.wait_ge(S("c_ei"), b * 8)
                    for lo in range(0, CTX, 512):
                        hi = min(lo + 512, CTX)
                        ins = M(PS[:, lo // 512, 0:hi - lo], QB4[r, j, 128 * half:128 * half + 128], KT4[r, j, lo:hi],
                                start=True, stop=True)
                    ins.then_inc(S("c_s"), 1)

                def turn(i):
                    pe.wait_ge(S("c_pn"), plus(b * 8, i + 1))
                    for g, ts in enumerate(GROUPS):
                        if g == 2:
                            pe.wait_ge(S("c_pta"), plus(b * 16, 2 * i + 1))
                        if g == 3:
                            pe.wait_ge(S("c_ptd"), plus(b * 16, 2 * i + 1))
                        for n, t in enumerate(ts):
                            lo, w = TILES[t]
                            ins = nc.tensor.transpose(PS[0:w, 4 + g % 2, n * P:(n + 1) * P],
                                                      PB4[:, i % 2, lo:lo + w], ident)
                        ins.then_inc(S("c_t"), 1)

                def weigh(i):
                    pe.wait_ge(S("c_pta"), plus(b * 16, 2 * i + 2))
                    pe.wait_ge(S("c_ptd"), plus(b * 16, 2 * i + 2))
                    flat = [t for g in GROUPS for t in g]
                    for n, t in enumerate(flat):
                        w = TILES[t][1]
                        ins = M(PS[:, 6, 0:64], PT4[0:w, n, :], V4[0:w, t, 64 * i:64 * i + 64],
                                start=(n == 0), stop=(n == CT - 1))
                    ins.then_inc(S("c_pv"), 1)

                def rows(j):
                    pe.wait_ge(S("c_os"), plus(b * 8, 2 * j + 2))
                    if j:
                        pe.wait_ge(S("c_at"), plus(b * 4, j))
                    nc.tensor.transpose(PS[:, 7, 0:P], OS4.rearrange("p a n -> p (a n)"), ident).then_inc(S("c_ot"), 1)

                scores(0)
                for i in range(8):
                    if i < 7:
                        scores(i + 1)
                    if i >= 2 and i % 2 == 0:
                        rows(i // 2 - 1)
                    turn(i)
                    weigh(i)
                rows(3)

            cross(0, True)
            with pe.Fori(1, B) as b:
                cross(b, False)
            pe.wait_ge(S("c_att"), KC)
            to_rows("c_", AT4, WO4, KC)

            norm("dn")

            def project(p):
                for m in range(20):
                    W, c, name = (WQ5, m, "q") if m < 16 else (WK5, m - 16, "k")
                    if c == 0:
                        pe.wait_ge(S("ld_" + name), 16 if p == "d_" else 32)
                    if m >= 4:
                        pe.wait_ge(S("proj_out"), 20 * SECOND[p] + m - 3)
                    for k in range(KC):
                        ins = M(PS[:, m % 4, :], W[:, k, c * P:(c + 1) * P], XNT[:, k, :],
                                start=(k == 0), stop=(k == KC - 1))
                    ins.then_inc(S("proj_" + name), 1)
                    if p == "e_" and m >= 1:
                        squares(m - 1)
                if p == "e_":
                    squares(19)
                pe.wait_ge(S("ld_v"), 16 if p == "d_" else 32)
                pe.wait_ge(S("proj_out"), 20 * SECOND[p] + 20)
                for t in range(TT):
                    for k in range(KC):
                        ins = M(PS[:, t, :], XNT[:, k, t * P:(t + 1) * P], WV5[:, k, :],
                                start=(k == 0), stop=(k == KC - 1))
                    ins.then_inc(S("proj_v"), 1)

            def squares(m):
                pe.wait_ge(S("proj_out"), 20 + m + 1)
                if m >= 2:
                    pe.wait_ge(S("sq_root"), 2 + m - 1)
                M(PS[:, 4 + m % 2, :], ones, SQ6[:, m % 2, :], start=True, stop=True).then_inc(S("sq_sum"), 1)

            project("d_")
            for n in (0, 1):
                pe.wait_ge(S("d_sq"), n + 1)
                M(PS[:, 4 + n, :], ones, ACC5[:, n, :], start=True, stop=True).then_inc(S("sq_sum"), 1)

            def core(p, n, PB, PT, score, weigh, old):
                def turn(i):
                    pe.wait_ge(S("core_pn"), CORE[p] + i + 1)
                    if i >= 2:
                        pe.wait_ge(S("core_pts"), CORE[p] + i - 1)
                    for h in range(4):
                        ins = nc.tensor.transpose(PS[:, 3 + i % 2, h * P:(h + 1) * P],
                                                  PB[:, i % 2, h * P:(h + 1) * P], ident)
                    ins.then_inc(S("core_t"), 1)

                for i in range(n + 3):
                    if i < n:
                        if i >= 3:
                            pe.wait_ge(S("core_sb"), CORE[p] + i - 2)
                        for h in range(4):
                            q, k = score(i, h)
                            ins = M(PS[:, i % 3, h * P:(h + 1) * P], q, k, start=True, stop=True)
                        ins.then_inc(S("core_s"), 1)
                    if 2 <= i < n + 2:
                        turn(i - 2)
                    if i >= 3:
                        pe.wait_ge(S("core_pts"), CORE[p] + i - 2)
                        if old(i - 3):
                            pe.wait_ge(S("core_oT"), HEADS_OUT[p] + old(i - 3))
                        o, v = weigh(i - 3)
                        M(o, v, PT[:, (i - 3) % 2, :], start=True, stop=True).then_inc(S("core_pv"), 1)

            def score5(i, h):
                t, g = i // 8, i % 8
                r, s = slice(64 * (g % 2), 64 * (g % 2) + 64), slice(t * P, (t + 1) * P)
                return QT5[r, 4 * (g // 2) + h, s], KT5[r, g // 2, s]

            def weigh5(i):
                t, g = i // 8, i % 8
                return (PS[64 * (g % 2):64 * (g % 2) + 64, 5 + i // 2 % 2, :], V5[:, t, 64 * g:64 * g + 64])

            pe.wait_ge(S("values_out"), TT)
            pe.wait_ge(S("d_qkn"), 2)
            core("d_", 32, PB5, PT5, score5, weigh5, lambda i: max(0, i // 2 - 1) if i % 2 == 0 else 0)
            pe.wait_ge(S("ld_o"), 16)
            pe.wait_ge(S("core_oT"), 16)
            to_rows("d_", OT5, WO5, 16)

            def rms_turn(p):
                for t in range(TT):
                    pe.wait_ge(S("n_xn"), before[p] * TT + t + 1)
                    for k in range(KC):
                        ins = nc.tensor.transpose(PS[:, t, k * P:(k + 1) * P], HN6[:, t, k * P:(k + 1) * P], ident)
                    ins.then_inc(S("n_xt"), 1)
                pe.wait_ge(S("n_xnT"), before[p] * TT + TT)

            rms_turn("en")
            project("e_")

            def score6(i, h):
                t, g = i // 4, i % 4
                s = slice(t * P, (t + 1) * P)
                return QT5[:, 4 * g + h, s], KT5[:, g, s]

            def weigh6(i):
                t, g = i // 4, i % 4
                return PS[:, 5 + i % 2, :], V5[:, t, P * g:P * g + P]

            pe.wait_ge(S("values_out"), 2 * TT)
            pe.wait_ge(S("e_rope"), 20)
            core("e_", 16, PB6, PT6, score6, weigh6, lambda i: max(0, i - 1))
            pe.wait_ge(S("ld_o"), 32)
            pe.wait_ge(S("core_oT"), 32)
            to_rows("e_", OT5, WO5, 16)
            rms_turn("fn")
            pe.wait_ge(S("ld_gate"), 32)
            gate("m1", GATE1)
            experts("m1_", NF1, 0, W1S, XS1, UP1, DOWN1, HS1, True)
            with pe.Fori(1, E8) as e:
                experts("m1_", NF1, e, W1S, XS1, UP1, DOWN1, HS1, False)


def lay(w):
    n, m = w.shape
    return np.ascontiguousarray(w.reshape(n // 128, 128, m).transpose(1, 0, 2))


def constants():
    c = np.zeros((128, 964), np.float32)
    p = np.arange(128)
    c[:, 0:128] = np.eye(128)
    c[:, 128:256] = 1.0
    c[:, 256:384] = p[:, None] // 32 == p[None, :] // 32
    inv = (1.0 / np.float32(1000000.0) ** (np.arange(0, 64, 2, dtype=np.float32) / np.float32(64))).astype(np.float32)
    f = np.arange(64, dtype=np.float32)[:, None] * inv[None, :]
    cos, sin = np.cos(f), np.sin(f)
    c[:, 384:448] = np.tile(np.concatenate([cos, cos], 1), (2, 1))
    c[:, 448:512] = np.tile(np.concatenate([-sin, sin], 1), (2, 1))
    ok = (np.arange(64)[None, :] <= p[:, None] % 64).astype(np.float32)
    c[:, 512:576] = ok
    c[:, 576:640] = ok - 1
    c[:, 640:704] = (np.arange(8)[None, :] < np.arange(8)[:, None]).astype(np.float32).reshape(1, 64)
    inv = (1.0 / np.float32(1000000.0) ** (np.arange(0, 128, 2, dtype=np.float32) / np.float32(128))).astype(np.float32)
    f = (np.arange(64, dtype=np.float32)[:, None] * inv[None, :]).T
    c[:, 708:772] = np.tile(np.cos(f), (2, 1))
    c[:, 772:836] = np.concatenate([np.sin(f), -np.sin(f)], 0)
    d = p[None, :] - p[:, None]
    same = (p[None, :] // 64 == p[:, None] // 64) & (d <= 0)
    c[:, 836:964] = np.where(same, 0.0, NEG)
    return c


def alibi_bias():
    p = np.arange(128)
    d = (p[None, :] - p[:, None]).astype(np.float32)
    same = (p[None, :] // 64 == p[:, None] // 64) & (d <= 0)
    slopes = np.asarray([(2.0 ** (-8.0 / 32)) ** i for i in range(32)], np.float32)
    full = np.where(same[:, None, :], slopes[None, :, None] * d[:, None, :], np.float32(NEG)).astype(np.float32)
    return full.reshape(128, 8, 4, 128)


def arrange(i):
    f = {k: np.asarray(v) for k, v in i.items()}
    d = {}
    d["x"] = np.ascontiguousarray(f["x"].reshape(4, 128, 512).transpose(1, 0, 2))
    c = constants()
    c[:, 704:708] = f["L0_xattn_bg"].reshape(4, 128).T
    d["const"] = c
    d["xq"] = lay(f["L0_xattn_Wq"].T)
    d["xg"] = lay(f["L0_xattn_Wg"].T)
    d["xk"] = lay(f["L0_xattn_Wkv"][:512].T)
    d["xv"] = lay(f["L0_xattn_Wkv"][512:].T)
    d["xo"] = lay(f["L0_xattn_Wo"].T)
    ctx = f["ctx_2048"]
    pad = np.zeros((8, 13 * 128, 512), np.float32)
    pad[:, :1601] = ctx
    rows = pad.reshape(8, 13, 128, 512)
    cols = rows.reshape(8, 13, 128, 4, 128).transpose(0, 1, 4, 3, 2).reshape(8, 13, 128, 512)
    d["ctx0"] = np.ascontiguousarray(np.concatenate([cols, rows], -1))
    wq = f["L0_attn_Wq"].reshape(2, 4, 64, 512).transpose(1, 0, 2, 3).reshape(512, 512)
    d["aqkv"] = lay(np.concatenate([wq, f["L0_attn_Wk"], f["L0_attn_Wv"]], 0).T)
    d["ao"] = lay(f["L0_attn_Wo"].T.reshape(2, 4, 64, 512).transpose(1, 0, 2, 3).reshape(512, 512))
    d["m0gate"] = lay(f["L0_ffn_Wg"])
    w1 = f["L0_ffn_W1"].reshape(8, 4, 128, 11, 128).transpose(0, 3, 2, 1, 4).reshape(8, 11, 128, 512)
    w3 = f["L0_ffn_W3"].reshape(8, 4, 128, 11, 128).transpose(0, 3, 2, 1, 4).reshape(8, 11, 128, 512)
    w2 = f["L0_ffn_W2"].reshape(8, 11, 128, 512)
    d["m0w"] = np.ascontiguousarray(np.concatenate([w1, w3, w2], -1))
    order = np.concatenate([np.arange(257), 257 + np.arange(1280, 1344), 257 + np.arange(1280)])
    g = f["ctx_2048"][:, order].reshape(8, 1601, 4, 128).transpose(0, 3, 2, 1)
    co, cn = [0, 321, 833, 1345], [321, 512, 512, 256]
    d["ctx1"] = np.concatenate([g[..., a:a + n].reshape(8, 128, 4 * n) for a, n in zip(co, cn)], -1)
    d["iota"] = np.ascontiguousarray(np.broadcast_to((order[257:] - 257).astype(np.int16), (128, 1344)))
    d["len"] = np.ascontiguousarray(np.broadcast_to(f["_lenS2"].astype(np.int32), (128, 8)))
    for short, name in (("cq", "q"), ("ck", "k"), ("cki", "k_img"), ("cv", "v"), ("cvi", "v_img"), ("co", "o")):
        d[short] = lay(f["L1_xattn_w_" + name].T)
    d["bo"] = np.ascontiguousarray(np.broadcast_to(f["L1_xattn_b_o"], (128, 512)))
    v = np.zeros((128, 64), np.float32)
    for n, name in enumerate(("b_q", "b_k", "b_k_img", "b_v", "b_v_img", "g_q", "g_k", "g_k_img")):
        v[:, 4 * n:4 * n + 4] = f["L1_xattn_" + name].reshape(4, 128).T
    perm = lambda w: w.reshape(4, 2, 4, 64, *w.shape[1:]).swapaxes(1, 2).reshape(w.shape)
    v[:, 32:48] = perm(f["L1_attn_q_norm_w"]).reshape(16, 128).T
    v[:, 48:52] = f["L1_attn_k_norm_w"].reshape(4, 128).T
    v[:, 52:56] = f["L1_ffn_attn_norm_w"].reshape(4, 128).T
    v[:, 56] = f["L1_ffn_q_norm_w"]
    v[:, 57] = f["L1_ffn_k_norm_w"]
    v[:, 58:62] = f["L1_ffn_ffn_norm_w"].reshape(4, 128).T
    d["vec"] = v
    d["dq"] = lay(perm(f["L1_attn_wq"]).T)
    d["dk"] = lay(f["L1_attn_wk"].T)
    d["dv"] = lay(f["L1_attn_wv"].T)
    d["do"] = lay(perm(np.ascontiguousarray(f["L1_attn_wo"].T)))
    d["alibi"] = alibi_bias()
    for short, name in (("eq", "q_w"), ("ek", "k_w"), ("ev", "v_w"), ("eo", "o_w")):
        d[short] = lay(f["L1_ffn_" + name].T)
    d["m1gate"] = lay(f["L1_ffn_gate_w"].T)
    up = lambda w: np.pad(w, ((0, 0), (0, 32), (0, 0))).reshape(8, 3, 128, 4, 128).transpose(0, 1, 4, 3, 2).reshape(8, 3, 128, 512)
    down = np.pad(f["L1_ffn_wd"].transpose(0, 2, 1), ((0, 0), (0, 32), (0, 0))).reshape(8, 3, 128, 512)
    d["m1w"] = np.ascontiguousarray(np.concatenate([up(f["L1_ffn_wg"]), up(f["L1_ffn_wu"]), down], -1))
    return d


def kernel(**inputs):
    import concourse.bacc as _bacc
    from concourse import mybir as _mybir
    from concourse.bass_utils import run_bass_kernel_spmd as _run

    nc = _bacc.Bacc("TRN2", target_bir_lowering=False, num_devices=1)
    data = arrange(inputs)
    arrays, D = {}, {}
    for name, a in data.items():
        arrays[f"in_{name}"] = a
        D[name] = nc.dram_tensor(f"in_{name}", a.shape, _mybir.dt.from_np(a.dtype), kind="ExternalInput").ap()
    o = nc.dram_tensor("out_x", (128, 4, 512), _mybir.dt.float32, kind="ExternalOutput").ap()
    build(nc, D, o)
    r = _run(nc, [arrays], core_ids=[0])
    return r.results[0]["out_x"].transpose(1, 0, 2).reshape(8, 64, 512)
```

```python
from contextlib import ExitStack

import numpy as np
import concourse.bass as bass
from concourse import mybir

ALU = mybir.AluOpType
ACT = mybir.ActivationFunctionType
AX = mybir.AxisListType
F32 = mybir.dt.float32
F32R = mybir.dt.float32r
I32 = mybir.dt.int32

P = 128
B, SEQ, C = 8, 64, 512
TOK = B * SEQ
TT = TOK // P
KC = C // P
CTX = 1601
CT = 13
LAST = CTX - 12 * P
RS = 7
IMG = 257
TXT = CTX - IMG
E8 = 8
F0, F1 = 1408, 352
NF0, NF1 = F0 // P, 3
H0 = 8
NEG = -1.0e30


class Link:

    def __init__(self, eng, sem):
        self.eng, self.sem, self.n, self.base = eng, sem, 0, 0

    def __call__(self, ins):
        self.n += 1
        ins.then_inc(self.sem, 1)
        self.eng.wait_ge(self.sem, self.base + self.n)

    def at(self, ins):
        self.n += 1
        ins.then_inc(self.sem, 1)

    def sync(self):
        self.eng.wait_ge(self.sem, self.base + self.n)


def plus(a, b):
    return a + b if b else a


def build(nc, D, out):
    ctx = ExitStack()
    sems = {}

    def S(name):
        if name not in sems:
            sems[name] = ctx.enter_context(nc.semaphore(name))
        return sems[name]

    def sb(name, shape, dt=F32):
        return ctx.enter_context(nc.sbuf_tensor(name, shape, dt))

    with ctx:
        X = sb("X", [P, TT, C])
        XN = sb("XN", [P, TT, C])
        XNT = sb("XNT", [P, KC, TOK])
        CONST = sb("CONST", [P, D["const"].shape[1]])
        SM = sb("SM", [P, 512])
        VEC = sb("VEC", [P, 64])
        LEN = sb("LEN", [P, B], I32)
        with nc.sbuf_tensor("ARENA", [P, 45200], F32) as ARENA:
            pass
        PS = ctx.enter_context(nc.psum_tensor("PS", [P, 8, 512], F32))

        ident = CONST[:, 0:128]
        ones = CONST[:, 128:256]
        block32 = CONST[:, 256:384]
        cosT = CONST[:, 384:448]
        sinT = CONST[:, 448:512]
        causal01 = CONST[:, 512:576]
        causalm1 = CONST[:, 576:640]
        tri8 = CONST[:, 640:704]
        bg = CONST[:, 704:708]
        cos6, sin6 = CONST[:, 708:772], CONST[:, 772:836]
        mask6 = CONST[:, 836:964]
        PSF = PS[:, :, :].rearrange("p a b -> p (a b)")
        bq1, bk1, bki1, bv1, bvi1, gq1, gk1, gki1 = (VEC[:, 4 * n:4 * n + 4] for n in range(8))
        qw5, kw5 = VEC[:, 32:48], VEC[:, 48:52]
        hw6, qw6, kw6, fw6 = VEC[:, 52:56], VEC[:, 56:57], VEC[:, 57:58], VEC[:, 58:62]

        def area(at, *shape):
            n = int(np.prod(shape))
            v = ARENA[:, at:at + n]
            if len(shape) == 2:
                v = v.rearrange("p (a b) -> p a b", a=shape[0])
            if len(shape) == 3:
                v = v.rearrange("p (a b c) -> p a b c", a=shape[0], b=shape[1])
            return v

        def parts(hi, lo, *shape):
            both = []
            for at in (hi, lo):
                with nc.sbuf_tensor(f"before{len(split)}", [P, at], F32):
                    with nc.sbuf_tensor(f"split{len(split)}", [P, *shape], F32R) as v:
                        both.append(v[tuple(slice(None) for _ in range(1 + len(shape)))])
                split.append(at)
            return both

        split = []

        def rest(eng, dst, src, hi):
            return eng.tensor_tensor(dst, src, hi.bitcast(F32), ALU.subtract)

        small = [0]

        def tiny(*shape):
            n = int(np.prod(shape))
            v = SM[:, small[0]:small[0] + n]
            small[0] += n
            if len(shape) == 2:
                v = v.rearrange("p (a b) -> p a b", a=shape[0])
            if len(shape) == 3:
                v = v.rearrange("p (a b c) -> p a b c", a=shape[0], b=shape[1])
            return v

        eps5, eps6, zero1 = tiny(1), tiny(1), tiny(1)
        stat = tiny(TT, 6)
        mv = tiny(TT, 2)
        std = tiny(TT)
        rstd = tiny(TT)
        nbg = tiny(KC)
        ksum = tiny(KC)
        red = tiny(48)
        red2 = tiny(48)
        red3 = tiny(48)
        gp = tiny(TT, E8)
        gw = tiny(TT, E8)
        gs = tiny(TT)
        lens = tiny(B)
        lenb = tiny(1)
        gqs, bvv = tiny(KC), tiny(KC)
        mx, nmx, lsum, rls = tiny(2, 2), tiny(2, 2), tiny(2, 2), tiny(2, 2)
        qws = tiny(16)
        nm5, l5, rl5 = tiny(4, 4), tiny(4, 4), tiny(4, 4)
        ms = tiny(TT)

        WK = area(0, KC, C)
        WV = area(2048, KC, C)
        WQ = area(4096, KC, C)
        WG = area(6144, KC, C)
        WO = area(8192, KC, C)
        RING = area(10240, RS, 1024)
        WKS = parts(19456, 21504, KC, C)
        CTS = [parts(at, at + 1024, 512) for at in (17408, 6144, 4096)]
        CRS = [parts(at + 512, at + 1536, 512) for at in (17408, 6144, 4096)]
        KM = area(23552, 3, 512)
        KBS = parts(25088, 512, 3, 512)
        KB = area(26624, 4, 512)
        KACC = area(28672, 512)
        CTK = area(29184, KC, C)
        QT = area(31232, KC, TOK)
        G1 = area(33280, KC, TOK)
        KV = area(35328, B, KC, P)
        KS = area(39424, B, KC, P)
        TMP = area(43520, 2, 512)
        AT = area(10240, KC, TOK)
        DEN = area(12288, KC, TOK)
        W2 = area(16896, KC, 768)
        WO2 = area(19968, KC, C)
        QKV = area(22016, TT, 12 * 64)
        XR = area(25088, TT, 12 * 64)
        TA = area(28160, TT, 12 * 64)
        TB = area(31232, TT, 12 * 64)
        PF = area(34304, TT, H0, P)
        TANH = area(22016, TT, H0, 64)
        MASKED = area(28160, TT * H0, 64)
        VAL = XR[:, :, 640:768]
        QT2 = area(38400, TT, 4, P)
        KT2 = area(40448, TT, P)
        PT2 = area(40960, 2, 512)
        OT2 = area(41984, 4, TOK)
        WQ4, WK4, WKI4, WV4, WVI4, WO4 = (area(25152 + 2048 * n, KC, C) for n in range(6))
        CO = [0, 321, 833, 1345]
        CN = [321, 512, 512, 256]
        CC = [area(37440 + 4 * CO[c], KC, CN[c]) for c in range(4)]
        BIAS = area(43844, TXT)
        KT4 = area(0, KC, CTX + 3)
        V4 = area(6416, CT, C)
        PB4 = area(13072, 2, CTX + 3)
        PT4 = [area(16280, CT + 1, P), area(22680, CT + 1, P)]
        ACC4 = area(16280, CTX + 3)
        SQ4 = area(17884, 512)
        QT4 = area(19608, KC, TOK)
        QB4 = area(21656, KC, 4 * SEQ)
        BO4 = area(18912, C)
        IOTA = area(24472, TXT // 2).bitcast(mybir.dt.int16)
        RS4 = XNT[:, :, :].rearrange("p k n -> p (k n)")
        AT4 = XN[:, :, :]
        TILES = [(0, P), (P, P), (IMG, 64)] + [(321 + P * n, P) for n in range(10)] + [(2 * P, 1)]
        GROUPS = [[0, 1, 13, 2], [3, 4, 5, 6], [7, 8, 9, 10], [11, 12]]
        PROD = [("K", c, j) for c in range(4) for j in range(KC)]
        for t in [0, 1, "R0", 2, 13, 3, "R1", 4, 5, "R2", 6, 7, "R3", 8, 9, 10, 11, 12]:
            PROD.append(("R", int(t[1]), 0) if isinstance(t, str) else ("V", t, 0))
        NV = CT + 1
        VLAST = area(18400, C)

        def values4(t):
            return VLAST if t == CT else V4[:, t, :]
        WQ5 = area(27200, KC, 2048)
        WK5 = area(37440, KC, C)
        WV5 = area(39488, KC, C)
        WO5 = area(12288, 16, C)
        QT5 = area(0, 16, TOK)
        KT5 = area(8192, 4, TOK)
        V5 = area(10240, TT, C)
        OT5 = QT5
        ALIBI = area(20480, 8, 4, P)
        ACC5 = area(41536, 2, 512)
        SQ5 = area(42560, 512)
        RS5 = area(43072, 2, 512)
        PB5 = XNT[:, :, :]
        PT5 = XN[:, 0:2, :]
        HN6 = area(20480, TT, C)
        PT6 = area(41536, 2, 512)
        SQ6 = area(22528, 2, 512)
        RS6 = area(23552, 2, 512)
        RA6 = area(24576, 2, 512)
        RB6 = area(25600, 2, 512)
        MW1 = area(27200, NF1, 1536)
        GATE1 = area(31808, KC, E8)
        W1S = [P, P, F1 - 2 * P]
        SIL1 = area(20480, 2, 512)
        XS1 = parts(12288, 14336, KC, TOK)
        UP1 = parts(5120, 7168, 2, 1024)
        DOWN1 = parts(9216, 10240, 2, 512)
        HS1 = parts(16384, 17408, 2, 512)
        MW0 = area(0, NF0, 1536)
        GATE0 = area(44032, KC, E8)
        SIL0 = area(22016, 2, 512)
        XS0 = parts(16896, 18944, KC, TOK)
        UP0 = parts(37440, 39488, 2, 1024)
        DOWN0 = parts(41536, 42560, 2, 512)
        HS0 = parts(20992, 23040, 2, 512)

        NORMS = ["xn", "an", "mn", "cn", "dn", "en", "fn"]
        before = {p: n for n, p in enumerate(NORMS)}
        def slot_base(stage, s):
            n = "cmxn".index(stage)
            context = sum(16 * B for t in range(CT) if t % RS == s)
            return (context if n else 0) + max(n - 1, 0) * 16 * B

        MOE = {"m0_": 0, "m1_": E8 * NF0}
        ACC = {"m0_": 0, "m1_": E8 * TT}
        GATED = {"m0": 0, "m1": 1}
        XS_OF = {"mn": 0, "fn": 1}
        SECOND = {"d_": 0, "e_": 1}
        ROWS = {p: TT * n for n, p in enumerate(("x_", "a_", "c_", "d_", "e_"))}
        CORE = {"d_": 0, "e_": 32}
        HEADS_OUT = {"d_": 0, "e_": 16}

        block = ctx.enter_context(nc.Block())

        @block.sync
        def _(sp):
            def load(dst, name, sem):
                sp.dma_start(dst, D[name]).then_inc(S(sem), 16)

            load(X[:, :, :], "x", "ld_x")
            load(CONST[:, :], "const", "ld_const")
            load(WQ, "xq", "ld_wq")
            load(WG, "xg", "ld_wg")
            load(WK, "xk", "ld_wk")

            def tiles(b, first):
                for t in range(CT):
                    if t == RS and first:
                        load(WV, "xv", "ld_wv")
                        load(WO, "xo", "ld_wo")
                    if t >= RS:
                        sp.wait_ge(S("rows_split"), plus(b * CT, t - RS + 1))
                    elif not first:
                        old = t + RS if t + RS < CT else t
                        sp.wait_ge(S("rows_split"), b * CT + (old + 1 - CT))
                    sp.dma_start(RING[:, t % RS, :], D["ctx0"][b, t]).then_inc(S(f"ld_slot{t % RS}"), 16)

            tiles(0, True)
            with sp.Fori(1, B) as b:
                tiles(b, False)
            sp.wait_ge(S("c_used"), B * CT)
            load(W2, "aqkv", "ld_self")
            load(WO2, "ao", "ld_self")
            sp.wait_ge(S("x_added"), ROWS["x_"] + TT)
            sp.dma_start(GATE0, D["m0gate"]).then_inc(S("ld_gate"), 16)

            load(VEC[:, :], "vec", "ld_vec")
            load(LEN[:, :], "len", "ld_vec")

            def experts0(e, first):
                for f in range(NF0):
                    if not first:
                        sp.wait_ge(S("w_down"), e * NF0 + (f + 1 - NF0))
                    sp.dma_start(MW0[:, f, :], D["m0w"][e, f]).then_inc(S(f"ld_slot{f}"), 16)

            experts0(0, True)
            with sp.Fori(1, E8) as e:
                experts0(e, False)
            for n, name in enumerate(("cq", "ck", "cki", "cv", "cvi", "co")):
                sp.dma_start(area(25152 + 2048 * n, KC, C), D[name]).then_inc(S("ld_cross"), 16)

            def context1(b, first):
                for c in range(4):
                    if not first:
                        sp.wait_ge(S("c_v"), b * NV)
                    sp.dma_start(CC[c], D["ctx1"][b, :, 4 * CO[c]:4 * (CO[c] + CN[c])]
                                 .rearrange("p (k n) -> p k n", k=KC)).then_inc(S(f"ld_slot{c}"), 16)

            sp.wait_ge(S("moe_acc"), E8 * TT)
            sp.dma_start(IOTA, D["iota"]).then_inc(S("ld_bo"), 16)
            load(BO4, "bo", "ld_bo")
            context1(0, True)
            with sp.Fori(1, B) as b:
                context1(b, False)
            sp.wait_ge(S("c_v"), B * NV)
            load(WQ5, "dq", "ld_q")
            load(WK5, "dk", "ld_k")
            load(WV5, "dv", "ld_v")
            sp.wait_ge(S("x_added"), ROWS["c_"] + TT)
            load(WO5, "do", "ld_o")
            load(ALIBI, "alibi", "ld_alibi")
            sp.wait_ge(S("proj_q"), 16)
            load(WQ5, "eq", "ld_q")
            sp.wait_ge(S("proj_k"), 4)
            load(WK5, "ek", "ld_k")
            sp.wait_ge(S("proj_v"), TT)
            load(WV5, "ev", "ld_v")
            sp.wait_ge(S("x_added"), ROWS["d_"] + TT)
            load(WO5, "eo", "ld_o")
            sp.wait_ge(S("proj_v"), 2 * TT)
            load(GATE1, "m1gate", "ld_gate")

            def experts1(e, first):
                for f in range(NF1):
                    if not first:
                        sp.wait_ge(S("w_down"), e * NF1 + (MOE["m1_"] + f + 1 - NF1))
                    sp.dma_start(MW1[:, f, :], D["m1w"][e, f]).then_inc(S(f"ld_slot{f}"), 16)

            experts1(0, True)
            with sp.Fori(1, E8) as e:
                experts1(e, False)
            sp.wait_ge(S("x_final"), 1)
            sp.dma_start(out, X[:, :, :]).then_inc(S("stored"), 16)
            sp.wait_ge(S("stored"), 16)

        @block.gpsimd
        def _(pool):
            chain = Link(pool, S("pool_chain"))

            def ksum_tiles(b, first):
                kb = lambda t, n: KB[0:n, t % 3 if t < CT - 1 else 3, :]

                def cols(t):
                    s = t % 2 if t < CT - 1 else 2
                    pool.wait_ge(S("cols_hi"), plus(b * CT, t + 1))
                    rest(pool, CTS[s][1], RING[:, t % RS, 0:512], CTS[s][0]).then_inc(S("cols_split"), 1)

                def rows(t):
                    s = t % 2 if t < CT - 1 else 2
                    pool.wait_ge(S("rows_hi"), plus(b * CT, t + 1))
                    rest(pool, CRS[s][1], RING[:, t % RS, 512:1024], CRS[s][0]).then_inc(S("rows_split"), 1)

                cols(0)
                rows(0)
                cols(1)
                for t in range(CT):
                    n = P if t < CT - 1 else LAST
                    if t + 2 < CT:
                        cols(t + 2)
                    if t == 0:
                        rows(1)
                        continue
                    pool.wait_ge(S("k_ready"), plus(b * CT, t + 1))
                    if t == 1:
                        if not first:
                            pool.wait_ge(S("x_kv"), b)
                        pool.tensor_tensor(KACC, kb(0, n), kb(1, n), ALU.add).then_inc(S("k_summed"), 1)
                    else:
                        pool.wait_ge(S("k_summed"), plus(b * (CT - 1), t - 1))
                        pool.tensor_tensor(KACC[0:n, :], KACC[0:n, :], kb(t, n), ALU.add).then_inc(S("k_summed"), 1)
                    if t + 1 < CT:
                        rows(t + 1)

            def rests(p, nf, e, MW, UP, DOWN):
                def up(f):
                    pool.wait_ge(S("w_up_hi"), plus(e * nf, MOE[p] + f + 1))
                    rest(pool, UP[1][:, f % 2, :], MW[:, f, 0:1024], UP[0][:, f % 2, :]).then_inc(S("w_up"), 1)

                def down(f):
                    pool.wait_ge(S("w_down_hi"), plus(e * nf, MOE[p] + f + 1))
                    rest(pool, DOWN[1][:, f % 2, :], MW[:, f, 1024:1536],
                         DOWN[0][:, f % 2, :]).then_inc(S("w_down"), 1)

                up(0)
                down(0)
                up(1)
                for f in range(nf):
                    if f + 2 < nf:
                        up(f + 2)
                    if f + 1 < nf:
                        down(f + 1)

            pool.wait_ge(S("wk_hi"), 1)
            rest(pool, WKS[1], WK, WKS[0]).then_inc(S("wk_split"), 1)
            ksum_tiles(0, True)
            with pool.Fori(1, B) as b:
                ksum_tiles(b, False)
            pool.wait_ge(S("x_added"), ROWS["x_"] + TT)
            pool.memset(PF, 0.0).then_inc(S("a_pf0"), 1)
            rests("m0_", NF0, 0, MW0, UP0, DOWN0)
            with pool.Fori(1, E8) as e:
                rests("m0_", NF0, e, MW0, UP0, DOWN0)
            pool.wait_ge(S("moe_acc"), E8 * TT)
            pool.memset(QB4, 0.0).then_inc(S("c_qb0"), 1)

            def squares(b):
                for c in range(4):
                    v = slice(CO[c], CO[c] + CN[c])
                    for j in range(KC):
                        pool.wait_ge(S("c_kt"), plus(b * 16, 4 * c + j + 1))
                        dst = ACC4[:, v] if j == 0 else SQ4[:, 0:CN[c]]
                        chain(pool.tensor_tensor(dst, KT4[:, j, v], KT4[:, j, v], ALU.mult))
                        if j:
                            ins = pool.tensor_tensor(ACC4[:, v], ACC4[:, v], SQ4[:, 0:CN[c]], ALU.add)
                            if j < 3:
                                chain(ins)
                            else:
                                ins.then_inc(S("c_sq"), 1)

            squares(0)
            n0 = chain.n
            with pool.Fori(1, B) as b:
                chain.n, chain.base = 0, b * n0
                squares(b)
                assert chain.n == n0
            chain.n, chain.base = n0 * B, 0

            for m in range(20):
                src = QT5[:, m, :] if m < 16 else KT5[:, m - 16, :]
                acc = ACC5[:, m // 16, :]
                pool.wait_ge(S("proj_out"), m + 1)
                if m % 16 == 0:
                    chain(pool.tensor_tensor(acc, src, src, ALU.mult))
                else:
                    chain(pool.tensor_tensor(SQ5, src, src, ALU.mult))
                    ins = pool.tensor_tensor(acc, acc, SQ5, ALU.add)
                    if m in (15, 19):
                        ins.then_inc(S("d_sq"), 1)
                    else:
                        chain(ins)

            def core(p, n, PB):
                for i in range(n):
                    pool.wait_ge(S("core_rl"), CORE[p] + i + 1)
                    v = PB[:, i % 4, :].rearrange("p (h n) -> p h n", h=4)
                    pool.tensor_tensor(v, v, rl5[:, i % 4, :].unsqueeze(2).to_broadcast([P, 4, P]),
                                       ALU.mult).then_inc(S("core_pn"), 1)

            core("d_", 32, PB5)
            for m in range(20):
                v = (QT5[:, m, :] if m < 16 else KT5[:, m - 16, :]).rearrange("p (b n) -> p b n", b=B)
                ra = RA6[:, m % 2, :].rearrange("p (b n) -> p b n", b=B)
                rb = RB6[:, m % 2, :].rearrange("p (b n) -> p b n", b=B)
                pool.wait_ge(S("e_n"), m + 1)
                chain(pool.tensor_tensor(ra, v, cos6.unsqueeze(1).to_broadcast([P, B, SEQ]), ALU.mult))
                pool.wait_ge(S("e_rb"), m + 1)
                pool.tensor_tensor(v, ra, rb, ALU.add).then_inc(S("e_rope"), 1)
            core("e_", 16, PB5)
            rests("m1_", NF1, 0, MW1, UP1, DOWN1)
            with pool.Fori(1, E8) as e:
                rests("m1_", NF1, e, MW1, UP1, DOWN1)

        @block.scalar
        def _(act):
            A = nc.scalar.activation
            chain = Link(act, S("act_chain"))

            def norm(p):
                act.wait_ge(S("n_var"), before[p] * TT + TT)
                A(std, mv[:, :, 1], ACT.Sqrt, bias=eps5).then_inc(S("n_std"), 1)
                for t in range(TT):
                    act.wait_ge(S("n_xt"), before[p] * TT + t + 1)
                    A(XNT[:, :, t * P:(t + 1) * P], PS[:, t, :].rearrange("p (k n) -> p k n", k=KC),
                      ACT.Copy).then_inc(S("n_xnT"), 1)

            def gate(p):
                act.wait_ge(S("gsub"), GATED[p] + 1)
                A(gw, gw, ACT.Exp).then_inc(S("gexp"), 1)

            def experts(p, nf, e, widths, SIL, MW, UP, DOWN, first, ld):
                n0 = MOE[p]

                def up(f):
                    act.wait_ge(S(f"ld_slot{f}"), plus(e * 16, slot_base(ld, f) + 16))
                    if f >= 2:
                        act.wait_ge(S("moe_h"), plus(e * nf, n0 + f - 1))
                    elif not first:
                        act.wait_ge(S("moe_h"), plus(e * nf, n0))
                    A(UP[0][:, f % 2, :], MW[:, f, 0:1024], ACT.Copy).then_inc(S("w_up_hi"), 1)

                def down(f):
                    if f >= 2:
                        act.wait_ge(S("moe_out"), plus(e * nf, n0 + f - 1))
                    elif not first:
                        act.wait_ge(S("moe_out"), plus(e * nf, n0))
                    A(DOWN[0][:, f % 2, :], MW[:, f, 1024:1536], ACT.Copy).then_inc(S("w_down_hi"), 1)

                up(0)
                down(0)
                up(1)
                for f in range(nf):
                    m = widths[f]
                    act.wait_ge(S("moe_h"), plus(e * nf, n0 + f + 1))
                    if f >= 2:
                        act.wait_ge(S("moe_hT"), plus(e * nf, n0 + f - 1))
                    elif not first:
                        act.wait_ge(S("moe_hT"), plus(e * nf, n0))
                    A(SIL[0:m, f % 2, :], PS[0:m, 4 + f % 2 * 2, :], ACT.Silu).then_inc(S("moe_silu"), 1)
                    if f + 2 < nf:
                        up(f + 2)
                    if f + 1 < nf:
                        down(f + 1)

            act.wait_ge(S("eps"), 3)
            norm("xn")
            act.wait_ge(S("ld_wk"), 16)
            A(WKS[0], WK, ACT.Copy).then_inc(S("wk_hi"), 1)
            for j in range(KC):
                act.wait_ge(S("x_qmin"), j + 1)
                A(TMP[:, j % 2, :], TMP[:, j % 2, :], ACT.Exp).then_inc(S("x_qexp"), 1)

            def cols(b, t):
                s = t % 2 if t < CT - 1 else 2
                act.wait_ge(S(f"ld_slot{t % RS}"), plus(b * (32 if t % RS < CT - RS else 16), 16 * (t // RS) + 16))
                if t >= 2:
                    act.wait_ge(S("k_ps"), plus(b * CT, t - 1))
                A(CTS[s][0], RING[:, t % RS, 0:512], ACT.Copy).then_inc(S("cols_hi"), 1)

            def rows(b, t, first):
                s = t % 2 if t < CT - 1 else 2
                if t >= 2 or not first:
                    act.wait_ge(S("c_used"), plus(b * CT, t - 1 if t else -2))
                A(CRS[s][0], RING[:, t % RS, 512:1024], ACT.Copy).then_inc(S("rows_hi"), 1)

            cols(0, 0)
            rows(0, 0, True)
            act.wait_ge(S("x_nbg"), 1)
            for j in range(KC):
                act.wait_ge(S("x_g"), j + 1)
                A(G1[:, j, :], PS[:, 4 + j, :], ACT.Exp, bias=nbg[:, j:j + 1], scale=-1.0).then_inc(S("x_gexp"), 1)

            def ctk_out(b1):
                act.wait_ge(S("c_used"), b1 * CT)
                for c in range(KC):
                    ins = A(CTK[:, c, :], PS[:, c, :], ACT.Copy)
                ins.then_inc(S("x_ctks"), 1)

            def keys(b, first):
                if not first:
                    cols(b, 0)
                    rows(b, 0, False)
                cols(b, 1)
                if not first:
                    ctk_out(b)
                for t in range(CT):
                    n = P if t < CT - 1 else LAST
                    s = t % 2 if t < CT - 1 else 2
                    act.wait_ge(S("k_min"), plus(b * CT, t + 1))
                    A(KM[0:n, s, :], KM[0:n, s, :], ACT.Exp).then_inc(S("k_exp"), 1)
                    if t + 2 < CT:
                        cols(b, t + 2)
                    if t + 1 < CT:
                        rows(b, t + 1, first)

            keys(0, True)
            with act.Fori(1, B) as b:
                keys(b, False)
            ctk_out(B)

            norm("an")
            for t in range(TT):
                act.wait_ge(S("a_qkv"), t + 1)
                A(QKV[:, t, 0:512], PS[:, 2 * t, :], ACT.Copy)
                A(QKV[:, t, 512:768], PS[:, 2 * t + 1, 0:256], ACT.Copy).then_inc(S("a_qkvs"), 1)
            act.wait_ge(S("a_stat"), 1)
            A(TB, TA, ACT.Square).then_inc(S("a_func"), 1)
            act.wait_ge(S("a_stat"), 2)
            A(red2, red2, ACT.Sqrt, bias=eps6, scale=1.0 / 64).then_inc(S("a_func"), 1)
            for t in range(TT):
                act.wait_ge(S("a_qt"), t + 1)
                A(QT2[:, t, :, :], PS[:, t, :].rearrange("p (c n) -> p c n", c=4), ACT.Copy).then_inc(S("a_qts"), 1)
            act.wait_ge(S("a_kt"), 1)
            A(KT2, PS[:, 4, :].rearrange("p (c n) -> p c n", c=4), ACT.Copy).then_inc(S("a_kts"), 1)
            TH = TANH
            for i in range(2 * TT):
                act.wait_ge(S("a_s"), i + 1)
                t, g = i // 2, i % 2
                v = PS[:, i, :].rearrange("p (c n) -> p c n", c=4)
                for h in (0, 1):
                    r = slice(64 * h, 64 * h + 64)
                    ins = A(TH[r, t, 4 * g:4 * g + 4, :], v[r, :, 64 * h:64 * h + 64], ACT.Tanh,
                            scale=256.0 / 8.0 / 30.0)
                ins.then_inc(S("a_tanh"), 1)
            act.wait_ge(S("a_stat"), 3)
            A(MASKED, MASKED, ACT.Exp, scale=30.0).then_inc(S("a_func"), 1)
            for i in range(2 * TT):
                act.wait_ge(S("a_pt"), i + 1)
                A(PT2[:, i % 2, :], PS[:, i % 2, :], ACT.Copy).then_inc(S("a_pts"), 1)

            norm("mn")
            gate("m0")
            experts("m0_", NF0, 0, [P] * NF0, SIL0, MW0, UP0, DOWN0, True, "m")
            with act.Fori(1, E8) as e:
                experts("m0_", NF0, e, [P] * NF0, SIL0, MW0, UP0, DOWN0, False, "m")

            norm("cn")
            act.wait_ge(S("ld_vec"), 32)
            SQQ = area(0, KC, C)
            for j in range(KC):
                act.wait_ge(S("c_q"), j + 1)
                A(QT4[:, j, :], PS[:, j, :], ACT.Identity, bias=bq1[:, j:j + 1])
                A(SQQ[:, j, :], PS[:, j, :], ACT.Square, bias=bq1[:, j:j + 1]).then_inc(S("c_qe"), 1)
            act.wait_ge(S("c_qr"), 1)
            A(RS4[:, 0:512], PS[:, 4, :], ACT.Sqrt, bias=eps6, scale=1.0 / C).then_inc(S("c_qstd"), 1)

            def cross(b, first):
                nk = 0
                for u, (kind, c, j) in enumerate(PROD):
                    bank = 4 + u % 4
                    if kind == "K":
                        act.wait_ge(S("c_k"), plus(b * 16, nk + 1))
                        nk += 1
                        lo = CO[c]
                        if c == 0:
                            A(KT4[:, j, 0:IMG], PS[:, bank, 0:IMG], ACT.Identity, bias=bki1[:, j:j + 1])
                            ins = A(KT4[:, j, IMG:CN[0]], PS[:, bank, IMG:CN[0]], ACT.Identity, bias=bk1[:, j:j + 1])
                        else:
                            ins = A(KT4[:, j, lo:lo + CN[c]], PS[:, bank, 0:CN[c]], ACT.Identity, bias=bk1[:, j:j + 1])
                        ins.then_inc(S("c_kt"), 1)
                    if kind == "R":
                        act.wait_ge(S("c_r"), plus(b * 4, c + 1))
                        if c == 0:
                            act.wait_ge(S("c_vs"), plus(b * NV, 1))
                        A(RS4[:, CO[c]:CO[c] + CN[c]], PS[:, bank, 0:CN[c]], ACT.Sqrt, bias=eps6,
                          scale=1.0 / C).then_inc(S("c_rs"), 1)
                for i in range(8):
                    pb = PB4[:, i % 2, :]
                    act.wait_ge(S("c_max"), plus(b * 8, i + 1))
                    A(pb[:, 0:IMG], PSF[:, 0:IMG], ACT.Exp, bias=nmx[:, i % 2, 0:1],
                      accum_out=lsum[:, i % 2, 0:1]).then_inc(S("c_ei"), 1)
                    A(pb[:, IMG:CTX], pb[:, IMG:CTX], ACT.Exp, bias=nmx[:, i % 2, 1:2],
                      accum_out=lsum[:, i % 2, 1:2]).then_inc(S("c_et"), 1)
                    for g in (0, 2):
                        act.wait_ge(S("c_t"), plus(b * 32, 4 * i + g + 1))
                        A(PT4[i % 2][:, 4 * g:4 * g + 4, :],
                          PS[:, 4 + g, :].rearrange("p (a n) -> p a n", a=4), ACT.Copy).then_inc(S("c_pta"), 1)

            cross(0, True)
            with act.Fori(1, B) as b:
                cross(b, False)

            norm("dn")

            def evac(p, lo, hi):
                for m in range(lo, hi):
                    dst = QT5[:, m, :] if m < 16 else KT5[:, m - 16, :]
                    if m < 16:
                        act.wait_ge(S("proj_q"), 16 * SECOND[p] + m + 1)
                    else:
                        act.wait_ge(S("proj_k"), 4 * SECOND[p] + m - 15)
                    ins = A(dst, PS[:, m % 4, :], ACT.Copy)
                    if p == "e_":
                        if m >= 2:
                            act.wait_ge(S("sq_sum"), 2 + m - 1)
                        ins = A(SQ6[:, m % 2, :], PS[:, m % 4, :], ACT.Square)
                    ins.then_inc(S("proj_out"), 1)
                    if p == "e_" and m >= 1:
                        std6(m - 1)

            def std6(m):
                act.wait_ge(S("sq_sum"), 2 + m + 1)
                if m >= 2:
                    act.wait_ge(S("e_n"), m - 1)
                A(RS6[:, m % 2, :], PS[:, 4 + m % 2, :], ACT.Sqrt, bias=eps6, scale=1.0 / 128).then_inc(S("sq_root"), 1)

            def values(p):
                for t in range(TT):
                    if p == "d_" and t % 2 == 0:
                        n = t // 2
                        act.wait_ge(S("sq_sum"), n + 1)
                        A(RS5[:, n, :], PS[:, 4 + n, :], ACT.Sqrt, bias=eps6,
                          scale=1.0 / (512 if n else 2048)).then_inc(S("sq_root"), 1)
                    act.wait_ge(S("proj_v"), TT * SECOND[p] + t + 1)
                    A(V5[:, t, :], PS[:, t, :], ACT.Copy).then_inc(S("values_out"), 1)

            evac("d_", 0, 20)
            values("d_")

            def core(p, n, PB, PT):
                def turn(i):
                    act.wait_ge(S("core_t"), CORE[p] + i + 1)
                    A(PT[:, i % 2, :], PS[:, 3 + i % 2, :], ACT.Copy).then_inc(S("core_pts"), 1)
                for i in range(n):
                    if i >= 3:
                        turn(i - 3)
                    act.wait_ge(S("core_m"), CORE[p] + i + 1)
                    for h in range(4):
                        v = PB[:, i % 4, h * P:(h + 1) * P]
                        ins = A(v, v, ACT.Exp, bias=nm5[:, i % 4, h:h + 1], accum_out=l5[:, i % 4, h:h + 1])
                    ins.then_inc(S("core_e"), 1)
                for i in range(n - 3, n):
                    turn(i)

            core("d_", 32, PB5, PT5)

            act.wait_ge(S("n_var"), before["en"] * TT + TT)
            A(std, mv[:, :, 1], ACT.Sqrt, bias=eps5).then_inc(S("n_std"), 1)

            def rms_rows(p, src):
                act.wait_ge(S("hidden"), TT if p == "en" else 2 * TT)
                for t in range(TT):
                    ins = A(HN6[:, t, :], src[:, t, :], ACT.Square, accum_out=ms[:, t:t + 1])
                    ins.then_inc(S("n_ms"), 1)
                act.wait_ge(S("n_ms"), TT if p == "en" else 2 * TT)
                A(std, ms, ACT.Sqrt, bias=eps6, scale=1.0 / C).then_inc(S("n_std"), 1)

            def rms_turn(p, w):
                for t in range(TT):
                    act.wait_ge(S("n_xt"), before[p] * TT + t + 1)
                    for k in range(KC):
                        ins = A(XNT[:, k, t * P:(t + 1) * P], PS[:, t, k * P:(k + 1) * P], ACT.Copy,
                                scale=w[:, k:k + 1])
                    ins.then_inc(S("n_xnT"), 1)

            rms_rows("en", XN)
            rms_turn("en", hw6)
            evac("e_", 0, 20)
            std6(19)
            values("e_")
            core("e_", 16, PB5, PT6)
            rms_rows("fn", XN)
            rms_turn("fn", fw6)
            gate("m1")
            experts("m1_", NF1, 0, W1S, SIL1, MW1, UP1, DOWN1, True, "n")
            with act.Fori(1, E8) as e:
                experts("m1_", NF1, e, W1S, SIL1, MW1, UP1, DOWN1, False, "n")


        @block.vector
        def _(dve):
            V = nc.vector
            link = Link(dve, S("dve_chain"))

            def norm(p):
                for t in range(TT):
                    link.at(V.bn_stats(stat[:, t, :], X[:, t, :]))
                link.sync()
                for t in range(TT):
                    V.bn_aggr(mv[:, t, :], stat[:, t, :]).then_inc(S("n_var"), 1)
                dve.wait_ge(S("n_std"), before[p] + 1 + (p in ("en", "fn")))
                link(V.reciprocal(rstd, std))
                for t in range(TT):
                    V.tensor_scalar(XN[:, t, :], X[:, t, :], mv[:, t, 0:1], rstd[:, t:t + 1],
                                    ALU.subtract, ALU.mult).then_inc(S("n_xn"), 1)

            def add_to_x(p, bank=0):
                for t in range(TT):
                    dve.wait_ge(S("rows"), ROWS[p] + t + 1)
                    V.tensor_tensor(X[:, t, :], X[:, t, :], PS[:, bank + t, :], ALU.add).then_inc(S("x_added"), 1)
                dve.wait_ge(S("x_added"), ROWS[p] + TT)

            def gate(p, eps):
                dve.wait_ge(S("glog"), GATED[p] + 1)
                lg = PS[:, 3, 0:TT * E8].rearrange("p (t e) -> p t e", t=TT)
                link(V.tensor_reduce(gs, lg, AX.X, ALU.max))
                V.tensor_tensor(gw, lg, gs.unsqueeze(2).to_broadcast([P, TT, E8]), ALU.subtract).then_inc(S("gsub"), 1)
                dve.wait_ge(S("gexp"), GATED[p] + 1)
                link(V.tensor_reduce(gs, gw, AX.X, ALU.add))
                link(V.reciprocal(gs, gs))
                link(V.tensor_tensor(gp, gw, gs.unsqueeze(2).to_broadcast([P, TT, E8]), ALU.mult))
                other = gp.unsqueeze(2).to_broadcast([P, TT, E8, E8])
                mine = gp.unsqueeze(3).to_broadcast([P, TT, E8, E8])
                r1 = area(24064, TT, E8, E8)
                r2 = area(24320, TT, E8, E8)
                link.at(V.tensor_tensor(r1, other, mine, ALU.is_gt))
                link(V.tensor_tensor(r2, other, mine, ALU.is_equal))
                tri = tri8.rearrange("p (a b) -> p a b", a=8).unsqueeze(1).to_broadcast([P, TT, E8, E8])
                link(V.tensor_tensor(r2, r2, tri, ALU.mult))
                link(V.tensor_tensor(r1, r1, r2, ALU.add))
                link(V.tensor_reduce(gw, r1, AX.X, ALU.add))
                link(V.tensor_scalar(gw, gw, 2.0, None, ALU.is_lt))
                link(V.tensor_tensor(gw, gw, gp, ALU.mult))
                link(V.tensor_reduce(gs, gw, AX.X, ALU.add))
                if eps:
                    link(V.tensor_scalar(gs, gs, eps, None, ALU.add))
                link(V.reciprocal(gs, gs))
                link(V.tensor_tensor(gw, gw, gs.unsqueeze(2).to_broadcast([P, TT, E8]), ALU.mult))

            def split_tokens(p, XS):
                dve.wait_ge(S("n_xnT"), before[p] * TT + TT)
                V.tensor_copy(XS[0], XNT[:, :, :]).then_inc(S("xs_hi"), 1)
                dve.wait_ge(S("xs_hi"), XS_OF[p] + 1)
                rest(V, XS[1], XNT[:, :, :], XS[0]).then_inc(S("xs"), 1)

            def experts(p, nf, e, widths, SIL, HS):
                for f in range(nf):
                    m = widths[f]
                    dve.wait_ge(S("moe_silu"), plus(e * nf, MOE[p] + f + 1))
                    h = SIL[0:m, f % 2, :]
                    V.tensor_tensor(h, h, PS[0:m, 5 + f % 2 * 2, :], ALU.mult).then_inc(S("h_step"), 1)
                    dve.wait_ge(S("h_step"), plus(e * 2 * nf, 2 * (MOE[p] + f) + 1))
                    V.tensor_copy(HS[0][0:m, f % 2, :], h).then_inc(S("h_step"), 1)
                    dve.wait_ge(S("h_step"), plus(e * 2 * nf, 2 * (MOE[p] + f) + 2))
                    rest(V, HS[1][0:m, f % 2, :], h, HS[0][0:m, f % 2, :]).then_inc(S("moe_hT"), 1)
                dve.wait_ge(S("moe_out"), plus(e * nf, MOE[p] + nf))
                for t in range(TT):
                    ins = V.scalar_tensor_tensor(X[:, t, :], PS[:, t, :], gw[:, t, :][:, bass.ds(e, 1)], X[:, t, :],
                                                 ALU.mult, ALU.add).then_inc(S("moe_acc"), 1)

            V.memset(eps5, 1e-5).then_inc(S("eps"), 1)
            V.memset(eps6, 1e-6).then_inc(S("eps"), 1)
            V.memset(zero1, 0.0).then_inc(S("eps"), 1)
            dve.wait_ge(S("ld_x"), 16)
            norm("xn")
            dve.wait_ge(S("ld_const"), 16)
            V.tensor_scalar(nbg, bg, -1.0, None, ALU.mult).then_inc(S("x_nbg"), 1)
            for j in range(KC):
                dve.wait_ge(S("x_q"), j + 1)
                if j >= 2:
                    link.sync()
                V.tensor_scalar(TMP[:, j % 2, :], PS[:, j, :], 0.0, None, ALU.min).then_inc(S("x_qmin"), 1)
                dve.wait_ge(S("x_qexp"), j + 1)
                link.at(V.scalar_tensor_tensor(QT[:, j, :], PS[:, j, :], 0.0, TMP[:, j % 2, :], ALU.max, ALU.add))
            link.sync()
            for j in range(KC):
                dve.wait_ge(S("x_gexp"), j + 1)
                V.tensor_scalar(G1[:, j, :], G1[:, j, :], 1.0, None, ALU.add).then_inc(S("x_pre"), 1)

            def kv_out(b0, b1):
                dve.wait_ge(S("x_kv"), b1)
                k = V.tensor_copy(ksum, PS[:, 7, 0:KC])
                link(k)
                for j in range(KC):
                    V.tensor_tensor(KV[:, bass.ds(b0, 1), j, :], PS[:, 6, j * P:(j + 1) * P].unsqueeze(1), block32.unsqueeze(1), ALU.mult)
                    ins = V.tensor_scalar(KS[:, bass.ds(b0, 1), j, :], block32.unsqueeze(1), ksum[:, j:j + 1], None, ALU.mult)
                ins.then_inc(S("x_kvs"), 1)

            def keys(b, first):
                for t in range(CT):
                    n = P if t < CT - 1 else LAST
                    s = t % 2 if t < CT - 1 else 2
                    kb = KB[0:n, t % 3 if t < CT - 1 else 3, :]
                    ps = PS[0:n, 4 + t % 2, :]
                    dve.wait_ge(S("k_ps"), plus(b * CT, t + 1))
                    V.tensor_scalar(KM[0:n, s, :], ps, 0.0, None, ALU.min).then_inc(S("k_min"), 1)
                    dve.wait_ge(S("k_exp"), plus(b * CT, t + 1))
                    if not first or t > 2:
                        dve.wait_ge(S("k_summed"), plus(b * (CT - 1), max(t - 3, 1) if t > 2 else t - 3))
                    V.scalar_tensor_tensor(kb, ps, 0.0, KM[0:n, s, :], ALU.max, ALU.add).then_inc(S("k_ready"), 1)
                    if not first or t >= 2:
                        dve.wait_ge(S("c_used"), plus(b * CT, t - 1))
                    dve.wait_ge(S("k_ready"), plus(b * CT, t + 1))
                    V.tensor_copy(KBS[0][0:n, s, :], kb).then_inc(S("k_hi"), 1)
                    dve.wait_ge(S("k_hi"), plus(b * CT, t + 1))
                    rest(V, KBS[1][0:n, s, :], kb, KBS[0][0:n, s, :]).then_inc(S("k_split"), 1)
                    if t == 0 and not first:
                        kv_out(plus(b, -1), b)

            keys(0, True)
            n0 = link.n
            with dve.Fori(1, B) as b:
                link.n, link.base = 0, n0 + (b - 1) * 1
                keys(b, False)
                assert link.n == 1
            link.n, link.base = n0 + (B - 1), 0
            kv_out(B - 1, B)
            for j in range(KC):
                dve.wait_ge(S("x_num"), j + 1)
                link(V.tensor_scalar(DEN[:, j, :], PS[:, 4 + j, :], 1e-6, None, ALU.add))
                link(V.tensor_tensor(DEN[:, j, :], DEN[:, j, :], G1[:, j, :], ALU.mult))
                link(V.reciprocal(DEN[:, j, :], DEN[:, j, :]))
                V.tensor_tensor(AT[:, j, :], PS[:, j, :], DEN[:, j, :], ALU.mult).then_inc(S("x_aT"), 1)
            add_to_x("x_")

            norm("an")
            h12 = lambda v: v.rearrange("p t (h d) -> p (t h) d", d=64)
            for t in range(TT):
                dve.wait_ge(S("a_qkvs"), t + 1)
                q = QKV[:, t, 0:640].rearrange("p (h d) -> p h d", d=64)
                a = TA[:, t, 0:640].rearrange("p (h d) -> p h d", d=64)
                r = XR[:, t, 0:640].rearrange("p (h d) -> p h d", d=64)
                co = cosT.unsqueeze(1).to_broadcast([P, 10, 64])
                si = sinT.unsqueeze(1).to_broadcast([P, 10, 64])
                link.at(V.tensor_tensor(a, q, co, ALU.mult))
                link.at(V.tensor_tensor(r[:, :, 0:32], q[:, :, 32:64], si[:, :, 0:32], ALU.mult))
                link.at(V.tensor_tensor(r[:, :, 32:64], q[:, :, 0:32], si[:, :, 32:64], ALU.mult))
                link.at(V.tensor_copy(XR[:, t, 640:768], QKV[:, t, 640:768]))
                link.sync()
                link.at(V.tensor_tensor(r, r, a, ALU.add))
            link.sync()
            link(V.tensor_reduce(red, h12(XR), AX.X, ALU.add))
            link(V.tensor_scalar(red, red, 1.0 / 64, None, ALU.mult))
            V.tensor_tensor(h12(TA), h12(XR), red.unsqueeze(2).to_broadcast([P, 48, 64]), ALU.subtract).then_inc(S("a_stat"), 1)
            dve.wait_ge(S("a_func"), 1)
            V.tensor_reduce(red2, h12(TB), AX.X, ALU.add).then_inc(S("a_stat"), 1)
            dve.wait_ge(S("a_func"), 2)
            link(V.reciprocal(red3, red2))
            V.tensor_tensor(h12(XR), h12(TA), red3.unsqueeze(2).to_broadcast([P, 48, 64]), ALU.mult).then_inc(S("a_qkvn"), 1)
            TM = MASKED
            dve.wait_ge(S("a_tanh"), 2 * TT)
            th = TANH.rearrange("p t h n -> p (t h) n")
            link(V.tensor_tensor(TM, th, causal01.unsqueeze(1).to_broadcast([P, 32, 64]), ALU.mult))
            link(V.tensor_tensor(TM, TM, causalm1.unsqueeze(1).to_broadcast([P, 32, 64]), ALU.add))
            link(V.tensor_reduce(red[:, 0:32], TM, AX.X, ALU.max))
            V.tensor_tensor(TM, TM, red[:, 0:32].unsqueeze(2).to_broadcast([P, 32, 64]), ALU.subtract).then_inc(S("a_stat"), 1)
            dve.wait_ge(S("a_func"), 3)
            link(V.tensor_reduce(red[:, 0:32], TM, AX.X, ALU.add))
            link(V.reciprocal(red[:, 0:32], red[:, 0:32]))
            dve.wait_ge(S("a_pf0"), 1)
            pf = PF.rearrange("p t h n -> p (t h) n")
            for h in (0, 1):
                r = slice(64 * h, 64 * h + 64)
                V.tensor_tensor(pf[r, :, 64 * h:64 * h + 64], TM[r, :, :],
                                red[r, 0:32].unsqueeze(2).to_broadcast([64, 32, 64]), ALU.mult).then_inc(S("a_p"), 1)
            for t in range(TT):
                dve.wait_ge(S("a_pv"), 2 * t + 2)
                V.tensor_copy(OT2[:, :, t * P:(t + 1) * P], PS[:, 2 + t % 2, :].rearrange("p (c n) -> p c n", c=4)).then_inc(S("a_oT"), 1)
            add_to_x("a_", 4)

            norm("mn")
            split_tokens("mn", XS0)
            gate("m0", 0.0)
            experts("m0_", NF0, 0, [P] * NF0, SIL0, HS0)
            with dve.Fori(1, E8) as e:
                dve.wait_ge(S("moe_acc"), e * TT)
                experts("m0_", NF0, e, [P] * NF0, SIL0, HS0)
            dve.wait_ge(S("moe_acc"), E8 * TT)

            norm("cn")
            dve.wait_ge(S("ld_vec"), 32)
            link.at(V.tensor_copy(lens, LEN[:, :]))
            link.at(V.tensor_scalar(gqs, gq1, 1.0 / 32 ** 0.5, None, ALU.mult))
            link.at(V.tensor_tensor(bvv, bv1, bvi1, ALU.add))
            dve.wait_ge(S("c_qstd"), 1)
            link(V.reciprocal(RS4[:, 0:512], RS4[:, 0:512]))
            for j in range(KC):
                link.at(V.scalar_tensor_tensor(QT4[:, j, :], QT4[:, j, :], gqs[:, j:j + 1], RS4[:, 0:512],
                                               ALU.mult, ALU.mult))
            link.sync()
            dve.wait_ge(S("c_qb0"), 1)
            dve.wait_ge(S("ld_bo"), 32)

            def cross(b, first):
                if not first:
                    dve.wait_ge(S("c_s"), b * 8)
                for h in range(4):
                    r = slice(32 * h, 32 * h + 32)
                    link.at(V.tensor_copy(QB4[r, :, h * SEQ:(h + 1) * SEQ], QT4[r, :, bass.ds(b * SEQ, SEQ)]))
                link(V.tensor_copy(lenb, lens[:, bass.ds(b, 1)]))
                link.at(V.tensor_scalar(BIAS, IOTA, lenb, -1e9, ALU.is_ge, ALU.mult))
                def maximum(i):
                    pb = PB4[:, i % 2, :]
                    dve.wait_ge(S("c_s"), plus(b * 8, i + 1))
                    link.at(V.tensor_reduce(mx[:, i % 2, 0:1], PSF[:, 0:IMG], AX.X, ALU.max))
                    link(V.tensor_tensor_reduce(pb[:, IMG:CTX], PSF[:, IMG:CTX], BIAS, 1.0, -3e38, ALU.add,
                                                ALU.max, mx[:, i % 2, 1:2]))
                    V.tensor_scalar(nmx[:, i % 2, :], mx[:, i % 2, :], -1.0, None, ALU.mult).then_inc(S("c_max"), 1)

                nv = 0
                for u, (kind, c, j) in enumerate(PROD):
                    bank = 4 + u % 4
                    if u == len(PROD) - 1:
                        maximum(0)
                    if kind == "V":
                        dve.wait_ge(S("c_v"), plus(b * NV, nv + 1))
                        nv += 1
                        n = TILES[c][1]
                        ins = V.tensor_copy(values4(c)[0:n, :], PS[0:n, bank, :])
                        ins.then_inc(S("c_vs"), 1)
                    if kind == "R":
                        dve.wait_ge(S("c_rs"), plus(b * 4, c + 1))
                        lo, hi = CO[c], CO[c] + CN[c]
                        link(V.reciprocal(RS4[:, lo:hi], RS4[:, lo:hi]))
                        tl = IMG if c == 0 else lo
                        link(V.scalar_tensor_tensor(RS4[:, tl:hi], IOTA[:, tl - IMG:hi - IMG], lenb, RS4[:, tl:hi],
                                                    ALU.is_lt, ALU.mult))
                        for jj in range(KC):
                            if c == 0:
                                V.scalar_tensor_tensor(KT4[:, jj, 0:IMG], KT4[:, jj, 0:IMG], gki1[:, jj:jj + 1],
                                                       RS4[:, 0:IMG], ALU.mult, ALU.mult)
                            ins = V.scalar_tensor_tensor(KT4[:, jj, tl:hi], KT4[:, jj, tl:hi], gk1[:, jj:jj + 1],
                                                         RS4[:, tl:hi], ALU.mult, ALU.mult)
                        ins.then_inc(S("c_kn"), 1)

                def turned(i):
                    dve.wait_ge(S("c_t"), plus(b * 32, 4 * i + 2))
                    V.tensor_copy(PT4[i % 2][:, 4:8, :], PS[:, 5, :].rearrange("p (a n) -> p a n", a=4)).then_inc(S("c_ptd"), 1)
                    dve.wait_ge(S("c_t"), plus(b * 32, 4 * i + 4))
                    V.tensor_copy(PT4[i % 2][:, 12:14, :], PS[:, 4, 0:2 * P].rearrange("p (a n) -> p a n", a=2)).then_inc(S("c_ptd"), 1)

                def heads_out(i):
                    dve.wait_ge(S("c_pv"), plus(b * 8, i + 1))
                    for h in (0, 1):
                        lo = 64 * (i % 2) + 32 * h
                        ins = V.tensor_copy(AT4[lo:lo + 32, i // 2, bass.ds(b * SEQ, SEQ)],
                                            PS[lo:lo + 32, 7, 64 * h:64 * h + 64])
                    ins.then_inc(S("c_at"), 1)

                for i in range(8):
                    pb = PB4[:, i % 2, :]
                    if i:
                        maximum(i)
                    if i:
                        turned(i - 1)
                    dve.wait_ge(S("c_et"), plus(b * 8, i + 1))
                    link(V.reciprocal(rls[:, i % 2, :], lsum[:, i % 2, :]))
                    V.tensor_scalar(pb[:, 0:IMG], pb[:, 0:IMG], rls[:, i % 2, 0:1], None, ALU.mult)
                    V.tensor_scalar(pb[:, IMG:CTX], pb[:, IMG:CTX], rls[:, i % 2, 1:2], None,
                                    ALU.mult).then_inc(S("c_pn"), 1)
                    if i >= 2:
                        heads_out(i - 2)
                turned(7)
                heads_out(6)
                heads_out(7)

            n1 = link.n
            cross(0, True)
            per = link.n - n1
            with dve.Fori(1, B) as b:
                link.n, link.base = 0, n1 + b * per
                cross(b, False)
                assert link.n == per
            link.n, link.base = n1 + B * per, 0
            dve.wait_ge(S("c_at"), B * 8)
            for j in range(KC):
                V.tensor_scalar(AT4[:, j, :], AT4[:, j, :], bvv[:, j:j + 1], None, ALU.add).then_inc(S("c_att"), 1)
            for t in range(TT):
                link.at(V.tensor_tensor(X[:, t, :], X[:, t, :], BO4, ALU.add))
            link.sync()
            add_to_x("c_")

            norm("dn")
            link(V.tensor_scalar(qws, qw5, 0.125, None, ALU.mult))
            for n in (0, 1):
                dve.wait_ge(S("sq_root"), n + 1)
                link(V.reciprocal(RS5[:, n, :], RS5[:, n, :]))
                for m in (range(16) if n == 0 else range(4)):
                    v, w = (QT5[:, m, :], qws[:, m:m + 1]) if n == 0 else (KT5[:, m, :], kw5[:, m:m + 1])
                    ins = V.scalar_tensor_tensor(v, v, w, RS5[:, n, :], ALU.mult, ALU.mult)
                ins.then_inc(S("d_qkn"), 1)

            def core(p, n, PB, bias, o_at):
                def recip(i):
                    dve.wait_ge(S("core_e"), CORE[p] + i + 1)
                    V.reciprocal(rl5[:, i % 4, :], l5[:, i % 4, :]).then_inc(S("core_rl"), 1)

                def outs(i):
                    dst, src, need = o_at(i)
                    dve.wait_ge(S("core_pv"), CORE[p] + need)
                    V.tensor_copy(dst, src).then_inc(S("core_oT"), 1)

                for i in range(n):
                    v = PB[:, i % 4, :].rearrange("p (h n) -> p h n", h=4)
                    dve.wait_ge(S("core_s"), CORE[p] + i + 1)
                    if i >= 4:
                        dve.wait_ge(S("core_t"), CORE[p] + i - 3)
                    ins = V.tensor_tensor(v, PS[:, i % 3, :].rearrange("p (h n) -> p h n", h=4), bias(i), ALU.add)
                    ins.then_inc(S("core_sb"), 1)
                    if i >= 2:
                        recip(i - 2)
                    dve.wait_ge(S("core_sb"), CORE[p] + i + 1)
                    V.tensor_reduce(nm5[:, i % 4, :], v, AX.X, ALU.max, negate=True).then_inc(S("core_m"), 1)
                    if i >= 5 and o_at(i - 5):
                        outs(i - 5)
                recip(n - 2)
                recip(n - 1)
                for i in range(n - 5, n):
                    if o_at(i):
                        outs(i)

            def o5(i):
                t, g = i // 8, i % 8
                if g % 2 == 0:
                    return None
                return (OT5[:, 4 * (g // 2):4 * (g // 2) + 4, t * P:(t + 1) * P],
                        PS[:, 5 + i // 2 % 2, :].rearrange("p (c n) -> p c n", c=4), i + 1)

            dve.wait_ge(S("ld_alibi"), 16)
            core("d_", 32, PB5, lambda i: ALIBI[:, i % 8, :, :], o5)
            add_to_x("d_")

            link_n = link
            for t in range(TT):
                link.at(V.bn_stats(stat[:, t, :], X[:, t, :]))
            link.sync()
            for t in range(TT):
                V.bn_aggr(mv[:, t, :], stat[:, t, :]).then_inc(S("n_var"), 1)
            dve.wait_ge(S("n_std"), before["en"] + 1)
            link(V.reciprocal(rstd, std))
            for t in range(TT):
                V.tensor_scalar(XN[:, t, :], X[:, t, :], mv[:, t, 0:1], rstd[:, t:t + 1],
                                ALU.subtract, ALU.mult).then_inc(S("hidden"), 1)

            def rms_rows(p):
                dve.wait_ge(S("n_std"), before[p] + 1 + (p in ("en", "fn")))
                link(V.reciprocal(rstd, std))
                for t in range(TT):
                    V.tensor_scalar(HN6[:, t, :], XN[:, t, :], rstd[:, t:t + 1], None, ALU.mult).then_inc(S("n_xn"), 1)

            rms_rows("en")
            link(V.tensor_scalar(qws[:, 0:1], qw6, 1.0 / 128 ** 0.5, None, ALU.mult))
            for m in range(20):
                v = QT5[:, m, :] if m < 16 else KT5[:, m - 16, :]
                w = qws[:, 0:1] if m < 16 else kw6
                dve.wait_ge(S("sq_root"), 2 + m + 1)
                link(V.reciprocal(RS6[:, m % 2, :], RS6[:, m % 2, :]))
                V.scalar_tensor_tensor(v, v, w, RS6[:, m % 2, :], ALU.mult, ALU.mult).then_inc(S("e_n"), 1)
                dve.wait_ge(S("e_n"), m + 1)
                if m >= 2:
                    dve.wait_ge(S("e_rope"), m - 1)
                for lo, hi in ((0, 64), (64, 0)):
                    ins = V.tensor_tensor(RB6[lo:lo + 64, m % 2, :].rearrange("p (b n) -> p b n", b=B),
                                          v[hi:hi + 64, :].rearrange("p (b n) -> p b n", b=B) if lo == 0 else
                                          v[0:64, :].rearrange("p (b n) -> p b n", b=B),
                                          sin6[(64 if lo == 0 else 0):(128 if lo == 0 else 64), :].unsqueeze(1).to_broadcast([64, B, SEQ]), ALU.mult)
                ins.then_inc(S("e_rb"), 1)

            def o6(i):
                t, g = i // 4, i % 4
                return (OT5[:, 4 * g:4 * g + 4, t * P:(t + 1) * P],
                        PS[:, 5 + i % 2, :].rearrange("p (c n) -> p c n", c=4), i + 1)

            core("e_", 16, PB5, lambda i: mask6.unsqueeze(1).to_broadcast([P, 4, P]), o6)
            for t in range(TT):
                dve.wait_ge(S("rows"), ROWS["e_"] + t + 1)
                V.tensor_tensor(XN[:, t, :], XN[:, t, :], PS[:, t, :], ALU.add).then_inc(S("hidden"), 1)
            dve.wait_ge(S("hidden"), 2 * TT)
            for t in range(TT):
                link.at(V.tensor_tensor(X[:, t, :], X[:, t, :], XN[:, t, :], ALU.add))
            rms_rows("fn")
            split_tokens("fn", XS1)
            gate("m1", 1e-9)
            experts("m1_", NF1, 0, W1S, SIL1, HS1)
            with dve.Fori(1, E8) as e:
                dve.wait_ge(S("moe_acc"), e * TT + E8 * TT)
                experts("m1_", NF1, e, W1S, SIL1, HS1)
            dve.wait_ge(S("moe_acc"), 2 * E8 * TT)
            V.memset(zero1, 0.0).then_inc(S("x_final"), 1)

        @block.tensor
        def _(pe):
            M = nc.tensor.matmul

            def M3(out, a, b, start, stop):
                M(out, a[0], b[0], start=start, stop=False)
                M(out, a[0], b[1], start=False, stop=False)
                return M(out, a[1], b[0], start=False, stop=stop)

            def norm(p):
                for t in range(TT):
                    pe.wait_ge(S("n_xn"), before[p] * TT + t + 1)
                    for k in range(KC):
                        ins = nc.tensor.transpose(PS[:, t, k * P:(k + 1) * P], XN[:, t, k * P:(k + 1) * P], ident)
                    ins.then_inc(S("n_xt"), 1)
                pe.wait_ge(S("n_xnT"), before[p] * TT + TT)

            def to_rows(p, lhs, rhs, nk, bank=0):
                for t in range(TT):
                    for k in range(nk):
                        ins = M(PS[:, bank + t, :], lhs[:, k, t * P:(t + 1) * P], rhs[:, k, :],
                                start=(k == 0), stop=(k == nk - 1))
                    ins.then_inc(S("rows"), 1)

            def gate(p, W):
                for t in range(TT):
                    for k in range(KC):
                        ins = M(PS[:, 3, t * E8:(t + 1) * E8], XNT[:, k, t * P:(t + 1) * P], W[:, k, :],
                                start=(k == 0), stop=(k == KC - 1))
                ins.then_inc(S("glog"), 1)

            def experts(p, nf, e, widths, XS, UP, DOWN, HS, first):
                if first:
                    pe.wait_ge(S("xs"), GATED[p[:-1]] + 1)

                def up(f):
                    m = widths[f]
                    pe.wait_ge(S("w_up"), plus(e * nf, MOE[p] + f + 1))
                    if f >= 2:
                        pe.wait_ge(S("moe_hT"), plus(e * nf, MOE[p] + f - 1))
                    for w in (0, 1):
                        for k in range(KC):
                            c = w * 512 + k * P
                            ins = M3(PS[0:m, 4 + f % 2 * 2 + w, :], [u[:, f % 2, c:c + m] for u in UP],
                                     [x[:, k, :] for x in XS], k == 0, k == KC - 1)
                    ins.then_inc(S("moe_h"), 1)

                def down(f):
                    m = widths[f]
                    pe.wait_ge(S("moe_hT"), plus(e * nf, MOE[p] + f + 1))
                    pe.wait_ge(S("w_down"), plus(e * nf, MOE[p] + f + 1))
                    if f == 0 and first:
                        pe.wait_ge(S("gsub"), GATED[p[:-1]] + 1)
                    if f == 0 and not first:
                        pe.wait_ge(S("moe_acc"), plus(e * TT, ACC[p]))
                    for t in range(TT):
                        ins = M3(PS[:, t, :], [h[0:m, f % 2, t * P:(t + 1) * P] for h in HS],
                                 [d[0:m, f % 2, :] for d in DOWN], f == 0, f == nf - 1)
                    ins.then_inc(S("moe_out"), 1)

                up(0)
                for f in range(nf):
                    if f + 1 < nf:
                        up(f + 1)
                    down(f)

            pe.wait_ge(S("ld_const"), 16)
            norm("xn")
            for name, W, ld, base in (("x_q", WQ, "ld_wq", 0), ("x_g", WG, "ld_wg", 4)):
                pe.wait_ge(S(ld), 16)
                for j in range(KC):
                    for k in range(KC):
                        ins = M(PS[:, base + j, :], W[:, k, j * P:(j + 1) * P], XNT[:, k, :],
                                start=(k == 0), stop=(k == KC - 1))
                    ins.then_inc(S(name), 1)
            pe.wait_ge(S("wk_split"), 1)
            pe.wait_ge(S("x_pre"), KC)

            def kv_sum(b1):
                pe.wait_ge(S("x_ctks"), b1)
                pe.wait_ge(S("k_summed"), b1 * (CT - 1))
                for j in range(KC):
                    for k in range(KC):
                        M(PS[:, 6, j * P:(j + 1) * P], CTK[:, k, j * P:(j + 1) * P], WV[:, k, j * P:(j + 1) * P],
                          start=(k == 0), stop=(k == KC - 1))
                for j in range(KC):
                    ins = M(PS[:, 7, j:j + 1], KACC[:, j * P:(j + 1) * P], ones[:, 0:1], start=True, stop=True)
                ins.then_inc(S("x_kv"), 1)

            def keys(b, first):
                def proj(t):
                    n = P if t < CT - 1 else LAST
                    s = t % 2 if t < CT - 1 else 2
                    pe.wait_ge(S("cols_split"), plus(b * CT, t + 1))
                    for k in range(KC):
                        ins = M3(PS[0:n, 4 + t % 2, :], [c[:, k * P:k * P + n] for c in CTS[s]],
                                 [w[:, k, :] for w in WKS], k == 0, k == KC - 1)
                    ins.then_inc(S("k_ps"), 1)

                def outer(t):
                    n = P if t < CT - 1 else LAST
                    s = t % 2 if t < CT - 1 else 2
                    pe.wait_ge(S("rows_split"), plus(b * CT, t + 1))
                    pe.wait_ge(S("k_split"), plus(b * CT, t + 1))
                    for c in range(KC):
                        ins = M3(PS[:, c, :], [x[0:n, c * P:(c + 1) * P] for x in CRS[s]],
                                 [k[0:n, s, :] for k in KBS], t == 0, t == CT - 1)
                    ins.then_inc(S("c_used"), 1)

                proj(0)
                if not first:
                    kv_sum(b)
                for t in range(CT):
                    if t + 1 < CT:
                        proj(t + 1)
                    outer(t)

            pe.wait_ge(S("ld_wv"), 16)
            keys(0, True)
            with pe.Fori(1, B) as b:
                keys(b, False)
            kv_sum(B)
            pe.wait_ge(S("x_kvs"), B)
            for j in range(KC):
                for b in range(B):
                    s = slice(b * SEQ, (b + 1) * SEQ)
                    M(PS[:, j, s], KV[:, b, j, :], QT[:, j, s], start=True, stop=True)
                    ins = M(PS[:, 4 + j, s], KS[:, b, j, :], QT[:, j, s], start=True, stop=True)
                ins.then_inc(S("x_num"), 1)
            pe.wait_ge(S("x_aT"), KC)
            pe.wait_ge(S("ld_wo"), 16)
            to_rows("x_", AT, WO, KC)

            norm("an")
            pe.wait_ge(S("ld_self"), 32)
            for t in range(TT):
                for lo, hi, bank in ((0, 512, 2 * t), (512, 768, 2 * t + 1)):
                    for k in range(KC):
                        ins = M(PS[:, bank, 0:hi - lo], XNT[:, k, t * P:(t + 1) * P], W2[:, k, lo:hi],
                                start=(k == 0), stop=(k == KC - 1))
                ins.then_inc(S("a_qkv"), 1)
            pe.wait_ge(S("a_qkvn"), 1)
            for t in range(TT):
                for c in range(4):
                    ins = nc.tensor.transpose(PS[:, t, c * P:(c + 1) * P], XR[:, t, c * P:(c + 1) * P], ident)
                ins.then_inc(S("a_qt"), 1)
            for t in range(TT):
                ins = nc.tensor.transpose(PS[:, 4, t * P:(t + 1) * P], XR[:, t, 512:640], ident)
            ins.then_inc(S("a_kt"), 1)
            pe.wait_ge(S("a_qts"), TT)
            pe.wait_ge(S("a_kts"), 1)
            for t in range(TT):
                for g in range(2):
                    r = slice(64 * g, 64 * g + 64)
                    for c in range(4):
                        ins = M(PS[:, 2 * t + g, c * P:(c + 1) * P], QT2[r, t, c, :], KT2[r, t, :],
                                start=True, stop=True)
                    ins.then_inc(S("a_s"), 1)
            pe.wait_ge(S("a_p"), 2)

            def trans(i):
                t, g = i // 2, i % 2
                if i >= 2:
                    pe.wait_ge(S("a_pts"), i - 1)
                for c in range(4):
                    ins = nc.tensor.transpose(PS[:, i % 2, c * P:(c + 1) * P], PF[:, t, 4 * g + c, :], ident)
                ins.then_inc(S("a_pt"), 1)

            trans(0)
            for i in range(2 * TT):
                t, g = i // 2, i % 2
                if i + 1 < 2 * TT:
                    trans(i + 1)
                pe.wait_ge(S("a_pts"), i + 1)
                if t >= 2 and g == 0:
                    pe.wait_ge(S("a_oT"), t - 1)
                M(PS[64 * g:64 * g + 64, 2 + t % 2, :], VAL[:, t, 64 * g:64 * g + 64], PT2[:, i % 2, :],
                  start=True, stop=True).then_inc(S("a_pv"), 1)
            pe.wait_ge(S("a_oT"), TT)
            to_rows("a_", OT2, WO2, 4, 4)

            norm("mn")
            pe.wait_ge(S("ld_gate"), 16)
            gate("m0", GATE0)
            experts("m0_", NF0, 0, [P] * NF0, XS0, UP0, DOWN0, HS0, True)
            with pe.Fori(1, E8) as e:
                experts("m0_", NF0, e, [P] * NF0, XS0, UP0, DOWN0, HS0, False)

            norm("cn")
            pe.wait_ge(S("moe_acc"), E8 * TT)
            pe.wait_ge(S("ld_cross"), 16 * 6)
            for j in range(KC):
                for k in range(KC):
                    ins = M(PS[:, j, :], WQ4[:, k, j * P:(j + 1) * P], XNT[:, k, :], start=(k == 0), stop=(k == KC - 1))
                ins.then_inc(S("c_q"), 1)
            SQQ = area(0, KC, C)
            for j in range(KC):
                pe.wait_ge(S("c_qe"), j + 1)
                ins = M(PS[:, 4, :], ones, SQQ[:, j, :], start=(j == 0), stop=(j == KC - 1))
            ins.then_inc(S("c_qr"), 1)
            pe.wait_ge(S("c_qstd"), 1)

            def cross(b, first):
                order = {"K": 0, "V": 0, "R": 0}
                at = []
                for c in range(4):
                    pe.wait_ge(S(f"ld_slot{c}"), plus(b * 16, slot_base("x", c) + 16))
                if not first:
                    pe.wait_ge(S("c_at"), b * 8)
                def scores(i):
                    j, half = i // 2, i % 2
                    r = slice(64 * half, 64 * half + 64)
                    if i or not first:
                        pe.wait_ge(S("c_max"), plus(b * 8, i))
                    for lo in (512, 1024, 1536, 0):
                        hi = min(lo + 512, CTX)
                        if lo == 0 and (i or not first):
                            pe.wait_ge(S("c_ei"), plus(b * 8, i))
                        ins = M(PS[:, lo // 512, 0:hi - lo], QB4[r, j, 128 * half:128 * half + 128], KT4[r, j, lo:hi],
                                start=True, stop=True)
                    ins.then_inc(S("c_s"), 1)

                for u, (kind, c, j) in enumerate(PROD):
                    bank = 4 + u % 4
                    if u == len(PROD) - 1:
                        pe.wait_ge(S("c_kn"), plus(b * 4, 4))
                        scores(0)
                    if u >= 4:
                        k0, n0 = at[u - 4]
                        sem, per = {"K": ("c_kt", 16), "V": ("c_vs", NV), "R": ("c_rs", 4)}[k0]
                        pe.wait_ge(S(sem), plus(b * per, n0 + 1))
                    at.append((kind, order[kind]))
                    order[kind] += 1
                    if kind == "K":
                        for W, lo, hi in (((WKI4, 0, IMG), (WK4, IMG, CN[0])) if c == 0 else ((WK4, 0, CN[c]),)):
                            for k in range(KC):
                                ins = M(PS[:, bank, lo:hi], W[:, k, j * P:(j + 1) * P], CC[c][:, k, lo:hi],
                                        start=(k == 0), stop=(k == KC - 1))
                        ins.then_inc(S("c_k"), 1)
                    if kind == "V":
                        lo, n = TILES[c]
                        W = WVI4 if lo < IMG else WV4
                        ch = max(x for x in range(4) if CO[x] <= lo)
                        for k in range(KC):
                            ins = M(PS[0:n, bank, :], CC[ch][:, k, lo - CO[ch]:lo - CO[ch] + n], W[:, k, :],
                                    start=(k == 0), stop=(k == KC - 1))
                        ins.then_inc(S("c_v"), 1)
                    if kind == "R":
                        pe.wait_ge(S("c_sq"), plus(b * 4, c + 1))
                        M(PS[:, bank, 0:CN[c]], ones, ACC4[:, CO[c]:CO[c] + CN[c]], start=True,
                          stop=True).then_inc(S("c_r"), 1)
                def turn(i, groups):
                    for g in groups:
                        if g == 0:
                            pe.wait_ge(S("c_pn"), plus(b * 8, i + 1))
                            if i:
                                pe.wait_ge(S("c_ptd"), plus(b * 16, 2 * i))
                        if g == 2 and i:
                            pe.wait_ge(S("c_pta"), plus(b * 16, 2 * i))
                        if g == 3:
                            pe.wait_ge(S("c_pta"), plus(b * 16, 2 * i + 1))
                        for n, t in enumerate(GROUPS[g]):
                            lo, w = TILES[t]
                            ins = nc.tensor.transpose(PS[0:w, 4 + g % 3, n * P:(n + 1) * P],
                                                      PB4[:, i % 2, lo:lo + w], ident)
                        ins.then_inc(S("c_t"), 1)

                def weigh(i):
                    pe.wait_ge(S("c_pta"), plus(b * 16, 2 * i + 2))
                    pe.wait_ge(S("c_ptd"), plus(b * 16, 2 * i + 2))
                    if i:
                        pe.wait_ge(S("c_at"), plus(b * 8, i))
                    h = 64 * (i % 2)
                    flat = [t for g in GROUPS for t in g]
                    for n, t in enumerate(flat):
                        w = TILES[t][1]
                        ins = M(PS[h:h + 64, 7, 0:P], values4(t)[0:w, 64 * i:64 * i + 64], PT4[i % 2][0:w, n, :],
                                start=(n == 0), stop=(n == CT))
                    ins.then_inc(S("c_pv"), 1)

                pe.wait_ge(S("c_vs"), plus(b * NV, NV))
                for i in range(8):
                    if i < 7:
                        scores(i + 1)
                    turn(i, (0, 1, 2))
                    if i:
                        weigh(i - 1)
                    turn(i, (3,))
                weigh(7)

            cross(0, True)
            with pe.Fori(1, B) as b:
                cross(b, False)
            pe.wait_ge(S("c_att"), KC)
            to_rows("c_", AT4, WO4, KC)

            norm("dn")

            def project(p):
                for m in range(20):
                    W, c, name = (WQ5, m, "q") if m < 16 else (WK5, m - 16, "k")
                    if c == 0:
                        pe.wait_ge(S("ld_" + name), 16 if p == "d_" else 32)
                    if m >= 4:
                        pe.wait_ge(S("proj_out"), 20 * SECOND[p] + m - 3)
                    for k in range(KC):
                        ins = M(PS[:, m % 4, :], W[:, k, c * P:(c + 1) * P], XNT[:, k, :],
                                start=(k == 0), stop=(k == KC - 1))
                    ins.then_inc(S("proj_" + name), 1)
                    if p == "e_" and m >= 1:
                        squares(m - 1)
                if p == "e_":
                    squares(19)
                pe.wait_ge(S("ld_v"), 16 if p == "d_" else 32)
                pe.wait_ge(S("proj_out"), 20 * SECOND[p] + 20)
                for t in range(TT):
                    if p == "d_" and t % 2 == 0:
                        pe.wait_ge(S("d_sq"), t // 2 + 1)
                        M(PS[:, 4 + t // 2, :], ones, ACC5[:, t // 2, :], start=True, stop=True).then_inc(S("sq_sum"), 1)
                    for k in range(KC):
                        ins = M(PS[:, t, :], XNT[:, k, t * P:(t + 1) * P], WV5[:, k, :],
                                start=(k == 0), stop=(k == KC - 1))
                    ins.then_inc(S("proj_v"), 1)

            def squares(m):
                pe.wait_ge(S("proj_out"), 20 + m + 1)
                if m >= 2:
                    pe.wait_ge(S("sq_root"), 2 + m - 1)
                M(PS[:, 4 + m % 2, :], ones, SQ6[:, m % 2, :], start=True, stop=True).then_inc(S("sq_sum"), 1)

            project("d_")

            def core(p, n, PB, PT, score, weigh, old):
                def turn(i):
                    pe.wait_ge(S("core_pn"), CORE[p] + i + 1)
                    if i >= 2:
                        pe.wait_ge(S("core_pts"), CORE[p] + i - 1)
                    for h in range(4):
                        ins = nc.tensor.transpose(PS[:, 3 + i % 2, h * P:(h + 1) * P],
                                                  PB[:, i % 4, h * P:(h + 1) * P], ident)
                    ins.then_inc(S("core_t"), 1)

                for i in range(n + 4):
                    if i < n:
                        if i >= 3:
                            pe.wait_ge(S("core_sb"), CORE[p] + i - 2)
                        for h in range(4):
                            q, k = score(i, h)
                            ins = M(PS[:, i % 3, h * P:(h + 1) * P], q, k, start=True, stop=True)
                        ins.then_inc(S("core_s"), 1)
                    if 3 <= i < n + 3:
                        turn(i - 3)
                    if i >= 4:
                        pe.wait_ge(S("core_pts"), CORE[p] + i - 3)
                        if old(i - 4):
                            pe.wait_ge(S("core_oT"), HEADS_OUT[p] + old(i - 4))
                        o, v = weigh(i - 4)
                        M(o, v, PT[:, (i - 4) % 2, :], start=True, stop=True).then_inc(S("core_pv"), 1)

            def score5(i, h):
                t, g = i // 8, i % 8
                r, s = slice(64 * (g % 2), 64 * (g % 2) + 64), slice(t * P, (t + 1) * P)
                return QT5[r, 4 * (g // 2) + h, s], KT5[r, g // 2, s]

            def weigh5(i):
                t, g = i // 8, i % 8
                return (PS[64 * (g % 2):64 * (g % 2) + 64, 5 + i // 2 % 2, :], V5[:, t, 64 * g:64 * g + 64])

            pe.wait_ge(S("values_out"), TT)
            pe.wait_ge(S("d_qkn"), 2)
            core("d_", 32, PB5, PT5, score5, weigh5, lambda i: max(0, i // 2 - 1) if i % 2 == 0 else 0)
            pe.wait_ge(S("ld_o"), 16)
            pe.wait_ge(S("core_oT"), 16)
            to_rows("d_", OT5, WO5, 16)

            def rms_turn(p):
                for t in range(TT):
                    pe.wait_ge(S("n_xn"), before[p] * TT + t + 1)
                    for k in range(KC):
                        ins = nc.tensor.transpose(PS[:, t, k * P:(k + 1) * P], HN6[:, t, k * P:(k + 1) * P], ident)
                    ins.then_inc(S("n_xt"), 1)
                pe.wait_ge(S("n_xnT"), before[p] * TT + TT)

            rms_turn("en")
            project("e_")

            def score6(i, h):
                t, g = i // 4, i % 4
                s = slice(t * P, (t + 1) * P)
                return QT5[:, 4 * g + h, s], KT5[:, g, s]

            def weigh6(i):
                t, g = i // 4, i % 4
                return PS[:, 5 + i % 2, :], V5[:, t, P * g:P * g + P]

            pe.wait_ge(S("values_out"), 2 * TT)
            pe.wait_ge(S("e_rope"), 20)
            core("e_", 16, PB5, PT6, score6, weigh6, lambda i: max(0, i - 1))
            pe.wait_ge(S("ld_o"), 32)
            pe.wait_ge(S("core_oT"), 32)
            to_rows("e_", OT5, WO5, 16)
            rms_turn("fn")
            pe.wait_ge(S("ld_gate"), 32)
            gate("m1", GATE1)
            experts("m1_", NF1, 0, W1S, XS1, UP1, DOWN1, HS1, True)
            with pe.Fori(1, E8) as e:
                experts("m1_", NF1, e, W1S, XS1, UP1, DOWN1, HS1, False)


def lay(w):
    n, m = w.shape
    return np.ascontiguousarray(w.reshape(n // 128, 128, m).transpose(1, 0, 2))


def constants():
    c = np.zeros((128, 964), np.float32)
    p = np.arange(128)
    c[:, 0:128] = np.eye(128)
    c[:, 128:256] = 1.0
    c[:, 256:384] = p[:, None] // 32 == p[None, :] // 32
    inv = (1.0 / np.float32(1000000.0) ** (np.arange(0, 64, 2, dtype=np.float32) / np.float32(64))).astype(np.float32)
    f = np.arange(64, dtype=np.float32)[:, None] * inv[None, :]
    cos, sin = np.cos(f), np.sin(f)
    c[:, 384:448] = np.tile(np.concatenate([cos, cos], 1), (2, 1))
    c[:, 448:512] = np.tile(np.concatenate([-sin, sin], 1), (2, 1))
    ok = (np.arange(64)[None, :] <= p[:, None] % 64).astype(np.float32)
    c[:, 512:576] = ok
    c[:, 576:640] = ok - 1
    c[:, 640:704] = (np.arange(8)[None, :] < np.arange(8)[:, None]).astype(np.float32).reshape(1, 64)
    inv = (1.0 / np.float32(1000000.0) ** (np.arange(0, 128, 2, dtype=np.float32) / np.float32(128))).astype(np.float32)
    f = (np.arange(64, dtype=np.float32)[:, None] * inv[None, :]).T
    c[:, 708:772] = np.tile(np.cos(f), (2, 1))
    c[:, 772:836] = np.concatenate([np.sin(f), -np.sin(f)], 0)
    d = p[None, :] - p[:, None]
    same = (p[None, :] // 64 == p[:, None] // 64) & (d <= 0)
    c[:, 836:964] = np.where(same, 0.0, NEG)
    return c


def alibi_bias():
    p = np.arange(128)
    d = (p[None, :] - p[:, None]).astype(np.float32)
    same = (p[None, :] // 64 == p[:, None] // 64) & (d <= 0)
    slopes = np.asarray([(2.0 ** (-8.0 / 32)) ** i for i in range(32)], np.float32)
    full = np.where(same[:, None, :], slopes[None, :, None] * d[:, None, :], np.float32(NEG)).astype(np.float32)
    return full.reshape(128, 8, 4, 128)


def arrange(i):
    f = {k: np.asarray(v) for k, v in i.items()}
    d = {}
    d["x"] = np.ascontiguousarray(f["x"].reshape(4, 128, 512).transpose(1, 0, 2))
    c = constants()
    c[:, 704:708] = f["L0_xattn_bg"].reshape(4, 128).T
    d["const"] = c
    d["xq"] = lay(f["L0_xattn_Wq"].T)
    d["xg"] = lay(f["L0_xattn_Wg"].T)
    d["xk"] = lay(f["L0_xattn_Wkv"][:512].T)
    d["xv"] = lay(f["L0_xattn_Wkv"][512:].T)
    d["xo"] = lay(f["L0_xattn_Wo"].T)
    ctx = f["ctx_2048"]
    pad = np.zeros((8, 13 * 128, 512), np.float32)
    pad[:, :1601] = ctx
    rows = pad.reshape(8, 13, 128, 512)
    cols = rows.reshape(8, 13, 128, 4, 128).transpose(0, 1, 4, 3, 2).reshape(8, 13, 128, 512)
    d["ctx0"] = np.ascontiguousarray(np.concatenate([cols, rows], -1))
    wq = f["L0_attn_Wq"].reshape(2, 4, 64, 512).transpose(1, 0, 2, 3).reshape(512, 512)
    d["aqkv"] = lay(np.concatenate([wq, f["L0_attn_Wk"], f["L0_attn_Wv"]], 0).T)
    d["ao"] = lay(f["L0_attn_Wo"].T.reshape(2, 4, 64, 512).transpose(1, 0, 2, 3).reshape(512, 512))
    d["m0gate"] = lay(f["L0_ffn_Wg"])
    w1 = f["L0_ffn_W1"].reshape(8, 4, 128, 11, 128).transpose(0, 3, 2, 1, 4).reshape(8, 11, 128, 512)
    w3 = f["L0_ffn_W3"].reshape(8, 4, 128, 11, 128).transpose(0, 3, 2, 1, 4).reshape(8, 11, 128, 512)
    w2 = f["L0_ffn_W2"].reshape(8, 11, 128, 512)
    d["m0w"] = np.ascontiguousarray(np.concatenate([w1, w3, w2], -1))
    order = np.concatenate([np.arange(257), 257 + np.arange(1280, 1344), 257 + np.arange(1280)])
    g = f["ctx_2048"][:, order].reshape(8, 1601, 4, 128).transpose(0, 3, 2, 1)
    co, cn = [0, 321, 833, 1345], [321, 512, 512, 256]
    d["ctx1"] = np.concatenate([g[..., a:a + n].reshape(8, 128, 4 * n) for a, n in zip(co, cn)], -1)
    d["iota"] = np.ascontiguousarray(np.broadcast_to((order[257:] - 257).astype(np.int16), (128, 1344)))
    d["len"] = np.ascontiguousarray(np.broadcast_to(f["_lenS2"].astype(np.int32), (128, 8)))
    for short, name in (("cq", "q"), ("ck", "k"), ("cki", "k_img"), ("cv", "v"), ("cvi", "v_img"), ("co", "o")):
        d[short] = lay(f["L1_xattn_w_" + name].T)
    d["bo"] = np.ascontiguousarray(np.broadcast_to(f["L1_xattn_b_o"], (128, 512)))
    v = np.zeros((128, 64), np.float32)
    for n, name in enumerate(("b_q", "b_k", "b_k_img", "b_v", "b_v_img", "g_q", "g_k", "g_k_img")):
        v[:, 4 * n:4 * n + 4] = f["L1_xattn_" + name].reshape(4, 128).T
    perm = lambda w: w.reshape(4, 2, 4, 64, *w.shape[1:]).swapaxes(1, 2).reshape(w.shape)
    v[:, 32:48] = perm(f["L1_attn_q_norm_w"]).reshape(16, 128).T
    v[:, 48:52] = f["L1_attn_k_norm_w"].reshape(4, 128).T
    v[:, 52:56] = f["L1_ffn_attn_norm_w"].reshape(4, 128).T
    v[:, 56] = f["L1_ffn_q_norm_w"]
    v[:, 57] = f["L1_ffn_k_norm_w"]
    v[:, 58:62] = f["L1_ffn_ffn_norm_w"].reshape(4, 128).T
    d["vec"] = v
    d["dq"] = lay(perm(f["L1_attn_wq"]).T)
    d["dk"] = lay(f["L1_attn_wk"].T)
    d["dv"] = lay(f["L1_attn_wv"].T)
    d["do"] = lay(perm(np.ascontiguousarray(f["L1_attn_wo"].T)))
    d["alibi"] = alibi_bias()
    for short, name in (("eq", "q_w"), ("ek", "k_w"), ("ev", "v_w"), ("eo", "o_w")):
        d[short] = lay(f["L1_ffn_" + name].T)
    d["m1gate"] = lay(f["L1_ffn_gate_w"].T)
    up = lambda w: np.pad(w, ((0, 0), (0, 32), (0, 0))).reshape(8, 3, 128, 4, 128).transpose(0, 1, 4, 3, 2).reshape(8, 3, 128, 512)
    down = np.pad(f["L1_ffn_wd"].transpose(0, 2, 1), ((0, 0), (0, 32), (0, 0))).reshape(8, 3, 128, 512)
    d["m1w"] = np.ascontiguousarray(np.concatenate([up(f["L1_ffn_wg"]), up(f["L1_ffn_wu"]), down], -1))
    return d


def kernel(**inputs):
    import concourse.bacc as _bacc
    from concourse import mybir as _mybir
    from concourse.bass_utils import run_bass_kernel_spmd as _run

    nc = _bacc.Bacc("TRN2", target_bir_lowering=False, num_devices=1)
    data = arrange(inputs)
    arrays, D = {}, {}
    for name, a in data.items():
        arrays[f"in_{name}"] = a
        D[name] = nc.dram_tensor(f"in_{name}", a.shape, _mybir.dt.from_np(a.dtype), kind="ExternalInput").ap()
    o = nc.dram_tensor("out_x", (128, 4, 512), _mybir.dt.float32, kind="ExternalOutput").ap()
    build(nc, D, o)
    r = _run(nc, [arrays], core_ids=[0])
    return r.results[0]["out_x"].transpose(1, 0, 2).reshape(8, 64, 512)
```

```python
from contextlib import ExitStack

import numpy as np
import concourse.bass as bass
from concourse import mybir

ALU = mybir.AluOpType
ACT = mybir.ActivationFunctionType
AX = mybir.AxisListType
F32 = mybir.dt.float32
F32R = mybir.dt.float32r
I32 = mybir.dt.int32

P = 128
B, SEQ, C = 8, 64, 512
TOK = B * SEQ
TT = TOK // P
KC = C // P
CTX = 1601
CT = 13
LAST = CTX - 12 * P
RS = 7
IMG = 257
TXT = CTX - IMG
E8 = 8
F0, F1 = 1408, 352
NF0, NF1 = F0 // P, 3
H0 = 8
NEG = -1.0e30


class Link:

    def __init__(self, eng, sem):
        self.eng, self.sem, self.n, self.base = eng, sem, 0, 0

    def __call__(self, ins):
        self.n += 1
        ins.then_inc(self.sem, 1)
        self.eng.wait_ge(self.sem, self.base + self.n)

    def at(self, ins):
        self.n += 1
        ins.then_inc(self.sem, 1)

    def sync(self):
        self.eng.wait_ge(self.sem, self.base + self.n)


def plus(a, b):
    return a + b if b else a


def build(nc, D, out):
    ctx = ExitStack()
    sems = {}

    def S(name):
        if name not in sems:
            sems[name] = ctx.enter_context(nc.semaphore(name))
        return sems[name]

    def sb(name, shape, dt=F32):
        return ctx.enter_context(nc.sbuf_tensor(name, shape, dt))

    with ctx:
        X = sb("X", [P, TT, C])
        XN = sb("XN", [P, TT, C])
        XNT = sb("XNT", [P, KC, TOK])
        CONST = sb("CONST", [P, D["const"].shape[1]])
        SM = sb("SM", [P, 512])
        VEC = sb("VEC", [P, 64])
        LEN = sb("LEN", [P, B], I32)
        with nc.sbuf_tensor("ARENA", [P, 45200], F32) as ARENA:
            pass
        PS = ctx.enter_context(nc.psum_tensor("PS", [P, 8, 512], F32))

        ident = CONST[:, 0:128]
        ones = CONST[:, 128:256]
        block32 = CONST[:, 256:384]
        cosT = CONST[:, 384:448]
        sinT = CONST[:, 448:512]
        causal01 = CONST[:, 512:576]
        causalm1 = CONST[:, 576:640]
        tri8 = CONST[:, 640:704]
        bg = CONST[:, 704:708]
        cos6, sin6 = CONST[:, 708:772], CONST[:, 772:836]
        mask6 = CONST[:, 836:964]
        PSF = PS[:, :, :].rearrange("p a b -> p (a b)")
        bq1, bk1, bki1, bv1, bvi1, gq1, gk1, gki1 = (VEC[:, 4 * n:4 * n + 4] for n in range(8))
        qw5, kw5 = VEC[:, 32:48], VEC[:, 48:52]
        hw6, qw6, kw6, fw6 = VEC[:, 52:56], VEC[:, 56:57], VEC[:, 57:58], VEC[:, 58:62]

        def area(at, *shape):
            n = int(np.prod(shape))
            v = ARENA[:, at:at + n]
            if len(shape) == 2:
                v = v.rearrange("p (a b) -> p a b", a=shape[0])
            if len(shape) == 3:
                v = v.rearrange("p (a b c) -> p a b c", a=shape[0], b=shape[1])
            return v

        def leading(at, *shape):
            with nc.sbuf_tensor(f"before{len(split)}", [P, at], F32):
                with nc.sbuf_tensor(f"split{len(split)}", [P, *shape], F32R) as v:
                    split.append(at)
            return v[tuple(slice(None) for _ in range(1 + len(shape)))]

        def parts(hi, lo, *shape):
            return [leading(at, *shape) for at in (hi, lo)]

        split = []

        def rest(eng, dst, src, hi):
            return eng.tensor_tensor(dst, src, hi.bitcast(F32), ALU.subtract)

        small = [0]

        def tiny(*shape):
            n = int(np.prod(shape))
            v = SM[:, small[0]:small[0] + n]
            small[0] += n
            if len(shape) == 2:
                v = v.rearrange("p (a b) -> p a b", a=shape[0])
            if len(shape) == 3:
                v = v.rearrange("p (a b c) -> p a b c", a=shape[0], b=shape[1])
            return v

        eps5, eps6 = tiny(1), tiny(1)
        stat = tiny(TT, 6)
        mv = tiny(TT, 2)
        std = tiny(TT)
        rstd = tiny(TT)
        nbg = tiny(KC)
        ksum = tiny(KC)
        red = tiny(48)
        red2 = tiny(48)
        red3 = tiny(48)
        gp = tiny(TT, E8)
        gw = tiny(TT, E8)
        gs = tiny(TT)
        lens = tiny(B)
        lenb = tiny(1)
        gqs, bvv = tiny(KC), tiny(KC)
        mx, nmx, lsum, rls = tiny(2, 2), tiny(2, 2), tiny(2, 2), tiny(2, 2)
        qws = tiny(16)
        nm5, l5, rl5 = tiny(4, 4), tiny(4, 4), tiny(4, 4)
        ms = tiny(TT)

        WK = area(0, KC, C)
        WV = area(2048, KC, C)
        WQ = area(4096, KC, C)
        WG = area(6144, KC, C)
        WO = area(8192, KC, C)
        RING = area(10240, RS, 1024)
        WKS = parts(19456, 21504, KC, C)
        CTS = [parts(at, at + 1024, 512) for at in (17408, 6144, 4096)]
        CRS = [parts(at + 512, at + 1536, 512) for at in (17408, 6144, 4096)]
        KM = area(23552, 3, 512)
        KBS = parts(25088, 512, 3, 512)
        KB = area(26624, 4, 512)
        KACC = area(28672, 512)
        CTK = area(29184, KC, C)
        QT = area(31232, KC, TOK)
        G1 = area(33280, KC, TOK)
        KV = area(35328, B, KC, P)
        KS = area(39424, B, KC, P)
        TMP = area(43520, 2, 512)
        AT = area(10240, KC, TOK)
        DEN = area(12288, KC, TOK)
        W2 = area(16896, KC, 768)
        WO2 = area(19968, KC, C)
        QKV = area(22016, TT, 12 * 64)
        XR = area(25088, TT, 12 * 64)
        TA = area(28160, TT, 12 * 64)
        TB = area(31232, TT, 12 * 64)
        PF = area(34304, TT, H0, P)
        TANH = area(22016, TT, H0, 64)
        MASKED = area(28160, TT * H0, 64)
        VAL = XR[:, :, 640:768]
        QT2 = area(38400, TT, 4, P)
        KT2 = area(40448, TT, P)
        PT2 = area(40960, 2, 512)
        OT2 = area(41984, 4, TOK)
        WQ4, WK4, WKI4, WV4, WVI4 = (area(25152 + 2048 * n, KC, C) for n in range(5))
        WO4 = area(41536, KC, C)
        WKS4 = parts(25152, 27200, KC, C)
        WVS4 = parts(35392, 31296, KC, C)
        CO = [0, 321, 833, 1345]
        CN = [321, 512, 512, 256]
        CA = [37440, 38728, 40776, 42824]
        CC = [area(CA[c], KC, CN[c]) for c in range(4)]
        SUB = [(0, IMG, 64)] + [(1 + n // 2, 321 + 256 * n, 256) for n in range(5)]
        CHI = [leading(at, KC, SUB[n][2]) for n, at in enumerate((23704, 22680, 14680, 13072, 22680, 14680))]
        CLO = [leading(CA[c], KC, CN[c]) for c in range(4)]

        def rest_of(n):
            c, lo, w = SUB[n]
            return CLO[c][:, :, lo - CO[c]:lo - CO[c] + w]

        def part_of(n):
            c, lo, w = SUB[n]
            return CC[c][:, :, lo - CO[c]:lo - CO[c] + w]

        BIAS = area(43848, TXT)
        KT4 = area(0, KC, CTX + 3)
        V4 = area(6416, CT, C)
        PB4 = area(13072, 2, CTX + 3)
        PT4 = [area(16280, CT + 1, P), area(22680, CT + 1, P)]
        ACC4 = area(16280, CTX + 3)
        SQ4 = area(17884, 512)
        QT4 = area(19608, KC, TOK)
        QB4 = area(21656, KC, 4 * SEQ)
        BO4 = area(18912, C)
        IOTA = area(24472, TXT // 2).bitcast(mybir.dt.int16)
        RS4 = XNT[:, :, :].rearrange("p k n -> p (k n)")
        AT4 = XN[:, :, :]
        TILES = [(0, P), (P, P), (IMG, 64)] + [(321 + P * n, P) for n in range(10)] + [(2 * P, 1)]
        GROUPS = [[0, 1, 13, 2], [3, 4, 5, 6], [7, 8, 9, 10], [11, 12]]
        PROD = []
        for w in ("I K0 V2 K1 V3 V4 R0 K2 V5 V6 R1 K3 V7 V8 K4 V9 V10 R2 K5 V11 V12 R3 V0 V1 V13").split():
            if w[0] in "IK":
                PROD += [(w[0], int(w[1:] or 0), j) for j in range(KC)]
            else:
                PROD.append((w[0], int(w[1:]), 0))
        KEYS = [x for x in PROD if x[0] in "IK"]
        NK = len(KEYS)
        NV = CT + 1
        VLAST = area(18400, C)

        def values4(t):
            return VLAST if t == CT else V4[:, t, :]
        WQ5 = area(27200, KC, 2048)
        WK5 = area(37440, KC, C)
        WV5 = area(39488, KC, C)
        WO5 = area(12288, 16, C)
        QT5 = area(0, 16, TOK)
        KT5 = area(8192, 4, TOK)
        V5 = area(10240, TT, C)
        OT5 = QT5
        ALIBI = area(20480, 8, 4, P)
        ACC5 = area(41536, 2, 512)
        SQ5 = area(42560, 512)
        RS5 = area(43072, 2, 512)
        PB5 = XNT[:, :, :]
        PT5 = XN[:, 0:2, :]
        HN6 = area(20480, TT, C)
        PT6 = area(41536, 2, 512)
        SQ6 = area(22528, 2, 512)
        RS6 = area(23552, 2, 512)
        RA6 = area(24576, 2, 512)
        RB6 = area(25600, 2, 512)
        MW1 = area(27200, NF1, 1536)
        GATE1 = area(31808, KC, E8)
        W1S = [P, P, F1 - 2 * P]
        SIL1 = area(20480, 2, 512)
        XS1 = parts(12288, 14336, KC, TOK)
        UP1 = parts(5120, 7168, 2, 1024)
        DOWN1 = parts(9216, 10240, 2, 512)
        HS1 = parts(16384, 17408, 2, 512)
        MW0 = area(0, NF0, 1536)
        GATE0 = area(44032, KC, E8)
        SIL0 = area(22016, 2, 512)
        XS0 = parts(16896, 18944, KC, TOK)
        UP0 = parts(37440, 39488, 2, 1024)
        DOWN0 = parts(41536, 42560, 2, 512)
        HS0 = parts(20992, 23040, 2, 512)

        STEPS = "A0 A1 B0 A2 B1 C0 A3 B2 C1 B3 C2 C3".split()
        STEP = {x: n + 1 for n, x in enumerate(x for x in STEPS if x[0] in "AB")}

        NORMS = ["xn", "an", "mn", "cn", "dn", "en", "fn"]
        before = {p: n for n, p in enumerate(NORMS)}
        def slot_base(stage, s):
            n = "cmxn".index(stage)
            context = sum(16 * B for t in range(CT) if t % RS == s)
            return (context if n else 0) + max(n - 1, 0) * 16 * B

        MOE = {"m0_": 0, "m1_": E8 * NF0}
        ACC = {"m0_": 0, "m1_": E8 * TT}
        GATED = {"m0": 0, "m1": 1}
        XS_OF = {"mn": 0, "fn": 1}
        ROOTS = {"xn": 0, "an": TT, "mn": 2 * TT, "cn": 3 * TT, "dn": 4 * TT, "en": 5 * TT, "en2": 6 * TT, "fn": 6 * TT + 1}
        SECOND = {"d_": 0, "e_": 1}
        ROWS = {p: TT * n for n, p in enumerate(("x_", "a_", "c_", "d_", "e_"))}
        CORE = {"d_": 0, "e_": 32}
        HEADS_OUT = {"d_": 0, "e_": 16}

        block = ctx.enter_context(nc.Block())

        @block.sync
        def _(sp):
            def load(dst, name, sem):
                sp.dma_start(dst, D[name]).then_inc(S(sem), 16)

            load(X[:, :, :], "x", "ld_x")
            load(CONST[:, :], "const", "ld_const")
            load(WQ, "xq", "ld_wq")
            load(WG, "xg", "ld_wg")
            load(WK, "xk", "ld_wk")

            def tiles(b, first):
                for t in range(CT):
                    if t == RS and first:
                        load(WV, "xv", "ld_wv")
                        load(WO, "xo", "ld_wo")
                    if t >= RS:
                        sp.wait_ge(S("rows_split"), plus(b * CT, t - RS + 1))
                    elif not first:
                        old = t + RS if t + RS < CT else t
                        sp.wait_ge(S("rows_split"), b * CT + (old + 1 - CT))
                    sp.dma_start(RING[:, t % RS, :], D["ctx0"][b, t]).then_inc(S(f"ld_slot{t % RS}"), 16)

            tiles(0, True)
            with sp.Fori(1, B) as b:
                tiles(b, False)
            sp.wait_ge(S("c_used"), B * CT)
            load(W2, "aqkv", "ld_self")
            load(WO2, "ao", "ld_self")
            sp.wait_ge(S("x_added"), ROWS["x_"] + TT)
            sp.dma_start(GATE0, D["m0gate"]).then_inc(S("ld_gate"), 16)

            load(VEC[:, :], "vec", "ld_vec")
            load(LEN[:, :], "len", "ld_vec")

            def experts0(e, first):
                for f in range(NF0):
                    if not first:
                        sp.wait_ge(S("w_down"), e * NF0 + (f + 1 - NF0))
                    sp.dma_start(MW0[:, f, :], D["m0w"][e, f]).then_inc(S(f"ld_slot{f}"), 16)

            experts0(0, True)
            with sp.Fori(1, E8) as e:
                experts0(e, False)
            for n, name in enumerate(("cq", "ck", "cki", "cv", "cvi")):
                sp.dma_start(area(25152 + 2048 * n, KC, C), D[name]).then_inc(S("ld_cross"), 16)

            def context1(b, first):
                for c in range(4):
                    if not first:
                        sp.wait_ge(S("c_v"), b * NV)
                    sp.dma_start(CC[c], D["ctx1"][b, :, 4 * CO[c]:4 * (CO[c] + CN[c])]
                                 .rearrange("p (k n) -> p k n", k=KC)).then_inc(S(f"ld_slot{c}"), 16)

            sp.wait_ge(S("moe_acc"), E8 * TT)
            sp.dma_start(IOTA, D["iota"]).then_inc(S("ld_bo"), 16)
            load(BO4, "bo", "ld_bo")
            context1(0, True)
            with sp.Fori(1, B) as b:
                context1(b, False)
            sp.wait_ge(S("c_v"), B * NV)
            load(WO4, "co", "ld_wo")
            load(WQ5, "dq", "ld_q")
            load(WK5, "dk", "ld_k")
            load(WV5, "dv", "ld_v")
            sp.wait_ge(S("x_added"), ROWS["c_"] + TT)
            load(WO5, "do", "ld_o")
            load(ALIBI, "alibi", "ld_alibi")
            sp.wait_ge(S("proj_q"), 16)
            load(WQ5, "eq", "ld_q")
            sp.wait_ge(S("proj_k"), 4)
            load(WK5, "ek", "ld_k")
            sp.wait_ge(S("proj_v"), TT)
            load(WV5, "ev", "ld_v")
            sp.wait_ge(S("x_added"), ROWS["d_"] + TT)
            load(WO5, "eo", "ld_o")
            sp.wait_ge(S("proj_v"), 2 * TT)
            load(GATE1, "m1gate", "ld_gate")

            def experts1(e, first):
                for f in range(NF1):
                    if not first:
                        sp.wait_ge(S("w_down"), e * NF1 + (MOE["m1_"] + f + 1 - NF1))
                    sp.dma_start(MW1[:, f, :], D["m1w"][e, f]).then_inc(S(f"ld_slot{f}"), 16)

            experts1(0, True)
            with sp.Fori(1, E8) as e:
                experts1(e, False)
            for t in range(TT):
                sp.wait_ge(S("moe_acc"), (2 * E8 - 1) * TT + t + 1)
                sp.dma_start(out[:, t, :], X[:, t, :]).then_inc(S("stored"), 16)
            sp.wait_ge(S("stored"), 16 * TT)

        @block.gpsimd
        def _(pool):
            chain = Link(pool, S("pool_chain"))

            def ksum_tiles(b, first):
                kb = lambda t, n: KB[0:n, t % 3 if t < CT - 1 else 3, :]

                def cols(t):
                    s = t % 2 if t < CT - 1 else 2
                    pool.wait_ge(S("cols_hi"), plus(b * CT, t + 1))
                    rest(pool, CTS[s][1], RING[:, t % RS, 0:512], CTS[s][0]).then_inc(S("cols_split"), 1)

                def rows(t):
                    s = t % 2 if t < CT - 1 else 2
                    pool.wait_ge(S("rows_hi"), plus(b * CT, t + 1))
                    rest(pool, CRS[s][1], RING[:, t % RS, 512:1024], CRS[s][0]).then_inc(S("rows_split"), 1)

                cols(0)
                rows(0)
                cols(1)
                for t in range(CT):
                    n = P if t < CT - 1 else LAST
                    if t + 2 < CT:
                        cols(t + 2)
                    if t == 0:
                        rows(1)
                        continue
                    pool.wait_ge(S("k_ready"), plus(b * CT, t + 1))
                    if t == 1:
                        if not first:
                            pool.wait_ge(S("x_kv"), b)
                        pool.tensor_tensor(KACC, kb(0, n), kb(1, n), ALU.add).then_inc(S("k_summed"), 1)
                    else:
                        pool.wait_ge(S("k_summed"), plus(b * (CT - 1), t - 1))
                        pool.tensor_tensor(KACC[0:n, :], KACC[0:n, :], kb(t, n), ALU.add).then_inc(S("k_summed"), 1)
                    if t + 1 < CT:
                        rows(t + 1)

            def rests(p, nf, e, MW, UP, DOWN):
                def up(f):
                    pool.wait_ge(S("w_up_hi"), plus(e * nf, MOE[p] + f + 1))
                    rest(pool, UP[1][:, f % 2, :], MW[:, f, 0:1024], UP[0][:, f % 2, :]).then_inc(S("w_up"), 1)

                def down(f):
                    pool.wait_ge(S("w_down_hi"), plus(e * nf, MOE[p] + f + 1))
                    rest(pool, DOWN[1][:, f % 2, :], MW[:, f, 1024:1536],
                         DOWN[0][:, f % 2, :]).then_inc(S("w_down"), 1)

                up(0)
                down(0)
                up(1)
                for f in range(nf):
                    if f + 2 < nf:
                        up(f + 2)
                    if f + 1 < nf:
                        down(f + 1)

            pool.wait_ge(S("wk_hi"), 1)
            rest(pool, WKS[1], WK, WKS[0]).then_inc(S("wk_split"), 1)
            ksum_tiles(0, True)
            with pool.Fori(1, B) as b:
                ksum_tiles(b, False)
            pool.wait_ge(S("x_added"), ROWS["x_"] + TT)
            pool.memset(PF, 0.0).then_inc(S("a_pf0"), 1)
            rests("m0_", NF0, 0, MW0, UP0, DOWN0)
            with pool.Fori(1, E8) as e:
                rests("m0_", NF0, e, MW0, UP0, DOWN0)
            pool.wait_ge(S("moe_acc"), E8 * TT)
            pool.memset(QB4, 0.0).then_inc(S("c_qb0"), 1)

            def squares(b):
                def rest_text(n):
                    pool.wait_ge(S("cols_hi"), plus(b * 6, B * CT + n + 1))
                    rest(pool, rest_of(n), part_of(n), CHI[n]).then_inc(S("cols_split"), 1)

                for n in range(4):
                    rest_text(n)
                for m in range(7):
                    lo, w = SUB[m - 1][1:] if m else (0, IMG)
                    if m in (4, 5):
                        rest_text(m)
                    for j in range(KC):
                        v = KT4[:, j, lo:lo + w]
                        pool.wait_ge(S("c_kt"), plus(b * NK, 4 * m + j + 1))
                        dst = ACC4[:, lo:lo + w] if j == 0 else SQ4[:, 0:w]
                        chain(pool.tensor_tensor(dst, v, v, ALU.mult))
                        if j:
                            ins = pool.tensor_tensor(ACC4[:, lo:lo + w], ACC4[:, lo:lo + w], SQ4[:, 0:w], ALU.add)
                            if j == KC - 1 and m in (1, 3, 5, 6):
                                ins.then_inc(S("c_sq"), 1)
                            else:
                                chain(ins)

            pool.wait_ge(S("wk_hi"), 2)
            rest(pool, WKS4[1], WK4, WKS4[0]).then_inc(S("wk_split"), 1)
            pool.wait_ge(S("wk_hi"), 3)
            rest(pool, WVS4[1], WV4, WVS4[0]).then_inc(S("wk_split"), 1)
            squares(0)
            n0 = chain.n
            with pool.Fori(1, B) as b:
                chain.n, chain.base = 0, b * n0
                squares(b)
                assert chain.n == n0
            chain.n, chain.base = n0 * B, 0

            for m in range(20):
                src = QT5[:, m, :] if m < 16 else KT5[:, m - 16, :]
                acc = ACC5[:, m // 16, :]
                pool.wait_ge(S("proj_out"), m + 1)
                if m % 16 == 0:
                    chain(pool.tensor_tensor(acc, src, src, ALU.mult))
                else:
                    chain(pool.tensor_tensor(SQ5, src, src, ALU.mult))
                    ins = pool.tensor_tensor(acc, acc, SQ5, ALU.add)
                    if m in (15, 19):
                        ins.then_inc(S("d_sq"), 1)
                    else:
                        chain(ins)

            def core(p, n, PB):
                for i in range(n):
                    pool.wait_ge(S("core_rl"), CORE[p] + i + 1)
                    v = PB[:, i % 4, :].rearrange("p (h n) -> p h n", h=4)
                    pool.tensor_tensor(v, v, rl5[:, i % 4, :].unsqueeze(2).to_broadcast([P, 4, P]),
                                       ALU.mult).then_inc(S("core_pn"), 1)

            core("d_", 32, PB5)
            for m in range(20):
                v = (QT5[:, m, :] if m < 16 else KT5[:, m - 16, :]).rearrange("p (b n) -> p b n", b=B)
                ra = RA6[:, m % 2, :].rearrange("p (b n) -> p b n", b=B)
                rb = RB6[:, m % 2, :].rearrange("p (b n) -> p b n", b=B)
                pool.wait_ge(S("e_n"), m + 1)
                chain(pool.tensor_tensor(ra, v, cos6.unsqueeze(1).to_broadcast([P, B, SEQ]), ALU.mult))
                pool.wait_ge(S("e_rb"), m + 1)
                pool.tensor_tensor(v, ra, rb, ALU.add).then_inc(S("e_rope"), 1)
            core("e_", 16, PB5)
            rests("m1_", NF1, 0, MW1, UP1, DOWN1)
            with pool.Fori(1, E8) as e:
                rests("m1_", NF1, e, MW1, UP1, DOWN1)

        @block.scalar
        def _(act):
            A = nc.scalar.activation
            chain = Link(act, S("act_chain"))

            def roots(p):
                for t in range(TT):
                    act.wait_ge(S("n_var"), before[p] * TT + t + 1)
                    A(std[:, t:t + 1], mv[:, t, 1:2], ACT.Sqrt, bias=eps5).then_inc(S("n_std"), 1)

            def norm(p):
                roots(p)
                for t in range(TT):
                    act.wait_ge(S("n_xt"), before[p] * TT + t + 1)
                    A(XNT[:, :, t * P:(t + 1) * P], PS[:, t, :].rearrange("p (k n) -> p k n", k=KC),
                      ACT.Copy).then_inc(S("n_xnT"), 1)

            def gate(p):
                act.wait_ge(S("gsub"), GATED[p] + 1)
                A(gw, gw, ACT.Exp).then_inc(S("gexp"), 1)

            def experts(p, nf, e, widths, SIL, MW, UP, DOWN, first, ld):
                n0 = MOE[p]

                def up(f):
                    act.wait_ge(S(f"ld_slot{f}"), plus(e * 16, slot_base(ld, f) + 16))
                    if f >= 2:
                        act.wait_ge(S("moe_h"), plus(e * nf, n0 + f - 1))
                    elif not first:
                        act.wait_ge(S("moe_h"), plus(e * nf, n0))
                    A(UP[0][:, f % 2, :], MW[:, f, 0:1024], ACT.Copy).then_inc(S("w_up_hi"), 1)

                def down(f):
                    if f >= 2:
                        act.wait_ge(S("moe_out"), plus(e * nf, n0 + f - 1))
                    elif not first:
                        act.wait_ge(S("moe_out"), plus(e * nf, n0))
                    A(DOWN[0][:, f % 2, :], MW[:, f, 1024:1536], ACT.Copy).then_inc(S("w_down_hi"), 1)

                up(0)
                down(0)
                up(1)
                if first:
                    gate(p[:-1])
                for f in range(nf):
                    m = widths[f]
                    act.wait_ge(S("moe_h"), plus(e * nf, n0 + f + 1))
                    if f >= 2:
                        act.wait_ge(S("moe_hT"), plus(e * nf, n0 + f - 1))
                    elif not first:
                        act.wait_ge(S("moe_hT"), plus(e * nf, n0))
                    A(SIL[0:m, f % 2, :], PS[0:m, 4 + f % 2 * 2, :], ACT.Silu).then_inc(S("moe_silu"), 1)
                    if f + 2 < nf:
                        up(f + 2)
                    if f + 1 < nf:
                        down(f + 1)

            act.wait_ge(S("eps"), 2)
            norm("xn")
            act.wait_ge(S("ld_wk"), 16)
            A(WKS[0], WK, ACT.Copy).then_inc(S("wk_hi"), 1)
            for j in range(KC):
                act.wait_ge(S("x_qmin"), j + 1)
                A(TMP[:, j % 2, :], TMP[:, j % 2, :], ACT.Exp).then_inc(S("x_qexp"), 1)

            def cols(b, t):
                s = t % 2 if t < CT - 1 else 2
                act.wait_ge(S(f"ld_slot{t % RS}"), plus(b * (32 if t % RS < CT - RS else 16), 16 * (t // RS) + 16))
                if t >= 2:
                    act.wait_ge(S("k_ps"), plus(b * CT, t - 1))
                A(CTS[s][0], RING[:, t % RS, 0:512], ACT.Copy).then_inc(S("cols_hi"), 1)

            def rows(b, t, first):
                s = t % 2 if t < CT - 1 else 2
                if t >= 2 or not first:
                    act.wait_ge(S("c_used"), plus(b * CT, t - 1 if t else -2))
                A(CRS[s][0], RING[:, t % RS, 512:1024], ACT.Copy).then_inc(S("rows_hi"), 1)

            cols(0, 0)
            rows(0, 0, True)
            act.wait_ge(S("x_nbg"), 1)
            for j in range(KC):
                act.wait_ge(S("x_g"), j + 1)
                A(G1[:, j, :], PS[:, 4 + j, :], ACT.Exp, bias=nbg[:, j:j + 1], scale=-1.0).then_inc(S("x_gexp"), 1)

            def ctk_out(b1):
                act.wait_ge(S("c_used"), b1 * CT)
                for c in range(KC):
                    ins = A(CTK[:, c, :], PS[:, c, :], ACT.Copy)
                ins.then_inc(S("x_ctks"), 1)

            def keys(b, first):
                if not first:
                    cols(b, 0)
                    rows(b, 0, False)
                cols(b, 1)
                if not first:
                    ctk_out(b)
                for t in range(CT):
                    n = P if t < CT - 1 else LAST
                    s = t % 2 if t < CT - 1 else 2
                    act.wait_ge(S("k_min"), plus(b * CT, t + 1))
                    A(KM[0:n, s, :], KM[0:n, s, :], ACT.Exp).then_inc(S("k_exp"), 1)
                    if t + 2 < CT:
                        cols(b, t + 2)
                    if t + 1 < CT:
                        rows(b, t + 1, first)

            keys(0, True)
            with act.Fori(1, B) as b:
                keys(b, False)
            ctk_out(B)

            norm("an")
            for step in "E0 E1 A0 E2 A1 B0 E3 A2 B1 A3 B2 B3".split():
                t = int(step[1])
                if step[0] == "E":
                    act.wait_ge(S("a_qkv"), t + 1)
                    A(QKV[:, t, 0:512], PS[:, 2 * t, :], ACT.Copy)
                    A(QKV[:, t, 512:768], PS[:, 2 * t + 1, 0:256], ACT.Copy).then_inc(S("a_qkvs"), 1)
                    continue
                act.wait_ge(S("a_stat"), STEP[step])
                if step[0] == "A":
                    A(TB[:, t, :], TA[:, t, :], ACT.Square).then_inc(S("a_func"), 1)
                else:
                    v = red2[:, 12 * t:12 * t + 12]
                    A(v, v, ACT.Sqrt, bias=eps6, scale=1.0 / 64).then_inc(S("a_func"), 1)
            for t in range(TT):
                act.wait_ge(S("a_qt"), t + 1)
                A(QT2[:, t, :, :], PS[:, t, :].rearrange("p (c n) -> p c n", c=4), ACT.Copy).then_inc(S("a_qts"), 1)
            act.wait_ge(S("a_kt"), 1)
            A(KT2, PS[:, 4, :].rearrange("p (c n) -> p c n", c=4), ACT.Copy).then_inc(S("a_kts"), 1)
            TH = TANH
            for i in range(2 * TT):
                act.wait_ge(S("a_s"), i + 1)
                t, g = i // 2, i % 2
                v = PS[:, i, :].rearrange("p (c n) -> p c n", c=4)
                for h in (0, 1):
                    r = slice(64 * h, 64 * h + 64)
                    ins = A(TH[r, t, 4 * g:4 * g + 4, :], v[r, :, 64 * h:64 * h + 64], ACT.Tanh,
                            scale=256.0 / 8.0 / 30.0)
                ins.then_inc(S("a_tanh"), 1)
            for t in range(TT):
                v = MASKED[:, 8 * t:8 * t + 8, :]
                act.wait_ge(S("a_stat"), 2 * TT + t + 1)
                A(v, v, ACT.Exp, scale=30.0).then_inc(S("a_func"), 1)
            for i in range(2 * TT):
                act.wait_ge(S("a_pt"), i + 1)
                A(PT2[:, i % 2, :], PS[:, i % 2, :], ACT.Copy).then_inc(S("a_pts"), 1)

            norm("mn")
            experts("m0_", NF0, 0, [P] * NF0, SIL0, MW0, UP0, DOWN0, True, "m")
            with act.Fori(1, E8) as e:
                experts("m0_", NF0, e, [P] * NF0, SIL0, MW0, UP0, DOWN0, False, "m")

            norm("cn")
            act.wait_ge(S("ld_vec"), 32)
            SQQ = area(0, KC, C)
            for j in range(KC):
                act.wait_ge(S("c_q"), j + 1)
                A(QT4[:, j, :], PS[:, j, :], ACT.Identity, bias=bq1[:, j:j + 1])
                A(SQQ[:, j, :], PS[:, j, :], ACT.Square, bias=bq1[:, j:j + 1]).then_inc(S("c_qe"), 1)
            A(WKS4[0], WK4, ACT.Copy).then_inc(S("wk_hi"), 1)
            A(WVS4[0], WV4, ACT.Copy).then_inc(S("wk_hi"), 1)
            act.wait_ge(S("c_qr"), 1)
            A(RS4[:, 0:512], PS[:, 4, :], ACT.Sqrt, bias=eps6, scale=1.0 / C).then_inc(S("c_qstd"), 1)

            def cross(b, first):
                def leading_text(n):
                    c = SUB[n][0]
                    act.wait_ge(S(f"ld_slot{c}"), plus(b * 16, slot_base("x", c) + 16))
                    A(CHI[n], part_of(n), ACT.Copy).then_inc(S("cols_hi"), 1)

                if not first:
                    act.wait_ge(S("c_pv"), b * 8)
                for n in range(4):
                    leading_text(n)
                nk = 0
                for u, (kind, c, j) in enumerate(PROD):
                    bank = 4 + u % 4
                    if kind in "IK":
                        act.wait_ge(S("c_k"), plus(b * NK, nk + 1))
                        nk += 1
                        lo, w = (0, IMG) if kind == "I" else SUB[c][1:]
                        bias = bki1 if kind == "I" else bk1
                        A(KT4[:, j, lo:lo + w], PS[:, bank, 0:w], ACT.Identity, bias=bias[:, j:j + 1]).then_inc(S("c_kt"), 1)
                        if kind == "K" and c in (2, 3) and j == KC - 1:
                            leading_text(c + 2)
                    if kind == "R":
                        act.wait_ge(S("c_r"), plus(b * 4, c + 1))
                        if c == 0:
                            act.wait_ge(S("c_vs"), plus(b * NV, 1))
                        A(RS4[:, CO[c]:CO[c] + CN[c]], PS[:, bank, 0:CN[c]], ACT.Sqrt, bias=eps6,
                          scale=1.0 / C).then_inc(S("c_rs"), 1)
                for i in range(8):
                    pb = PB4[:, i % 2, :]
                    act.wait_ge(S("c_max"), plus(b * 8, i + 1))
                    A(pb[:, 0:IMG], PSF[:, 0:IMG], ACT.Exp, bias=nmx[:, i % 2, 0:1],
                      accum_out=lsum[:, i % 2, 0:1]).then_inc(S("c_ei"), 1)
                    A(pb[:, IMG:CTX], pb[:, IMG:CTX], ACT.Exp, bias=nmx[:, i % 2, 1:2],
                      accum_out=lsum[:, i % 2, 1:2]).then_inc(S("c_et"), 1)
                    for g in (0, 2):
                        act.wait_ge(S("c_t"), plus(b * 32, 4 * i + g + 1))
                        A(PT4[i % 2][:, 4 * g:4 * g + 4, :],
                          PS[:, 4 + g, :].rearrange("p (a n) -> p a n", a=4), ACT.Copy).then_inc(S("c_pta"), 1)

            cross(0, True)
            with act.Fori(1, B) as b:
                cross(b, False)

            norm("dn")

            def all_root(n):
                act.wait_ge(S("sq_sum"), n + 1)
                A(RS5[:, n, :], PS[:, 4 + n, :], ACT.Sqrt, bias=eps6,
                  scale=1.0 / (512 if n else 2048)).then_inc(S("sq_root"), 1)

            def evac(p, lo, hi):
                for m in range(lo, hi):
                    dst = QT5[:, m, :] if m < 16 else KT5[:, m - 16, :]
                    if m < 16:
                        act.wait_ge(S("proj_q"), 16 * SECOND[p] + m + 1)
                    else:
                        act.wait_ge(S("proj_k"), 4 * SECOND[p] + m - 15)
                    ins = A(dst, PS[:, m % 4, :], ACT.Copy)
                    if p == "e_":
                        if m >= 2:
                            act.wait_ge(S("sq_sum"), 2 + m - 1)
                        ins = A(SQ6[:, m % 2, :], PS[:, m % 4, :], ACT.Square)
                    ins.then_inc(S("proj_out"), 1)
                    if p == "d_" and m == 17:
                        all_root(0)
                    if p == "e_" and m >= 1:
                        std6(m - 1)

            def std6(m):
                act.wait_ge(S("sq_sum"), 2 + m + 1)
                if m >= 2:
                    act.wait_ge(S("e_n"), m - 1)
                A(RS6[:, m % 2, :], PS[:, 4 + m % 2, :], ACT.Sqrt, bias=eps6, scale=1.0 / 128).then_inc(S("sq_root"), 1)

            def values(p):
                for t in range(TT):
                    if p == "d_" and t == 2:
                        all_root(1)
                    act.wait_ge(S("proj_v"), TT * SECOND[p] + t + 1)
                    A(V5[:, t, :], PS[:, t, :], ACT.Copy).then_inc(S("values_out"), 1)

            evac("d_", 0, 20)
            values("d_")

            def core(p, n, PB, PT):
                def turn(i):
                    act.wait_ge(S("core_t"), CORE[p] + i + 1)
                    A(PT[:, i % 2, :], PS[:, 3 + i % 2, :], ACT.Copy).then_inc(S("core_pts"), 1)
                for i in range(n):
                    if i >= 3:
                        turn(i - 3)
                    act.wait_ge(S("core_m"), CORE[p] + i + 1)
                    for h in range(4):
                        v = PB[:, i % 4, h * P:(h + 1) * P]
                        ins = A(v, v, ACT.Exp, bias=nm5[:, i % 4, h:h + 1], accum_out=l5[:, i % 4, h:h + 1])
                    ins.then_inc(S("core_e"), 1)
                for i in range(n - 3, n):
                    turn(i)

            core("d_", 32, PB5, PT5)

            roots("en")

            def rms_rows(p, src):
                for t in range(TT):
                    act.wait_ge(S("hidden"), (0 if p == "en" else TT) + t + 1)
                    ins = A(HN6[:, t, :], src[:, t, :], ACT.Square, accum_out=ms[:, t:t + 1])
                    ins.then_inc(S("n_ms"), 1)
                act.wait_ge(S("n_ms"), TT if p == "en" else 2 * TT)
                A(std, ms, ACT.Sqrt, bias=eps6, scale=1.0 / C).then_inc(S("n_std"), 1)

            def rms_turn(p, w):
                for t in range(TT):
                    act.wait_ge(S("n_xt"), before[p] * TT + t + 1)
                    for k in range(KC):
                        ins = A(XNT[:, k, t * P:(t + 1) * P], PS[:, t, k * P:(k + 1) * P], ACT.Copy,
                                scale=w[:, k:k + 1])
                    ins.then_inc(S("n_xnT"), 1)

            rms_rows("en", XN)
            rms_turn("en", hw6)
            evac("e_", 0, 20)
            std6(19)
            values("e_")
            core("e_", 16, PB5, PT6)
            rms_rows("fn", XN)
            rms_turn("fn", fw6)
            experts("m1_", NF1, 0, W1S, SIL1, MW1, UP1, DOWN1, True, "n")
            with act.Fori(1, E8) as e:
                experts("m1_", NF1, e, W1S, SIL1, MW1, UP1, DOWN1, False, "n")


        @block.vector
        def _(dve):
            V = nc.vector
            link = Link(dve, S("dve_chain"))

            def norm(p, rows=None, bank=0, to="n_xn"):
                def scale(t):
                    dve.wait_ge(S("n_std"), ROOTS[p] + t + 1)
                    link(V.reciprocal(rstd[:, t:t + 1], std[:, t:t + 1]))
                    V.tensor_scalar(XN[:, t, :], X[:, t, :], mv[:, t, 0:1], rstd[:, t:t + 1],
                                    ALU.subtract, ALU.mult).then_inc(S(to), 1)

                for t in range(TT):
                    if rows:
                        dve.wait_ge(S("rows"), ROWS[rows] + t + 1)
                        V.tensor_tensor(X[:, t, :], X[:, t, :], PS[:, bank + t, :], ALU.add).then_inc(S("x_added"), 1)
                        dve.wait_ge(S("x_added"), ROWS[rows] + t + 1)
                    link(V.bn_stats(stat[:, t, :], X[:, t, :]))
                    V.bn_aggr(mv[:, t, :], stat[:, t, :]).then_inc(S("n_var"), 1)
                    if t and rows != "c_":
                        scale(t - 1)
                for t in (range(TT) if rows == "c_" else (TT - 1,)):
                    scale(t)

            def gate(p, eps):
                dve.wait_ge(S("glog"), GATED[p] + 1)
                lg = PS[:, 3, 0:TT * E8].rearrange("p (t e) -> p t e", t=TT)
                link(V.tensor_reduce(gs, lg, AX.X, ALU.max))
                V.tensor_tensor(gw, lg, gs.unsqueeze(2).to_broadcast([P, TT, E8]), ALU.subtract).then_inc(S("gsub"), 1)
                dve.wait_ge(S("gexp"), GATED[p] + 1)
                link(V.tensor_reduce(gs, gw, AX.X, ALU.add))
                link(V.reciprocal(gs, gs))
                link(V.tensor_tensor(gp, gw, gs.unsqueeze(2).to_broadcast([P, TT, E8]), ALU.mult))
                other = gp.unsqueeze(2).to_broadcast([P, TT, E8, E8])
                mine = gp.unsqueeze(3).to_broadcast([P, TT, E8, E8])
                r1 = area(24064, TT, E8, E8)
                r2 = area(24320, TT, E8, E8)
                link.at(V.tensor_tensor(r1, other, mine, ALU.is_gt))
                link(V.tensor_tensor(r2, other, mine, ALU.is_equal))
                tri = tri8.rearrange("p (a b) -> p a b", a=8).unsqueeze(1).to_broadcast([P, TT, E8, E8])
                link(V.tensor_tensor(r2, r2, tri, ALU.mult))
                link(V.tensor_tensor(r1, r1, r2, ALU.add))
                link(V.tensor_reduce(gw, r1, AX.X, ALU.add))
                link(V.tensor_scalar(gw, gw, 2.0, None, ALU.is_lt))
                link(V.tensor_tensor(gw, gw, gp, ALU.mult))
                link(V.tensor_reduce(gs, gw, AX.X, ALU.add))
                if eps:
                    link(V.tensor_scalar(gs, gs, eps, None, ALU.add))
                link(V.reciprocal(gs, gs))
                link(V.tensor_tensor(gw, gw, gs.unsqueeze(2).to_broadcast([P, TT, E8]), ALU.mult))

            def split_tokens(p, XS):
                for t in range(TT):
                    ts = slice(t * P, (t + 1) * P)
                    dve.wait_ge(S("n_xnT"), before[p] * TT + t + 1)
                    V.tensor_copy(XS[0][:, :, ts], XNT[:, :, ts]).then_inc(S("xs_hi"), 1)
                    dve.wait_ge(S("xs_hi"), XS_OF[p] * TT + t + 1)
                    rest(V, XS[1][:, :, ts], XNT[:, :, ts], XS[0][:, :, ts]).then_inc(S("xs"), 1)

            def experts(p, nf, e, widths, SIL, HS):
                for f in range(nf):
                    m = widths[f]
                    dve.wait_ge(S("moe_silu"), plus(e * nf, MOE[p] + f + 1))
                    h = SIL[0:m, f % 2, :]
                    V.tensor_tensor(h, h, PS[0:m, 5 + f % 2 * 2, :], ALU.mult).then_inc(S("h_step"), 1)
                    dve.wait_ge(S("h_step"), plus(e * 2 * nf, 2 * (MOE[p] + f) + 1))
                    V.tensor_copy(HS[0][0:m, f % 2, :], h).then_inc(S("h_step"), 1)
                    dve.wait_ge(S("h_step"), plus(e * 2 * nf, 2 * (MOE[p] + f) + 2))
                    rest(V, HS[1][0:m, f % 2, :], h, HS[0][0:m, f % 2, :]).then_inc(S("moe_hT"), 1)
                dve.wait_ge(S("moe_out"), plus(e * nf, MOE[p] + nf))
                for t in range(TT):
                    ins = V.scalar_tensor_tensor(X[:, t, :], PS[:, t, :], gw[:, t, :][:, bass.ds(e, 1)], X[:, t, :],
                                                 ALU.mult, ALU.add).then_inc(S("moe_acc"), 1)

            V.memset(eps5, 1e-5).then_inc(S("eps"), 1)
            V.memset(eps6, 1e-6).then_inc(S("eps"), 1)
            dve.wait_ge(S("ld_x"), 16)
            norm("xn")
            dve.wait_ge(S("ld_const"), 16)
            V.tensor_scalar(nbg, bg, -1.0, None, ALU.mult).then_inc(S("x_nbg"), 1)
            for j in range(KC):
                dve.wait_ge(S("x_q"), j + 1)
                if j >= 2:
                    link.sync()
                V.tensor_scalar(TMP[:, j % 2, :], PS[:, j, :], 0.0, None, ALU.min).then_inc(S("x_qmin"), 1)
                dve.wait_ge(S("x_qexp"), j + 1)
                link.at(V.scalar_tensor_tensor(QT[:, j, :], PS[:, j, :], 0.0, TMP[:, j % 2, :], ALU.max, ALU.add))
            link.sync()
            for j in range(KC):
                dve.wait_ge(S("x_gexp"), j + 1)
                V.tensor_scalar(G1[:, j, :], G1[:, j, :], 1.0, None, ALU.add).then_inc(S("x_pre"), 1)

            def kv_out(b0, b1):
                dve.wait_ge(S("x_kv"), b1)
                k = V.tensor_copy(ksum, PS[:, 7, 0:KC])
                link(k)
                for j in range(KC):
                    V.tensor_tensor(KV[:, bass.ds(b0, 1), j, :], PS[:, 6, j * P:(j + 1) * P].unsqueeze(1), block32.unsqueeze(1), ALU.mult)
                    ins = V.tensor_scalar(KS[:, bass.ds(b0, 1), j, :], block32.unsqueeze(1), ksum[:, j:j + 1], None, ALU.mult)
                ins.then_inc(S("x_kvs"), 1)

            def keys(b, first):
                for t in range(CT):
                    n = P if t < CT - 1 else LAST
                    s = t % 2 if t < CT - 1 else 2
                    kb = KB[0:n, t % 3 if t < CT - 1 else 3, :]
                    ps = PS[0:n, 4 + t % 2, :]
                    dve.wait_ge(S("k_ps"), plus(b * CT, t + 1))
                    V.tensor_scalar(KM[0:n, s, :], ps, 0.0, None, ALU.min).then_inc(S("k_min"), 1)
                    dve.wait_ge(S("k_exp"), plus(b * CT, t + 1))
                    if not first or t > 2:
                        dve.wait_ge(S("k_summed"), plus(b * (CT - 1), max(t - 3, 1) if t > 2 else t - 3))
                    V.scalar_tensor_tensor(kb, ps, 0.0, KM[0:n, s, :], ALU.max, ALU.add).then_inc(S("k_ready"), 1)
                    if not first or t >= 2:
                        dve.wait_ge(S("c_used"), plus(b * CT, t - 1))
                    dve.wait_ge(S("k_ready"), plus(b * CT, t + 1))
                    V.tensor_copy(KBS[0][0:n, s, :], kb).then_inc(S("k_hi"), 1)
                    dve.wait_ge(S("k_hi"), plus(b * CT, t + 1))
                    rest(V, KBS[1][0:n, s, :], kb, KBS[0][0:n, s, :]).then_inc(S("k_split"), 1)
                    if t == 0 and not first:
                        kv_out(plus(b, -1), b)

            keys(0, True)
            n0 = link.n
            with dve.Fori(1, B) as b:
                link.n, link.base = 0, n0 + (b - 1) * 1
                keys(b, False)
                assert link.n == 1
            link.n, link.base = n0 + (B - 1), 0
            kv_out(B - 1, B)
            for j in range(KC):
                dve.wait_ge(S("x_num"), j + 1)
                link(V.tensor_scalar(DEN[:, j, :], PS[:, 4 + j, :], 1e-6, None, ALU.add))
                link(V.tensor_tensor(DEN[:, j, :], DEN[:, j, :], G1[:, j, :], ALU.mult))
                link(V.reciprocal(DEN[:, j, :], DEN[:, j, :]))
                V.tensor_tensor(AT[:, j, :], PS[:, j, :], DEN[:, j, :], ALU.mult).then_inc(S("x_aT"), 1)

            norm("an", "x_")
            for step in STEPS:
                t = int(step[1])
                means, vars_, rvars = (x[:, 12 * t:12 * t + 12] for x in (red, red2, red3))
                xr, ta, tb = (x[:, t, :].rearrange("p (h d) -> p h d", d=64) for x in (XR, TA, TB))
                if step[0] == "A":
                    dve.wait_ge(S("a_qkvs"), t + 1)
                    q = QKV[:, t, 0:640].rearrange("p (h d) -> p h d", d=64)
                    a = TA[:, t, 0:640].rearrange("p (h d) -> p h d", d=64)
                    r = XR[:, t, 0:640].rearrange("p (h d) -> p h d", d=64)
                    co = cosT.unsqueeze(1).to_broadcast([P, 10, 64])
                    si = sinT.unsqueeze(1).to_broadcast([P, 10, 64])
                    link.at(V.tensor_tensor(a, q, co, ALU.mult))
                    link.at(V.tensor_tensor(r[:, :, 0:32], q[:, :, 32:64], si[:, :, 0:32], ALU.mult))
                    link.at(V.tensor_tensor(r[:, :, 32:64], q[:, :, 0:32], si[:, :, 32:64], ALU.mult))
                    link(V.tensor_copy(XR[:, t, 640:768], QKV[:, t, 640:768]))
                    link(V.tensor_tensor(r, r, a, ALU.add))
                    link(V.tensor_reduce(means, xr, AX.X, ALU.add))
                    link(V.tensor_scalar(means, means, 1.0 / 64, None, ALU.mult))
                    V.tensor_tensor(ta, xr, means.unsqueeze(2).to_broadcast([P, 12, 64]), ALU.subtract).then_inc(S("a_stat"), 1)
                if step[0] == "B":
                    dve.wait_ge(S("a_func"), STEP[f"A{t}"])
                    V.tensor_reduce(vars_, tb, AX.X, ALU.add).then_inc(S("a_stat"), 1)
                if step[0] == "C":
                    dve.wait_ge(S("a_func"), STEP[f"B{t}"])
                    link(V.reciprocal(rvars, vars_))
                    V.tensor_tensor(xr, ta, rvars.unsqueeze(2).to_broadcast([P, 12, 64]), ALU.mult).then_inc(S("a_qkvn"), 1)
            th = TANH.rearrange("p t h n -> p (t h) n")
            pf = PF.rearrange("p t h n -> p (t h) n")
            for step in "D0 D1 F0 D2 F1 D3 F2 F3".split():
                t = int(step[1])
                hs = slice(8 * t, 8 * t + 8)
                tm, top = MASKED[:, hs, :], red[:, hs]
                if step[0] == "D":
                    dve.wait_ge(S("a_tanh"), 2 * t + 2)
                    link(V.tensor_tensor(tm, th[:, hs, :], causal01.unsqueeze(1).to_broadcast([P, 8, 64]), ALU.mult))
                    link(V.tensor_tensor(tm, tm, causalm1.unsqueeze(1).to_broadcast([P, 8, 64]), ALU.add))
                    link(V.tensor_reduce(top, tm, AX.X, ALU.max))
                    V.tensor_tensor(tm, tm, top.unsqueeze(2).to_broadcast([P, 8, 64]), ALU.subtract).then_inc(S("a_stat"), 1)
                else:
                    dve.wait_ge(S("a_func"), 2 * TT + t + 1)
                    link(V.tensor_reduce(top, tm, AX.X, ALU.add))
                    link(V.reciprocal(top, top))
                    if t == 0:
                        dve.wait_ge(S("a_pf0"), 1)
                    for h in (0, 1):
                        r = slice(64 * h, 64 * h + 64)
                        V.tensor_tensor(pf[r, hs, 64 * h:64 * h + 64], MASKED[r, hs, :],
                                        red[r, hs].unsqueeze(2).to_broadcast([64, 8, 64]), ALU.mult).then_inc(S("a_p"), 1)
            for t in range(TT):
                dve.wait_ge(S("a_pv"), 2 * t + 2)
                V.tensor_copy(OT2[:, :, t * P:(t + 1) * P], PS[:, 2 + t % 2, :].rearrange("p (c n) -> p c n", c=4)).then_inc(S("a_oT"), 1)

            norm("mn", "a_", 4)
            split_tokens("mn", XS0)
            gate("m0", 0.0)
            experts("m0_", NF0, 0, [P] * NF0, SIL0, HS0)
            with dve.Fori(1, E8) as e:
                dve.wait_ge(S("moe_acc"), e * TT)
                experts("m0_", NF0, e, [P] * NF0, SIL0, HS0)
            dve.wait_ge(S("moe_acc"), E8 * TT)

            norm("cn")
            dve.wait_ge(S("ld_vec"), 32)
            link.at(V.tensor_copy(lens, LEN[:, :]))
            link.at(V.tensor_scalar(gqs, gq1, 1.0 / 32 ** 0.5, None, ALU.mult))
            link.at(V.tensor_tensor(bvv, bv1, bvi1, ALU.add))
            dve.wait_ge(S("c_qstd"), 1)
            link(V.reciprocal(RS4[:, 0:512], RS4[:, 0:512]))
            for j in range(KC):
                link.at(V.scalar_tensor_tensor(QT4[:, j, :], QT4[:, j, :], gqs[:, j:j + 1], RS4[:, 0:512],
                                               ALU.mult, ALU.mult))
            link.sync()
            dve.wait_ge(S("c_qb0"), 1)
            dve.wait_ge(S("ld_bo"), 32)

            def cross(b, first):
                if not first:
                    dve.wait_ge(S("c_s"), b * 8)
                for h in range(4):
                    r = slice(32 * h, 32 * h + 32)
                    link.at(V.tensor_copy(QB4[r, :, h * SEQ:(h + 1) * SEQ], QT4[r, :, bass.ds(b * SEQ, SEQ)]))
                link(V.tensor_copy(lenb, lens[:, bass.ds(b, 1)]))
                link.at(V.tensor_scalar(BIAS, IOTA, lenb, -1e9, ALU.is_ge, ALU.mult))
                def maximum(i):
                    pb = PB4[:, i % 2, :]
                    dve.wait_ge(S("c_s"), plus(b * 8, i + 1))
                    link.at(V.tensor_reduce(mx[:, i % 2, 0:1], PSF[:, 0:IMG], AX.X, ALU.max))
                    link(V.tensor_tensor_reduce(pb[:, IMG:CTX], PSF[:, IMG:CTX], BIAS, 1.0, -3e38, ALU.add,
                                                ALU.max, mx[:, i % 2, 1:2]))
                    V.tensor_scalar(nmx[:, i % 2, :], mx[:, i % 2, :], -1.0, None, ALU.mult).then_inc(S("c_max"), 1)

                nv = 0
                for u, (kind, c, j) in enumerate(PROD):
                    bank = 4 + u % 4
                    if u == len(PROD) - 1:
                        maximum(0)
                    if kind == "V":
                        dve.wait_ge(S("c_v"), plus(b * NV, nv + 1))
                        nv += 1
                        n = TILES[c][1]
                        ins = V.tensor_copy(values4(c)[0:n, :], PS[0:n, bank, :])
                        ins.then_inc(S("c_vs"), 1)
                    if kind == "R":
                        dve.wait_ge(S("c_rs"), plus(b * 4, c + 1))
                        lo, hi = CO[c], CO[c] + CN[c]
                        link(V.reciprocal(RS4[:, lo:hi], RS4[:, lo:hi]))
                        tl = IMG if c == 0 else lo
                        link(V.scalar_tensor_tensor(RS4[:, tl:hi], IOTA[:, tl - IMG:hi - IMG], lenb, RS4[:, tl:hi],
                                                    ALU.is_lt, ALU.mult))
                        for jj in range(KC):
                            if c == 0:
                                V.scalar_tensor_tensor(KT4[:, jj, 0:IMG], KT4[:, jj, 0:IMG], gki1[:, jj:jj + 1],
                                                       RS4[:, 0:IMG], ALU.mult, ALU.mult)
                            ins = V.scalar_tensor_tensor(KT4[:, jj, tl:hi], KT4[:, jj, tl:hi], gk1[:, jj:jj + 1],
                                                         RS4[:, tl:hi], ALU.mult, ALU.mult)
                        ins.then_inc(S("c_kn"), 1)

                def turned(i):
                    dve.wait_ge(S("c_t"), plus(b * 32, 4 * i + 2))
                    V.tensor_copy(PT4[i % 2][:, 4:8, :], PS[:, 5, :].rearrange("p (a n) -> p a n", a=4)).then_inc(S("c_ptd"), 1)
                    dve.wait_ge(S("c_t"), plus(b * 32, 4 * i + 4))
                    V.tensor_copy(PT4[i % 2][:, 12:14, :], PS[:, 4, 0:2 * P].rearrange("p (a n) -> p a n", a=2)).then_inc(S("c_ptd"), 1)

                def heads_out(i):
                    dve.wait_ge(S("c_pv"), plus(b * 8, i + 1))
                    for h in (0, 1):
                        lo = 64 * (i % 2) + 32 * h
                        ins = V.tensor_copy(AT4[lo:lo + 32, i // 2, bass.ds(b * SEQ, SEQ)],
                                            PS[lo:lo + 32, 7, 64 * h:64 * h + 64])
                    ins.then_inc(S("c_at"), 1)

                for i in range(8):
                    pb = PB4[:, i % 2, :]
                    if i:
                        maximum(i)
                    if i:
                        turned(i - 1)
                    if i >= 2:
                        heads_out(i - 2)
                    dve.wait_ge(S("c_et"), plus(b * 8, i + 1))
                    link(V.reciprocal(rls[:, i % 2, :], lsum[:, i % 2, :]))
                    V.tensor_scalar(pb[:, 0:IMG], pb[:, 0:IMG], rls[:, i % 2, 0:1], None, ALU.mult)
                    V.tensor_scalar(pb[:, IMG:CTX], pb[:, IMG:CTX], rls[:, i % 2, 1:2], None,
                                    ALU.mult).then_inc(S("c_pn"), 1)
                heads_out(6)
                turned(7)
                heads_out(7)

            n1 = link.n
            cross(0, True)
            per = link.n - n1
            with dve.Fori(1, B) as b:
                link.n, link.base = 0, n1 + b * per
                cross(b, False)
                assert link.n == per
            link.n, link.base = n1 + B * per, 0
            dve.wait_ge(S("c_at"), B * 8)
            for j in range(KC):
                V.tensor_scalar(AT4[:, j, :], AT4[:, j, :], bvv[:, j:j + 1], None, ALU.add).then_inc(S("c_att"), 1)
            for t in range(TT):
                link.at(V.tensor_tensor(X[:, t, :], X[:, t, :], BO4, ALU.add))
            link.sync()

            norm("dn", "c_")
            link(V.tensor_scalar(qws, qw5, 0.125, None, ALU.mult))
            for n in (0, 1):
                dve.wait_ge(S("sq_root"), n + 1)
                link(V.reciprocal(RS5[:, n, :], RS5[:, n, :]))
                for m in (range(16) if n == 0 else range(4)):
                    v, w = (QT5[:, m, :], qws[:, m:m + 1]) if n == 0 else (KT5[:, m, :], kw5[:, m:m + 1])
                    ins = V.scalar_tensor_tensor(v, v, w, RS5[:, n, :], ALU.mult, ALU.mult)
                ins.then_inc(S("d_qkn"), 1)

            def core(p, n, PB, bias, o_at):
                def recip(i):
                    dve.wait_ge(S("core_e"), CORE[p] + i + 1)
                    V.reciprocal(rl5[:, i % 4, :], l5[:, i % 4, :]).then_inc(S("core_rl"), 1)

                def outs(i):
                    dst, src, need = o_at(i)
                    dve.wait_ge(S("core_pv"), CORE[p] + need)
                    V.tensor_copy(dst, src).then_inc(S("core_oT"), 1)

                for i in range(n):
                    v = PB[:, i % 4, :].rearrange("p (h n) -> p h n", h=4)
                    dve.wait_ge(S("core_s"), CORE[p] + i + 1)
                    if i >= 4:
                        dve.wait_ge(S("core_t"), CORE[p] + i - 3)
                    ins = V.tensor_tensor(v, PS[:, i % 3, :].rearrange("p (h n) -> p h n", h=4), bias(i), ALU.add)
                    ins.then_inc(S("core_sb"), 1)
                    if i >= 2:
                        recip(i - 2)
                    dve.wait_ge(S("core_sb"), CORE[p] + i + 1)
                    V.tensor_reduce(nm5[:, i % 4, :], v, AX.X, ALU.max, negate=True).then_inc(S("core_m"), 1)
                    if i >= 5 and o_at(i - 5):
                        outs(i - 5)
                recip(n - 2)
                recip(n - 1)
                for i in range(n - 5, n):
                    if o_at(i):
                        outs(i)

            def o5(i):
                t, g = i // 8, i % 8
                if g % 2 == 0:
                    return None
                return (OT5[:, 4 * (g // 2):4 * (g // 2) + 4, t * P:(t + 1) * P],
                        PS[:, 5 + i // 2 % 2, :].rearrange("p (c n) -> p c n", c=4), i + 1)

            dve.wait_ge(S("ld_alibi"), 16)
            core("d_", 32, PB5, lambda i: ALIBI[:, i % 8, :, :], o5)

            norm("en", "d_", to="hidden")

            def rms_rows(p):
                dve.wait_ge(S("n_std"), (ROOTS["en2"] if p == "en" else ROOTS["fn"]) + 1)
                link(V.reciprocal(rstd, std))
                for t in range(TT):
                    V.tensor_scalar(HN6[:, t, :], XN[:, t, :], rstd[:, t:t + 1], None, ALU.mult).then_inc(S("n_xn"), 1)

            rms_rows("en")
            link(V.tensor_scalar(qws[:, 0:1], qw6, 1.0 / 128 ** 0.5, None, ALU.mult))
            for m in range(20):
                v = QT5[:, m, :] if m < 16 else KT5[:, m - 16, :]
                w = qws[:, 0:1] if m < 16 else kw6
                dve.wait_ge(S("sq_root"), 2 + m + 1)
                link(V.reciprocal(RS6[:, m % 2, :], RS6[:, m % 2, :]))
                V.scalar_tensor_tensor(v, v, w, RS6[:, m % 2, :], ALU.mult, ALU.mult).then_inc(S("e_n"), 1)
                dve.wait_ge(S("e_n"), m + 1)
                if m >= 2:
                    dve.wait_ge(S("e_rope"), m - 1)
                for lo, hi in ((0, 64), (64, 0)):
                    ins = V.tensor_tensor(RB6[lo:lo + 64, m % 2, :].rearrange("p (b n) -> p b n", b=B),
                                          v[hi:hi + 64, :].rearrange("p (b n) -> p b n", b=B) if lo == 0 else
                                          v[0:64, :].rearrange("p (b n) -> p b n", b=B),
                                          sin6[(64 if lo == 0 else 0):(128 if lo == 0 else 64), :].unsqueeze(1).to_broadcast([64, B, SEQ]), ALU.mult)
                ins.then_inc(S("e_rb"), 1)

            def o6(i):
                t, g = i // 4, i % 4
                return (OT5[:, 4 * g:4 * g + 4, t * P:(t + 1) * P],
                        PS[:, 5 + i % 2, :].rearrange("p (c n) -> p c n", c=4), i + 1)

            core("e_", 16, PB5, lambda i: mask6.unsqueeze(1).to_broadcast([P, 4, P]), o6)
            for t in range(TT):
                dve.wait_ge(S("rows"), ROWS["e_"] + t + 1)
                V.tensor_tensor(XN[:, t, :], XN[:, t, :], PS[:, t, :], ALU.add).then_inc(S("hidden"), 1)
            dve.wait_ge(S("hidden"), 2 * TT)
            for t in range(TT):
                link.at(V.tensor_tensor(X[:, t, :], X[:, t, :], XN[:, t, :], ALU.add))
            rms_rows("fn")
            split_tokens("fn", XS1)
            gate("m1", 1e-9)
            experts("m1_", NF1, 0, W1S, SIL1, HS1)
            with dve.Fori(1, E8) as e:
                dve.wait_ge(S("moe_acc"), e * TT + E8 * TT)
                experts("m1_", NF1, e, W1S, SIL1, HS1)

        @block.tensor
        def _(pe):
            M = nc.tensor.matmul

            def M3(out, a, b, start, stop):
                M(out, a[0], b[0], start=start, stop=False)
                M(out, a[0], b[1], start=False, stop=False)
                return M(out, a[1], b[0], start=False, stop=stop)

            def norm(p):
                for t in range(TT):
                    pe.wait_ge(S("n_xn"), before[p] * TT + t + 1)
                    for k in range(KC):
                        ins = nc.tensor.transpose(PS[:, t, k * P:(k + 1) * P], XN[:, t, k * P:(k + 1) * P], ident)
                    ins.then_inc(S("n_xt"), 1)
                pe.wait_ge(S("n_xnT"), before[p] * TT + TT)

            def to_rows(p, lhs, rhs, nk, bank=0):
                for t in range(TT):
                    for k in range(nk):
                        ins = M(PS[:, bank + t, :], lhs[:, k, t * P:(t + 1) * P], rhs[:, k, :],
                                start=(k == 0), stop=(k == nk - 1))
                    ins.then_inc(S("rows"), 1)

            def gate(p, W):
                for t in range(TT):
                    for k in range(KC):
                        ins = M(PS[:, 3, t * E8:(t + 1) * E8], XNT[:, k, t * P:(t + 1) * P], W[:, k, :],
                                start=(k == 0), stop=(k == KC - 1))
                ins.then_inc(S("glog"), 1)

            def experts(p, nf, e, widths, XS, UP, DOWN, HS, first):
                if first:
                    pe.wait_ge(S("xs"), (GATED[p[:-1]] + 1) * TT)

                def up(f):
                    m = widths[f]
                    pe.wait_ge(S("w_up"), plus(e * nf, MOE[p] + f + 1))
                    if f >= 2:
                        pe.wait_ge(S("moe_hT"), plus(e * nf, MOE[p] + f - 1))
                    for w in (0, 1):
                        for k in range(KC):
                            c = w * 512 + k * P
                            ins = M3(PS[0:m, 4 + f % 2 * 2 + w, :], [u[:, f % 2, c:c + m] for u in UP],
                                     [x[:, k, :] for x in XS], k == 0, k == KC - 1)
                    ins.then_inc(S("moe_h"), 1)

                def down(f):
                    m = widths[f]
                    pe.wait_ge(S("moe_hT"), plus(e * nf, MOE[p] + f + 1))
                    pe.wait_ge(S("w_down"), plus(e * nf, MOE[p] + f + 1))
                    if f == 0 and first:
                        pe.wait_ge(S("gsub"), GATED[p[:-1]] + 1)
                    if f == 0 and not first:
                        pe.wait_ge(S("moe_acc"), plus(e * TT, ACC[p]))
                    for t in range(TT):
                        ins = M3(PS[:, t, :], [h[0:m, f % 2, t * P:(t + 1) * P] for h in HS],
                                 [d[0:m, f % 2, :] for d in DOWN], f == 0, f == nf - 1)
                    ins.then_inc(S("moe_out"), 1)

                up(0)
                for f in range(nf):
                    if f + 1 < nf:
                        up(f + 1)
                    down(f)

            pe.wait_ge(S("ld_const"), 16)
            norm("xn")
            for name, W, ld, base in (("x_q", WQ, "ld_wq", 0), ("x_g", WG, "ld_wg", 4)):
                pe.wait_ge(S(ld), 16)
                for j in range(KC):
                    for k in range(KC):
                        ins = M(PS[:, base + j, :], W[:, k, j * P:(j + 1) * P], XNT[:, k, :],
                                start=(k == 0), stop=(k == KC - 1))
                    ins.then_inc(S(name), 1)
            pe.wait_ge(S("wk_split"), 1)
            pe.wait_ge(S("x_pre"), KC)

            def kv_sum(b1):
                pe.wait_ge(S("x_ctks"), b1)
                pe.wait_ge(S("k_summed"), b1 * (CT - 1))
                for j in range(KC):
                    for k in range(KC):
                        M(PS[:, 6, j * P:(j + 1) * P], CTK[:, k, j * P:(j + 1) * P], WV[:, k, j * P:(j + 1) * P],
                          start=(k == 0), stop=(k == KC - 1))
                for j in range(KC):
                    ins = M(PS[:, 7, j:j + 1], KACC[:, j * P:(j + 1) * P], ones[:, 0:1], start=True, stop=True)
                ins.then_inc(S("x_kv"), 1)

            def keys(b, first):
                def proj(t):
                    n = P if t < CT - 1 else LAST
                    s = t % 2 if t < CT - 1 else 2
                    pe.wait_ge(S("cols_split"), plus(b * CT, t + 1))
                    for k in range(KC):
                        ins = M3(PS[0:n, 4 + t % 2, :], [c[:, k * P:k * P + n] for c in CTS[s]],
                                 [w[:, k, :] for w in WKS], k == 0, k == KC - 1)
                    ins.then_inc(S("k_ps"), 1)

                def outer(t):
                    n = P if t < CT - 1 else LAST
                    s = t % 2 if t < CT - 1 else 2
                    pe.wait_ge(S("rows_split"), plus(b * CT, t + 1))
                    pe.wait_ge(S("k_split"), plus(b * CT, t + 1))
                    for c in range(KC):
                        ins = M3(PS[:, c, :], [x[0:n, c * P:(c + 1) * P] for x in CRS[s]],
                                 [k[0:n, s, :] for k in KBS], t == 0, t == CT - 1)
                    ins.then_inc(S("c_used"), 1)

                proj(0)
                if not first:
                    kv_sum(b)
                for t in range(CT):
                    if t + 1 < CT:
                        proj(t + 1)
                    outer(t)

            pe.wait_ge(S("ld_wv"), 16)
            keys(0, True)
            with pe.Fori(1, B) as b:
                keys(b, False)
            kv_sum(B)
            pe.wait_ge(S("x_kvs"), B)
            for j in range(KC):
                for b in range(B):
                    s = slice(b * SEQ, (b + 1) * SEQ)
                    M(PS[:, j, s], KV[:, b, j, :], QT[:, j, s], start=True, stop=True)
                    ins = M(PS[:, 4 + j, s], KS[:, b, j, :], QT[:, j, s], start=True, stop=True)
                ins.then_inc(S("x_num"), 1)
            pe.wait_ge(S("x_aT"), KC)
            pe.wait_ge(S("ld_wo"), 16)
            to_rows("x_", AT, WO, KC)

            norm("an")
            pe.wait_ge(S("ld_self"), 32)
            for t in range(TT):
                for lo, hi, bank in ((0, 512, 2 * t), (512, 768, 2 * t + 1)):
                    for k in range(KC):
                        ins = M(PS[:, bank, 0:hi - lo], XNT[:, k, t * P:(t + 1) * P], W2[:, k, lo:hi],
                                start=(k == 0), stop=(k == KC - 1))
                ins.then_inc(S("a_qkv"), 1)
            for t in range(TT):
                pe.wait_ge(S("a_qkvn"), t + 1)
                for c in range(4):
                    ins = nc.tensor.transpose(PS[:, t, c * P:(c + 1) * P], XR[:, t, c * P:(c + 1) * P], ident)
                ins.then_inc(S("a_qt"), 1)
            for t in range(TT):
                ins = nc.tensor.transpose(PS[:, 4, t * P:(t + 1) * P], XR[:, t, 512:640], ident)
            ins.then_inc(S("a_kt"), 1)
            pe.wait_ge(S("a_qts"), TT)
            pe.wait_ge(S("a_kts"), 1)
            for t in range(TT):
                for g in range(2):
                    r = slice(64 * g, 64 * g + 64)
                    for c in range(4):
                        ins = M(PS[:, 2 * t + g, c * P:(c + 1) * P], QT2[r, t, c, :], KT2[r, t, :],
                                start=True, stop=True)
                    ins.then_inc(S("a_s"), 1)
            def trans(i):
                t, g = i // 2, i % 2
                pe.wait_ge(S("a_p"), 2 * t + 2)
                if i >= 2:
                    pe.wait_ge(S("a_pts"), i - 1)
                for c in range(4):
                    ins = nc.tensor.transpose(PS[:, i % 2, c * P:(c + 1) * P], PF[:, t, 4 * g + c, :], ident)
                ins.then_inc(S("a_pt"), 1)

            trans(0)
            for i in range(2 * TT):
                t, g = i // 2, i % 2
                if i + 1 < 2 * TT:
                    trans(i + 1)
                pe.wait_ge(S("a_pts"), i + 1)
                if t >= 2 and g == 0:
                    pe.wait_ge(S("a_oT"), t - 1)
                M(PS[64 * g:64 * g + 64, 2 + t % 2, :], VAL[:, t, 64 * g:64 * g + 64], PT2[:, i % 2, :],
                  start=True, stop=True).then_inc(S("a_pv"), 1)
            pe.wait_ge(S("a_oT"), TT)
            to_rows("a_", OT2, WO2, 4, 4)

            norm("mn")
            pe.wait_ge(S("ld_gate"), 16)
            gate("m0", GATE0)
            experts("m0_", NF0, 0, [P] * NF0, XS0, UP0, DOWN0, HS0, True)
            with pe.Fori(1, E8) as e:
                experts("m0_", NF0, e, [P] * NF0, XS0, UP0, DOWN0, HS0, False)

            norm("cn")
            pe.wait_ge(S("moe_acc"), E8 * TT)
            pe.wait_ge(S("ld_cross"), 16 * 5)
            for j in range(KC):
                for k in range(KC):
                    ins = M(PS[:, j, :], WQ4[:, k, j * P:(j + 1) * P], XNT[:, k, :], start=(k == 0), stop=(k == KC - 1))
                ins.then_inc(S("c_q"), 1)
            SQQ = area(0, KC, C)
            for j in range(KC):
                pe.wait_ge(S("c_qe"), j + 1)
                ins = M(PS[:, 4, :], ones, SQQ[:, j, :], start=(j == 0), stop=(j == KC - 1))
            ins.then_inc(S("c_qr"), 1)
            pe.wait_ge(S("c_qstd"), 1)

            def cross(b, first):
                order = {"K": 0, "V": 0, "R": 0}
                at = []
                for c in range(4):
                    pe.wait_ge(S(f"ld_slot{c}"), plus(b * 16, slot_base("x", c) + 16))
                if not first:
                    pe.wait_ge(S("c_at"), b * 8)
                def scores(i):
                    j, half = i // 2, i % 2
                    r = slice(64 * half, 64 * half + 64)
                    if i or not first:
                        pe.wait_ge(S("c_max"), plus(b * 8, i))
                    for lo in (512, 1024, 1536, 0):
                        hi = min(lo + 512, CTX)
                        if lo == 0 and (i or not first):
                            pe.wait_ge(S("c_ei"), plus(b * 8, i))
                        ins = M(PS[:, lo // 512, 0:hi - lo], QB4[r, j, 128 * half:128 * half + 128], KT4[r, j, lo:hi],
                                start=True, stop=True)
                    ins.then_inc(S("c_s"), 1)

                for u, (kind, c, j) in enumerate(PROD):
                    bank = 4 + u % 4
                    if u == len(PROD) - 1:
                        pe.wait_ge(S("c_kn"), plus(b * 4, 4))
                        scores(0)
                    if u >= 4:
                        k0, n0 = at[u - 4]
                        sem, per = {"I": ("c_kt", NK), "K": ("c_kt", NK), "V": ("c_vs", NV), "R": ("c_rs", 4)}[k0]
                        pe.wait_ge(S(sem), plus(b * per, n0 + 1))
                    kk = "K" if kind == "I" else kind
                    at.append((kk, order[kk]))
                    order[kk] += 1
                    if kind == "I":
                        for k in range(KC):
                            ins = M(PS[:, bank, 0:IMG], WKI4[:, k, j * P:(j + 1) * P], CC[0][:, k, 0:IMG],
                                    start=(k == 0), stop=(k == KC - 1))
                        ins.then_inc(S("c_k"), 1)
                    if kind == "K":
                        if j == 0:
                            pe.wait_ge(S("cols_split"), plus(b * 6, B * CT + c + 1))
                            if first:
                                pe.wait_ge(S("wk_split"), 2)
                        for k in range(KC):
                            ins = M3(PS[:, bank, 0:SUB[c][2]], [w[:, k, j * P:(j + 1) * P] for w in WKS4],
                                     [CHI[c][:, k, :], rest_of(c)[:, k, :]], k == 0, k == KC - 1)
                        ins.then_inc(S("c_k"), 1)
                    if kind == "V":
                        lo, n = TILES[c]
                        if first:
                            pe.wait_ge(S("wk_split"), 3)
                        for k in range(KC):
                            if lo < IMG:
                                ins = M(PS[0:n, bank, :], CC[0][:, k, lo:lo + n], WVI4[:, k, :],
                                        start=(k == 0), stop=(k == KC - 1))
                            else:
                                part, o = (0, 0) if c == 2 else (1 + (c - 3) // 2, P * ((c - 3) % 2))
                                ins = M3(PS[0:n, bank, :], [CHI[part][:, k, o:o + n], rest_of(part)[:, k, o:o + n]],
                                         [w[:, k, :] for w in WVS4], k == 0, k == KC - 1)
                        ins.then_inc(S("c_v"), 1)
                    if kind == "R":
                        pe.wait_ge(S("c_sq"), plus(b * 4, c + 1))
                        M(PS[:, bank, 0:CN[c]], ones, ACC4[:, CO[c]:CO[c] + CN[c]], start=True,
                          stop=True).then_inc(S("c_r"), 1)
                def turn(i, groups):
                    for g in groups:
                        if g == 0:
                            pe.wait_ge(S("c_pn"), plus(b * 8, i + 1))
                            if i:
                                pe.wait_ge(S("c_ptd"), plus(b * 16, 2 * i))
                        if g == 2 and i:
                            pe.wait_ge(S("c_pta"), plus(b * 16, 2 * i))
                        if g == 3:
                            pe.wait_ge(S("c_pta"), plus(b * 16, 2 * i + 1))
                        for n, t in enumerate(GROUPS[g]):
                            lo, w = TILES[t]
                            ins = nc.tensor.transpose(PS[0:w, 4 + g % 3, n * P:(n + 1) * P],
                                                      PB4[:, i % 2, lo:lo + w], ident)
                        ins.then_inc(S("c_t"), 1)

                def weigh(i):
                    pe.wait_ge(S("c_pta"), plus(b * 16, 2 * i + 2))
                    pe.wait_ge(S("c_ptd"), plus(b * 16, 2 * i + 2))
                    if i:
                        pe.wait_ge(S("c_at"), plus(b * 8, i))
                    h = 64 * (i % 2)
                    flat = [t for g in GROUPS for t in g]
                    for n, t in enumerate(flat):
                        w = TILES[t][1]
                        ins = M(PS[h:h + 64, 7, 0:P], values4(t)[0:w, 64 * i:64 * i + 64], PT4[i % 2][0:w, n, :],
                                start=(n == 0), stop=(n == CT))
                    ins.then_inc(S("c_pv"), 1)

                for i in range(7):
                    scores(i + 1)
                    if i == 0:
                        pe.wait_ge(S("c_vs"), plus(b * NV, NV))
                    turn(i, (0, 1, 2))
                    if i:
                        weigh(i - 1)
                    turn(i, (3,))
                weigh(6)
                turn(7, (0, 1, 2))
                turn(7, (3,))
                weigh(7)

            cross(0, True)
            with pe.Fori(1, B) as b:
                cross(b, False)
            pe.wait_ge(S("c_att"), KC)
            pe.wait_ge(S("ld_wo"), 32)
            to_rows("c_", AT4, WO4, KC)

            norm("dn")

            def project(p):
                for m in range(20):
                    W, c, name = (WQ5, m, "q") if m < 16 else (WK5, m - 16, "k")
                    if c == 0:
                        pe.wait_ge(S("ld_" + name), 16 if p == "d_" else 32)
                    if m >= 4:
                        pe.wait_ge(S("proj_out"), 20 * SECOND[p] + m - 3)
                    for k in range(KC):
                        ins = M(PS[:, m % 4, :], W[:, k, c * P:(c + 1) * P], XNT[:, k, :],
                                start=(k == 0), stop=(k == KC - 1))
                    ins.then_inc(S("proj_" + name), 1)
                    if p == "d_" and m == 17:
                        all_squares(0)
                    if p == "e_" and m >= 1:
                        squares(m - 1)
                pe.wait_ge(S("ld_v"), 16 if p == "d_" else 32)
                for t in range(TT):
                    pe.wait_ge(S("proj_out"), 20 * SECOND[p] + 17 + t)
                    if p == "e_" and t == 1:
                        squares(19)
                    if p == "d_" and t == 2:
                        all_squares(1)
                    for k in range(KC):
                        ins = M(PS[:, t, :], XNT[:, k, t * P:(t + 1) * P], WV5[:, k, :],
                                start=(k == 0), stop=(k == KC - 1))
                    ins.then_inc(S("proj_v"), 1)

            def all_squares(n):
                pe.wait_ge(S("d_sq"), n + 1)
                M(PS[:, 4 + n, :], ones, ACC5[:, n, :], start=True, stop=True).then_inc(S("sq_sum"), 1)

            def squares(m):
                pe.wait_ge(S("proj_out"), 20 + m + 1)
                if m >= 2:
                    pe.wait_ge(S("sq_root"), 2 + m - 1)
                M(PS[:, 4 + m % 2, :], ones, SQ6[:, m % 2, :], start=True, stop=True).then_inc(S("sq_sum"), 1)

            project("d_")

            def core(p, n, PB, PT, score, weigh, old):
                def turn(i):
                    pe.wait_ge(S("core_pn"), CORE[p] + i + 1)
                    if i >= 2:
                        pe.wait_ge(S("core_pts"), CORE[p] + i - 1)
                    for h in range(4):
                        ins = nc.tensor.transpose(PS[:, 3 + i % 2, h * P:(h + 1) * P],
                                                  PB[:, i % 4, h * P:(h + 1) * P], ident)
                    ins.then_inc(S("core_t"), 1)

                for i in range(n + 4):
                    if i < n:
                        if i >= 3:
                            pe.wait_ge(S("core_sb"), CORE[p] + i - 2)
                        for h in range(4):
                            q, k = score(i, h)
                            ins = M(PS[:, i % 3, h * P:(h + 1) * P], q, k, start=True, stop=True)
                        ins.then_inc(S("core_s"), 1)
                    if 3 <= i < n + 3:
                        turn(i - 3)
                    if i >= 4:
                        pe.wait_ge(S("core_pts"), CORE[p] + i - 3)
                        if old(i - 4):
                            pe.wait_ge(S("core_oT"), HEADS_OUT[p] + old(i - 4))
                        o, v = weigh(i - 4)
                        M(o, v, PT[:, (i - 4) % 2, :], start=True, stop=True).then_inc(S("core_pv"), 1)

            def score5(i, h):
                t, g = i // 8, i % 8
                r, s = slice(64 * (g % 2), 64 * (g % 2) + 64), slice(t * P, (t + 1) * P)
                return QT5[r, 4 * (g // 2) + h, s], KT5[r, g // 2, s]

            def weigh5(i):
                t, g = i // 8, i % 8
                return (PS[64 * (g % 2):64 * (g % 2) + 64, 5 + i // 2 % 2, :], V5[:, t, 64 * g:64 * g + 64])

            pe.wait_ge(S("values_out"), TT)
            pe.wait_ge(S("d_qkn"), 2)
            core("d_", 32, PB5, PT5, score5, weigh5, lambda i: max(0, i // 2 - 1) if i % 2 == 0 else 0)
            pe.wait_ge(S("ld_o"), 16)
            pe.wait_ge(S("core_oT"), 16)
            to_rows("d_", OT5, WO5, 16)

            def rms_turn(p):
                for t in range(TT):
                    pe.wait_ge(S("n_xn"), before[p] * TT + t + 1)
                    for k in range(KC):
                        ins = nc.tensor.transpose(PS[:, t, k * P:(k + 1) * P], HN6[:, t, k * P:(k + 1) * P], ident)
                    ins.then_inc(S("n_xt"), 1)
                pe.wait_ge(S("n_xnT"), before[p] * TT + TT)

            rms_turn("en")
            project("e_")

            def score6(i, h):
                t, g = i // 4, i % 4
                s = slice(t * P, (t + 1) * P)
                return QT5[:, 4 * g + h, s], KT5[:, g, s]

            def weigh6(i):
                t, g = i // 4, i % 4
                return PS[:, 5 + i % 2, :], V5[:, t, P * g:P * g + P]

            pe.wait_ge(S("values_out"), 2 * TT)
            pe.wait_ge(S("e_rope"), 20)
            core("e_", 16, PB5, PT6, score6, weigh6, lambda i: max(0, i - 1))
            pe.wait_ge(S("ld_o"), 32)
            pe.wait_ge(S("core_oT"), 32)
            to_rows("e_", OT5, WO5, 16)
            rms_turn("fn")
            pe.wait_ge(S("ld_gate"), 32)
            gate("m1", GATE1)
            experts("m1_", NF1, 0, W1S, XS1, UP1, DOWN1, HS1, True)
            with pe.Fori(1, E8) as e:
                experts("m1_", NF1, e, W1S, XS1, UP1, DOWN1, HS1, False)


def lay(w):
    n, m = w.shape
    return np.ascontiguousarray(w.reshape(n // 128, 128, m).transpose(1, 0, 2))


def constants():
    c = np.zeros((128, 964), np.float32)
    p = np.arange(128)
    c[:, 0:128] = np.eye(128)
    c[:, 128:256] = 1.0
    c[:, 256:384] = p[:, None] // 32 == p[None, :] // 32
    inv = (1.0 / np.float32(1000000.0) ** (np.arange(0, 64, 2, dtype=np.float32) / np.float32(64))).astype(np.float32)
    f = np.arange(64, dtype=np.float32)[:, None] * inv[None, :]
    cos, sin = np.cos(f), np.sin(f)
    c[:, 384:448] = np.tile(np.concatenate([cos, cos], 1), (2, 1))
    c[:, 448:512] = np.tile(np.concatenate([-sin, sin], 1), (2, 1))
    ok = (np.arange(64)[None, :] <= p[:, None] % 64).astype(np.float32)
    c[:, 512:576] = ok
    c[:, 576:640] = ok - 1
    c[:, 640:704] = (np.arange(8)[None, :] < np.arange(8)[:, None]).astype(np.float32).reshape(1, 64)
    inv = (1.0 / np.float32(1000000.0) ** (np.arange(0, 128, 2, dtype=np.float32) / np.float32(128))).astype(np.float32)
    f = (np.arange(64, dtype=np.float32)[:, None] * inv[None, :]).T
    c[:, 708:772] = np.tile(np.cos(f), (2, 1))
    c[:, 772:836] = np.concatenate([np.sin(f), -np.sin(f)], 0)
    d = p[None, :] - p[:, None]
    same = (p[None, :] // 64 == p[:, None] // 64) & (d <= 0)
    c[:, 836:964] = np.where(same, 0.0, NEG)
    return c


def alibi_bias():
    p = np.arange(128)
    d = (p[None, :] - p[:, None]).astype(np.float32)
    same = (p[None, :] // 64 == p[:, None] // 64) & (d <= 0)
    slopes = np.asarray([(2.0 ** (-8.0 / 32)) ** i for i in range(32)], np.float32)
    full = np.where(same[:, None, :], slopes[None, :, None] * d[:, None, :], np.float32(NEG)).astype(np.float32)
    return full.reshape(128, 8, 4, 128)


def arrange(i):
    f = {k: np.asarray(v) for k, v in i.items()}
    d = {}
    d["x"] = np.ascontiguousarray(f["x"].reshape(4, 128, 512).transpose(1, 0, 2))
    c = constants()
    c[:, 704:708] = f["L0_xattn_bg"].reshape(4, 128).T
    d["const"] = c
    d["xq"] = lay(f["L0_xattn_Wq"].T)
    d["xg"] = lay(f["L0_xattn_Wg"].T)
    d["xk"] = lay(f["L0_xattn_Wkv"][:512].T)
    d["xv"] = lay(f["L0_xattn_Wkv"][512:].T)
    d["xo"] = lay(f["L0_xattn_Wo"].T)
    ctx = f["ctx_2048"]
    pad = np.zeros((8, 13 * 128, 512), np.float32)
    pad[:, :1601] = ctx
    rows = pad.reshape(8, 13, 128, 512)
    cols = rows.reshape(8, 13, 128, 4, 128).transpose(0, 1, 4, 3, 2).reshape(8, 13, 128, 512)
    d["ctx0"] = np.ascontiguousarray(np.concatenate([cols, rows], -1))
    wq = f["L0_attn_Wq"].reshape(2, 4, 64, 512).transpose(1, 0, 2, 3).reshape(512, 512)
    d["aqkv"] = lay(np.concatenate([wq, f["L0_attn_Wk"], f["L0_attn_Wv"]], 0).T)
    d["ao"] = lay(f["L0_attn_Wo"].T.reshape(2, 4, 64, 512).transpose(1, 0, 2, 3).reshape(512, 512))
    d["m0gate"] = lay(f["L0_ffn_Wg"])
    w1 = f["L0_ffn_W1"].reshape(8, 4, 128, 11, 128).transpose(0, 3, 2, 1, 4).reshape(8, 11, 128, 512)
    w3 = f["L0_ffn_W3"].reshape(8, 4, 128, 11, 128).transpose(0, 3, 2, 1, 4).reshape(8, 11, 128, 512)
    w2 = f["L0_ffn_W2"].reshape(8, 11, 128, 512)
    d["m0w"] = np.ascontiguousarray(np.concatenate([w1, w3, w2], -1))
    order = np.concatenate([np.arange(257), 257 + np.arange(1280, 1344), 257 + np.arange(1280)])
    g = f["ctx_2048"][:, order].reshape(8, 1601, 4, 128).transpose(0, 3, 2, 1)
    co, cn = [0, 321, 833, 1345], [321, 512, 512, 256]
    d["ctx1"] = np.concatenate([g[..., a:a + n].reshape(8, 128, 4 * n) for a, n in zip(co, cn)], -1)
    d["iota"] = np.ascontiguousarray(np.broadcast_to((order[257:] - 257).astype(np.int16), (128, 1344)))
    d["len"] = np.ascontiguousarray(np.broadcast_to(f["_lenS2"].astype(np.int32), (128, 8)))
    for short, name in (("cq", "q"), ("ck", "k"), ("cki", "k_img"), ("cv", "v"), ("cvi", "v_img"), ("co", "o")):
        d[short] = lay(f["L1_xattn_w_" + name].T)
    d["bo"] = np.ascontiguousarray(np.broadcast_to(f["L1_xattn_b_o"], (128, 512)))
    v = np.zeros((128, 64), np.float32)
    for n, name in enumerate(("b_q", "b_k", "b_k_img", "b_v", "b_v_img", "g_q", "g_k", "g_k_img")):
        v[:, 4 * n:4 * n + 4] = f["L1_xattn_" + name].reshape(4, 128).T
    perm = lambda w: w.reshape(4, 2, 4, 64, *w.shape[1:]).swapaxes(1, 2).reshape(w.shape)
    v[:, 32:48] = perm(f["L1_attn_q_norm_w"]).reshape(16, 128).T
    v[:, 48:52] = f["L1_attn_k_norm_w"].reshape(4, 128).T
    v[:, 52:56] = f["L1_ffn_attn_norm_w"].reshape(4, 128).T
    v[:, 56] = f["L1_ffn_q_norm_w"]
    v[:, 57] = f["L1_ffn_k_norm_w"]
    v[:, 58:62] = f["L1_ffn_ffn_norm_w"].reshape(4, 128).T
    d["vec"] = v
    d["dq"] = lay(perm(f["L1_attn_wq"]).T)
    d["dk"] = lay(f["L1_attn_wk"].T)
    d["dv"] = lay(f["L1_attn_wv"].T)
    d["do"] = lay(perm(np.ascontiguousarray(f["L1_attn_wo"].T)))
    d["alibi"] = alibi_bias()
    for short, name in (("eq", "q_w"), ("ek", "k_w"), ("ev", "v_w"), ("eo", "o_w")):
        d[short] = lay(f["L1_ffn_" + name].T)
    d["m1gate"] = lay(f["L1_ffn_gate_w"].T)
    up = lambda w: np.pad(w, ((0, 0), (0, 32), (0, 0))).reshape(8, 3, 128, 4, 128).transpose(0, 1, 4, 3, 2).reshape(8, 3, 128, 512)
    down = np.pad(f["L1_ffn_wd"].transpose(0, 2, 1), ((0, 0), (0, 32), (0, 0))).reshape(8, 3, 128, 512)
    d["m1w"] = np.ascontiguousarray(np.concatenate([up(f["L1_ffn_wg"]), up(f["L1_ffn_wu"]), down], -1))
    return d


def kernel(**inputs):
    import concourse.bacc as _bacc
    from concourse import mybir as _mybir
    from concourse.bass_utils import run_bass_kernel_spmd as _run

    nc = _bacc.Bacc("TRN2", target_bir_lowering=False, num_devices=1)
    data = arrange(inputs)
    arrays, D = {}, {}
    for name, a in data.items():
        arrays[f"in_{name}"] = a
        D[name] = nc.dram_tensor(f"in_{name}", a.shape, _mybir.dt.from_np(a.dtype), kind="ExternalInput").ap()
    o = nc.dram_tensor("out_x", (128, 4, 512), _mybir.dt.float32, kind="ExternalOutput").ap()
    build(nc, D, o)
    r = _run(nc, [arrays], core_ids=[0])
    return r.results[0]["out_x"].transpose(1, 0, 2).reshape(8, 64, 512)
```
